# Optimizing a Trainium2 kernel written in Bass

```python
import numpy as np
import jax
import jax.numpy as jnp

def _softmax(x, axis=-1):
    return jax.nn.softmax(x, axis=axis)

def _gelu(x):
    return jax.nn.gelu(x, approximate=True)

def _silu(x):
    return jax.nn.silu(x)

def _sigmoid(x):
    return jax.nn.sigmoid(x)

def _layernorm(x, axis=-1, eps=1e-05):
    m = jnp.mean(x, axis=axis, keepdims=True)
    v = jnp.var(x, axis=axis, keepdims=True)
    return (x - m) / jnp.sqrt(v + eps)

def _scatter_add(tgt, idx, src, axis=0):
    return tgt.at[idx].add(src)

def _segment_sum(src, seg, n):
    return jax.ops.segment_sum(src, seg, n)
kernel_name = 'mk_metaformer_d1_conv_nchw256_r4_0c400a'

def setup_inputs(seed: int=0):
    np.random.seed(seed)
    _w = jnp.asarray

    def _rec_inputs():
        import jax
        import jax.numpy as jnp
        _gk = jax.random.key(seed)
        x = -0.0003957 + 1 * jax.random.normal(jax.random.fold_in(_gk, 1), (16, 64, 56, 56), jnp.float32)
        return x
    x = _rec_inputs()

    def _L0_conv_setup():
        import jax, jax.numpy as jnp
        import numpy as np
        B, C, H, W = (16, 64, 56, 56)
        K = 7
        G = 16
        RR = 4
        CR = C // RR
        EPS = 1e-05
        key = jax.random.key(seed)
        ks = jax.random.split(key, 7)
        s1 = 1.0 / np.sqrt(C)
        s2 = 1.0 / np.sqrt(CR)
        return {'x': jax.random.normal(ks[0], (B, C, H, W), jnp.float32), 'w1': jax.random.uniform(ks[1], (CR, C), jnp.float32, -s1, s1), 'b1': jax.random.uniform(ks[2], (CR,), jnp.float32, -s1, s1), 'gamma': jnp.ones((CR,), jnp.float32), 'beta': jnp.zeros((CR,), jnp.float32), 'w2': jax.random.uniform(ks[3], (K * K * G, CR), jnp.float32, -s2, s2), 'b2': jax.random.uniform(ks[4], (K * K * G,), jnp.float32, -s2, s2)}
    _L0_conv_all = _L0_conv_setup()
    _L0_conv_in = {k: v for k, v in _L0_conv_all.items() if k in ('w1', 'b1', 'gamma', 'beta', 'w2', 'b2')}
    del _L0_conv_all

    def _L0_ffn_setup():
        import jax, jax.numpy as jnp
        import numpy as np
        TOP_K = 2
        key = jax.random.key(seed)
        ks = jax.random.split(key, 4)
        B, L, D, H, E = (8, 1024, 64, 256, 8)
        s = 0.02
        return {'x': jax.random.normal(ks[0], (B, L, D), jnp.float32), 'Wg': jax.random.normal(ks[1], (D, E), jnp.float32) * s, 'bg': jnp.zeros((E,), jnp.float32), 'W1': jax.random.normal(ks[2], (E, D, H), jnp.float32) * s, 'b1': jnp.zeros((E, H), jnp.float32), 'W2': jax.random.normal(ks[3], (E, H, D), jnp.float32) * s, 'b2': jnp.zeros((E, D), jnp.float32)}
    _L0_ffn_all = _L0_ffn_setup()
    _L0_ffn_in = {k: v for k, v in _L0_ffn_all.items() if k in ('Wg', 'bg', 'W1', 'b1', 'W2', 'b2')}
    del _L0_ffn_all
    return {'x': x, 'L0_conv_w1': _L0_conv_in['w1'], 'L0_conv_b1': _L0_conv_in['b1'], 'L0_conv_gamma': _L0_conv_in['gamma'], 'L0_conv_beta': _L0_conv_in['beta'], 'L0_conv_w2': _L0_conv_in['w2'], 'L0_conv_b2': _L0_conv_in['b2'], 'L0_ffn_Wg': _L0_ffn_in['Wg'], 'L0_ffn_bg': _L0_ffn_in['bg'], 'L0_ffn_W1': _L0_ffn_in['W1'], 'L0_ffn_b1': _L0_ffn_in['b1'], 'L0_ffn_W2': _L0_ffn_in['W2'], 'L0_ffn_b2': _L0_ffn_in['b2']}

def reference(x, L0_conv_w1, L0_conv_b1, L0_conv_gamma, L0_conv_beta, L0_conv_w2, L0_conv_b2, L0_ffn_Wg, L0_ffn_bg, L0_ffn_W1, L0_ffn_b1, L0_ffn_W2, L0_ffn_b2):
    import jax
    import jax.numpy as jnp

    def _L0_conv_ref(x, w1, b1, gamma, beta, w2, b2):
        import jax, jax.numpy as jnp
        import numpy as np
        B, C, H, W = (16, 64, 56, 56)
        K = 7
        G = 16
        RR = 4
        CR = C // RR
        EPS = 1e-05
        b, c, h, w = x.shape
        d = c // G
        r = jnp.einsum('bchw,oc->bohw', x, w1) + b1[None, :, None, None]
        mean = r.mean(axis=(0, 2, 3), keepdims=True)
        var = r.var(axis=(0, 2, 3), keepdims=True)
        r = (r - mean) * jax.lax.rsqrt(var + EPS)
        r = r * gamma[None, :, None, None] + beta[None, :, None, None]
        r = jax.nn.relu(r)
        ker = jnp.einsum('bchw,oc->bohw', r, w2) + b2[None, :, None, None]
        ker = ker.reshape(b, K, K, G, h, w).transpose(0, 3, 1, 2, 4, 5)
        ker = ker.reshape(b, G, K * K, h, w)
        p = K // 2
        xp = jnp.pad(x, ((0, 0), (0, 0), (p, p), (p, p)))
        out = jnp.zeros((b, G, d, h, w), x.dtype)
        for i in range(K):
            for j in range(K):
                xs = xp[:, :, i:i + h, j:j + w].reshape(b, G, d, h, w)
                out = out + xs * ker[:, :, i * K + j][:, :, None, :, :]
        return out.reshape(b, c, h, w)

    def _L0_ffn_ref(x, Wg, bg, W1, b1, W2, b2):
        import jax, jax.numpy as jnp
        import numpy as np
        TOP_K = 2
        B, L, D = x.shape
        E = W1.shape[0]
        xf = x.reshape(-1, D)
        gate_logits = xf @ Wg + bg
        top_w, top_i = jax.lax.top_k(gate_logits, TOP_K)
        top_w = jax.nn.softmax(top_w, axis=-1)
        w_dense = jnp.sum(jax.nn.one_hot(top_i, E, dtype=xf.dtype) * top_w[..., None], axis=1)
        out = jnp.zeros_like(xf)
        for e in range(E):
            h = jax.nn.gelu(xf @ W1[e] + b1[e], approximate=False)
            out = out + w_dense[:, e:e + 1] * (h @ W2[e] + b2[e])
        return out.reshape(B, L, D)

    def _gn(v, G=32, eps=1e-05):
        B_, C_, H_, W_ = v.shape
        g = v.reshape(B_, G, C_ // G, H_, W_)
        m = jnp.mean(g, axis=(2, 3, 4), keepdims=True)
        s = jnp.var(g, axis=(2, 3, 4), keepdims=True)
        return ((g - m) / jnp.sqrt(s + eps)).reshape(v.shape)

    def _ln_c(v, eps=1e-06):
        m = jnp.mean(v, axis=1, keepdims=True)
        s = jnp.var(v, axis=1, keepdims=True)
        return (v - m) / jnp.sqrt(s + eps)

    def _ln_t(v, eps=1e-05):
        m = jnp.mean(v, axis=-1, keepdims=True)
        s = jnp.var(v, axis=-1, keepdims=True)
        return (v - m) / jnp.sqrt(s + eps)

    def _to_tokens(v):
        B_, C_, H_, W_ = v.shape
        return v.reshape(B_, C_, H_ * W_).transpose(0, 2, 1)

    def _from_tokens(t, like):
        B_, C_, H_, W_ = like.shape
        return t.transpose(0, 2, 1).reshape(B_, C_, H_, W_)
    x = x + _L0_conv_ref(_ln_c(x), L0_conv_w1, L0_conv_b1, L0_conv_gamma, L0_conv_beta, L0_conv_w2, L0_conv_b2)
    t = _to_tokens(x)
    t = t + _L0_ffn_ref(_ln_t(t), L0_ffn_Wg, L0_ffn_bg, L0_ffn_W1, L0_ffn_b1, L0_ffn_W2, L0_ffn_b2)
    x = _from_tokens(t, x)
    return x

_drawn_inputs = setup_inputs


def setup_inputs(seed=0):
    import zlib

    import numpy as np

    out = dict(_drawn_inputs(seed))
    spreads = {'L0_conv_gamma': (1.0, 0.2),
     'L0_conv_beta': (0.0, 0.1),
     'L0_ffn_bg': (0.0, 0.496),
     'L0_ffn_b1': (0.0, 0.8),
     'L0_ffn_b2': (0.0, 0.368)}
    factors = {'L0_conv_b1': 8.0, 'L0_ffn_Wg': 2.804, 'L0_ffn_W1': 8.0, 'L0_ffn_W2': 7.475}
    for name, (base, spread) in spreads.items():
        noise = np.random.default_rng([zlib.crc32(name.encode()), seed]).standard_normal(out[name].shape)
        drawn = base * np.exp(spread * noise) if base else spread * noise
        out[name] = jnp.asarray(drawn.astype(out[name].dtype))
    for name, factor in factors.items():
        out[name] = (out[name] * factor).astype(out[name].dtype)
    return out
```

```python
from contextlib import ExitStack

import concourse.bass as bass
from concourse import mybir

F32 = mybir.dt.float32
F32R = mybir.dt.float32r
ALU = mybir.AluOpType
ACT = mybir.ActivationFunctionType
AX_X = mybir.AxisListType.X

P = 128

B, C, H, W = 16, 64, 56, 56
HW = H * W
K = 7
PAD = K // 2
G = 16
D = C // G
CR = 16
F = CR + 1
E = 8
HID = 256
HB = E * HID // P
EPS_C, EPS_BN, EPS_T = 1e-6, 1e-5, 1e-5

PARITY = 2
P8 = B // PARITY
T = 392
TR = T // W
UNIT = 2 * T
UNITS = HW // UNIT
SUB = 98
NSUB = UNIT // SUB
WP = 64
HH = H // 2
KR = 32
KS = P // KR
JA = -(-K // KS)
MROWS = 7
MB = HH // MROWS
MF = MROWS * F
TL = 64
TAP0 = 29
ROW0 = (0, 24)
TOFF = (5, 1)
CH = 4
CN = D * 2 * W

XS_H = C * P8 * WP
XS_SIZE = PARITY * H * XS_H
V_J = TL * F
V_G = KS * JA * V_J
V_SIZE = G * V_G


def before(it, k, per, lag):
    return (it, k - lag) if k >= lag else (it - 1, k - lag + per)


def stands(it, k, per, total):
    return not isinstance(it, int) or 0 <= it * per + k < total


def rounds(eng, total, per, tail, step):
    for k in range(per):
        step(0, k)
    with eng.Fori(1, total // per) as it:
        for k in range(per):
            step(it, k)
    for k in range(tail):
        step(total // per, k)


def wait_count(eng, sem, count):
    if not isinstance(count, int) or count > 0:
        eng.wait_ge(sem, count)


def metaformer_block(nc, x, conv_w1, conv_b1, gamma, beta, conv_w2, conv_b2,
                     wg, bg, w1, b1, w2, b2, out):
    xs = nc.dram_tensor("xs", (XS_SIZE + WP,), F32)
    rs = nc.dram_tensor("rs", (H, F, PARITY, P8, W), F32)
    vf = nc.dram_tensor("vf", (V_SIZE,), F32)
    co = nc.dram_tensor("co", (B, C, H, W), F32)
    with ExitStack() as kept:
        ident = kept.enter_context(nc.sbuf_tensor("ident", [P, P], F32))
        affine = kept.enter_context(nc.sbuf_tensor("affine", [MF, 2], F32))
        norm_stage(nc, x, conv_w1, conv_b1, gamma, beta, conv_w2, conv_b2, xs, rs, vf, ident, affine)
        conv_stage(nc, xs, rs, vf, co, affine)
        moe_stage(nc, x, co, wg, bg, w1, b1, w2, b2, out, ident)


def norm_stage(nc, x, conv_w1, conv_b1, gamma, beta, conv_w2, conv_b2, xs, rs, vf, ident, affine):
    STEPS = P8 * UNITS
    PER = 2 * UNITS
    PAIR_ROWS = H // UNITS
    GROUPS = 2

    with ExitStack() as ctx:
        def sb(name, shape, dt=F32):
            return ctx.enter_context(nc.sbuf_tensor(name, shape, dt))

        def ps(name, shape):
            return ctx.enter_context(nc.psum_tensor(name, shape, F32))

        def sem(name):
            return ctx.enter_context(nc.semaphore(name))

        center = sb("center", [P, P])
        mean_col = sb("mean_col", [P, 2])
        w1t = sb("w1t", [P, 2 * CR])
        b1c = sb("b1c", [P, 1])
        eps_c = sb("eps_c", [P, 1])
        eps_bn = sb("eps_bn", [P, 1])
        avg = sb("avg", [P, CR])
        spread = sb("spread", [F, MF])
        zeros = sb("zeros", [P, V_SIZE // P])
        ones = sb("ones", [H, PARITY * P8 * W])
        xin = [sb(f"xin{i}", [P, HW]) for i in range(2)]
        xpad = [sb(f"xpad{i}", [P, H, WP]) for i in range(2)]
        cen = [sb(f"cen{i}", [P, 2, T]) for i in range(4)]
        sq = [sb(f"sq{i}", [P, 2, T]) for i in range(2)]
        std = sb("std", [SUB, NSUB, 2])
        rstd = sb("rstd", [SUB, NSUB, 2])
        rstd_wide = sb("rstd_wide", [SUB, NSUB, 2, C])
        rt = [sb(f"rt{i}", [P, T]) for i in range(2)]
        stats = sb("stats", [P, P8 * GROUPS, 6])
        mv = sb("mv", [P, 2])
        m2 = sb("m2", [P, 1])
        chan = sb("chan", [CR, 6])
        gb = sb("gb", [CR, 2])
        ab = sb("ab", [F, 2])
        cen_ps = [ps(f"cen_ps{i}", [P, 2, 512]) for i in range(2)]
        wide_ps = ps("wide_ps", [P, 2, 512])
        var_ps = ps("var_ps", [P, 512])
        r_ps = ps("r_ps", [P, 512])

        weights_in = sem("weights_in")
        cleared = sem("cleared")
        pads_clear = sem("pads_clear")
        shaped = sem("shaped")
        blanks_done = sem("blanks_done")
        filters_out = sem("filters_out")
        x_in = [sem(f"x_in{i}") for i in range(2)]
        centered = sem("centered")
        cen_out = sem("cen_out")
        squared = sem("squared")
        var_done = sem("var_done")
        std_done = sem("std_done")
        rstd_own = sem("rstd_own")
        rstd_done = sem("rstd_done")
        wide_done = sem("wide_done")
        normed = sem("normed")
        r_done = sem("r_done")
        rt_done = sem("rt_done")
        stats_done = sem("stats_done")
        rs_out = [sem(f"rs_out{i}") for i in range(2)]
        xs_out = [sem(f"xs_out{i}") for i in range(2)]
        bn_own = sem("bn_own")
        bn_pe = sem("bn_pe")
        bn_sqrt = sem("bn_sqrt")

        xs_map = xs[0:XS_SIZE].rearrange("(i h c x) -> i c h x", i=PARITY, h=H, c=C)
        vf_map = vf[:].rearrange("(g j t f) -> g j t f", g=G, j=KS * JA, t=TL)
        w2_map = conv_w2.rearrange("(i j g) c -> i g j c", i=K, j=K)
        b2_map = conv_b2.rearrange("(i j g u) -> i g j u", i=K, j=K, u=1)
        WEIGHTS = 2 + 8 + 2
        CLEARED = 14

        block = ctx.enter_context(nc.Block())

        @block.sync
        def _(sp):
            x_pairs = x.rearrange("(p i) c h w -> p (i c) (h w)", i=PARITY)
            sp.dma_start(xin[0][:, :], x_pairs[0]).then_inc(x_in[0], 16)
            sp.dma_start(xin[1][:, :], x_pairs[1]).then_inc(x_in[1], 16)
            sp.wait_ge(cleared, 3)
            sp.dma_start(vf[:].rearrange("(p x) -> p x", p=P), zeros[:, :]).then_inc(blanks_done, 16)
            sp.dma_start(xs[XS_SIZE:XS_SIZE + WP].rearrange("(a x) -> a x", a=1),
                         zeros[0:1, 0:WP]).then_inc(blanks_done, 16)
            sp.dma_start(rs[:, CR, :, :, :].rearrange("h i p w -> h (i p w)"),
                         ones[:, :]).then_inc(blanks_done, 16)

            def step(it, k):
                j, v = before(it, k, PER, 3)
                if v % 2 == 1 and stands(j, v, PER, STEPS):
                    pair = j * 2 + v // UNITS
                    grp = v // 2 % GROUPS
                    sp.wait_ge(rt_done, j * (PER // 2) + v // 2 + 1)
                    for q in range(4):
                        row = (4 * grp + q) * TR
                        for i in range(PARITY):
                            dst = rs[row:row + TR, 0:CR, i, bass.ds(pair, 1), :]
                            sp.dma_start(dst.rearrange("h c u w -> c h (u w)"),
                                         rt[grp][32 * q + CR * i:32 * q + CR * (i + 1), :]
                                         .rearrange("c (h w) -> c h w", h=TR)).then_inc(rs_out[grp], 16)
                if v % UNITS == UNITS - 1 and stands(j, v, PER, STEPS):
                    pair, slot = j * 2 + v // UNITS, v // UNITS
                    sp.wait_ge(normed, j * PER + v + 1)
                    for i in range(PARITY):
                        sp.dma_start(xs_map[i][:, :, bass.ds(pair * WP, WP)],
                                     xpad[slot][C * i:C * (i + 1), :, :]).then_inc(xs_out[slot], 16)
                    if isinstance(j, int) and j * 2 + slot + 2 >= P8:
                        return
                    sp.wait_ge(centered, j * PER + v + 1)
                    sp.dma_start(xin[slot][:, :], x_pairs[bass.ds(pair + 2, 1)]
                                 .rearrange("u p n -> p (u n)")).then_inc(x_in[slot], 16)

            rounds(sp, STEPS - PER, PER, 0, step)
            for k in range(PER + 3):
                if k < PER:
                    step(STEPS // PER - 1, k)
                else:
                    step(STEPS // PER, k - PER)
            sp.wait_ge(blanks_done, 3 * 16)
            sp.wait_ge(filters_out, 2 * K * 16)
            for i in range(2):
                sp.wait_ge(rs_out[i], P8 * 8 * 16)
                sp.wait_ge(xs_out[i], P8 // 2 * PARITY * 16)

        @block.gpsimd
        def _(pool):
            blank = [(zeros[:, :], 0.0), (ones[:, :], 1.0), (w1t[:, :], 0.0), (ident[:, :], 0.0),
                     (avg[:, :], 0.0), (spread[:, :], 0.0), (center[:, :], 0.0), (mean_col[:, :], 0.0),
                     (eps_c[:, :], EPS_C), (eps_bn[:, :], EPS_BN)]
            for i in range(PARITY):
                half = slice(C * i, C * (i + 1))
                blank += [(center[half, half], -1.0 / C), (mean_col[half, i:i + 1], 1.0 / C)]
            assert len(blank) == CLEARED
            for n, (part, value) in enumerate(blank):
                pool.memset(part, value).then_inc(cleared, 1)
                pool.wait_ge(cleared, n + 1)
            pool.affine_select(out=ident[:, :], in_=ident[:, :], compare_op=ALU.not_equal, fill=1.0,
                               base=0, pattern=[[-1, P]], channel_multiplier=1).then_inc(shaped, 1)
            pool.wait_ge(shaped, 1)
            pool.affine_select(out=center[:, :], in_=center[:, :], compare_op=ALU.not_equal,
                               fill=1.0 - 1.0 / C, base=0, pattern=[[-1, P]],
                               channel_multiplier=1).then_inc(shaped, 1)
            pool.wait_ge(shaped, 2)
            wide = spread[:, :].rearrange("p (r f) -> p r f", r=MROWS)
            pool.affine_select(out=wide, in_=wide, compare_op=ALU.not_equal, fill=1.0, base=0,
                               pattern=[[0, MROWS], [-1, F]], channel_multiplier=1).then_inc(shaped, 1)
            for n in range(P // CR):
                pool.wait_ge(shaped, 3 + n)
                pool.affine_select(out=avg[:, :], in_=avg[:, :], compare_op=ALU.not_equal,
                                   fill=CR / P, base=-CR * n, pattern=[[-1, CR]],
                                   channel_multiplier=1).then_inc(shaped, 1)
            pool.wait_ge(blanks_done, 3 * 16)
            for i in range(K):
                pool.dma_start(vf_map[:, 0:K, TAP0 + i, 0:CR], w2_map[i]).then_inc(filters_out, 16)
                pool.dma_start(vf_map[:, 0:K, TAP0 + i, CR:F], b2_map[i],
                               allow_slow_non_contiguous=True).then_inc(filters_out, 16)

        @block.scalar
        def _(act):
            act.wait_ge(cleared, 3)
            for i in range(PARITY):
                act.dma_start(w1t[C * i:C * (i + 1), CR * i:CR * (i + 1)],
                              conv_w1.rearrange("o c -> c o"), allow_slow_non_contiguous=True).then_inc(weights_in, 16)
            for n in range(P // CR):
                act.dma_start(b1c[CR * n:CR * (n + 1), :],
                              conv_b1.rearrange("(c u) -> c u", u=1)).then_inc(weights_in, 16)
            act.dma_start(gb[:, 0:1], gamma.rearrange("(c u) -> c u", u=1)).then_inc(weights_in, 16)
            act.dma_start(gb[:, 1:2], beta.rearrange("(c u) -> c u", u=1)).then_inc(weights_in, 16)
            act.wait_ge(weights_in, WEIGHTS * 16)
            act.wait_ge(cleared, CLEARED)

            def center_and_square(it, k):
                n = it * PER + k
                act.wait_ge(centered, n + 1)
                wait_count(act, normed, n - 3)
                nc.scalar.activation(cen[k % 4][:, :, :], cen_ps[k % 2][:, :, 0:T],
                                     ACT.Copy).then_inc(cen_out, 1)
                wait_count(act, var_done, n - 1)
                act.wait_ge(cen_out, n + 1)
                nc.scalar.activation(sq[k % 2][:, :, :], cen[k % 4][:, :, :],
                                     ACT.Square).then_inc(squared, 1)

            def deviation(it, k):
                n = it * PER + k
                act.wait_ge(var_done, n + 1)
                wait_count(act, rstd_own, n)
                nc.scalar.activation(std[:, :, :], var_ps[0:SUB, 0:2 * NSUB]
                                     .rearrange("p (s i) -> p s i", i=2), ACT.Sqrt,
                                     bias=eps_c[0:SUB, :]).then_inc(std_done, 1)

            def r_tiles(it, k):
                if k % 2 == 0:
                    return
                grp = k // 2 % GROUPS
                count = it * (PER // 2) + k // 2
                act.wait_ge(r_done, it * PER + k + 1)
                wait_count(act, rs_out[grp], (it * 2 + k // UNITS) * 8 * 16)
                wait_count(act, stats_done, count - 1)
                nc.scalar.activation(rt[grp][:, :], r_ps[:, 0:T], ACT.Identity,
                                     bias=b1c[:, :]).then_inc(rt_done, 1)

            def step(it, k):
                if stands(it, k, PER, STEPS):
                    center_and_square(it, k)
                a = before(it, k, PER, 1)
                if stands(*a, PER, STEPS):
                    deviation(*a)
                a = before(it, k, PER, 3)
                if stands(*a, PER, STEPS):
                    r_tiles(*a)

            rounds(act, STEPS, PER, 3, step)
            act.wait_ge(bn_own, 6)
            nc.scalar.activation(chan[:, 3:4], chan[:, 2:3], ACT.Sqrt,
                                 bias=eps_bn[0:CR, :]).then_inc(bn_sqrt, 1)

        @block.tensor
        def _(pe):
            pe.wait_ge(shaped, 3 + P // CR)
            pe.wait_ge(weights_in, WEIGHTS * 16)

            def center_unit(it, k):
                n = it * PER + k
                if k % UNITS == 0:
                    slot = k // UNITS
                    pe.wait_ge(x_in[slot], it * 16 + 16)
                wait_count(pe, cen_out, n - 1)
                for t in range(2):
                    at = (2 * (k % UNITS) + t) * T
                    mm = nc.tensor.matmul(cen_ps[k % 2][:, t, 0:T], center[:, :],
                                          xin[k // UNITS][:, at:at + T], start=True, stop=True)
                mm.then_inc(centered, 1)

            def variances(it, k):
                n = it * PER + k
                pe.wait_ge(squared, n + 1)
                wait_count(pe, std_done, n)
                flat = sq[k % 2][:, :, :].rearrange("p a t -> p (a t)")
                for s in range(NSUB):
                    mm = nc.tensor.matmul(var_ps[0:SUB, 2 * s:2 * s + 2],
                                          flat[:, SUB * s:SUB * (s + 1)], mean_col[:, :],
                                          start=True, stop=True)
                mm.then_inc(var_done, 1)

            def widen(it, k):
                n = it * PER + k
                pe.wait_ge(rstd_done, n + 1)
                wait_count(pe, normed, n)
                for s in range(NSUB):
                    t, at = s // (NSUB // 2), s % (NSUB // 2) * SUB
                    mm = nc.tensor.transpose(wide_ps[:, t, at:at + SUB],
                                             rstd_wide[:, s, :, :].rearrange("p i c -> p (i c)"),
                                             ident[0:SUB, 0:SUB])
                mm.then_inc(wide_done, 1)

            def reduce_channels(it, k):
                n = it * PER + k
                pe.wait_ge(normed, n + 1)
                if k % 2 == 0:
                    wait_count(pe, rt_done, it * (PER // 2) + k // 2)
                for t in range(2):
                    q = 2 * (k % 2) + t
                    row = (2 * (k % UNITS) + t) * TR
                    mm = nc.tensor.matmul(r_ps[32 * q:32 * (q + 1), 0:T], w1t[:, :],
                                          xpad[k // UNITS][:, row:row + TR, PAD:PAD + W],
                                          start=True, stop=True)
                mm.then_inc(r_done, 1)

            def step(it, k):
                if stands(it, k, PER, STEPS):
                    center_unit(it, k)
                a = before(it, k, PER, 1)
                if stands(*a, PER, STEPS):
                    variances(*a)
                a = before(it, k, PER, 3)
                if stands(*a, PER, STEPS):
                    reduce_channels(*a)
                a = before(it, k, PER, 2)
                if stands(*a, PER, STEPS):
                    widen(*a)

            rounds(pe, STEPS, PER, 3, step)
            pe.wait_ge(bn_own, 3)
            nc.tensor.matmul(var_ps[0:CR, 64:66], avg[:, :], mv[:, :], start=True,
                             stop=True).then_inc(bn_pe, 1)
            pe.wait_ge(bn_own, 10)
            nc.tensor.matmul(var_ps[0:MF, 128:130], spread[:, :], ab[:, :], start=True,
                             stop=True).then_inc(bn_pe, 1)

        @block.vector
        def _(dve):
            nc.vector.memset(xpad[0][:, :, :], 0.0).then_inc(pads_clear, 1)
            nc.vector.memset(xpad[1][:, :, :], 0.0).then_inc(pads_clear, 1)
            dve.wait_ge(pads_clear, 2)

            def reciprocals(it, k):
                n = it * PER + k
                dve.wait_ge(std_done, n + 1)
                nc.vector.reciprocal(rstd[:, :, :], std[:, :, :]).then_inc(rstd_own, 1)
                wait_count(dve, wide_done, n)
                dve.wait_ge(rstd_own, n + 1)
                nc.vector.tensor_copy(rstd_wide[:, :, :, :],
                                      rstd[:, :, :].unsqueeze(3).broadcast_to([SUB, NSUB, 2, C])
                                      ).then_inc(rstd_done, 1)

            def normalise(it, k):
                n = it * PER + k
                slot, row = k // UNITS, k % UNITS * PAIR_ROWS
                dve.wait_ge(wide_done, n + 1)
                if k % UNITS == 0:
                    wait_count(dve, xs_out[slot], it * PARITY * 16)
                nc.vector.tensor_tensor(
                    xpad[slot][:, row:row + PAIR_ROWS, PAD:PAD + W]
                    .rearrange("p (a r) w -> p a r w", a=2),
                    cen[k % 4][:, :, :].rearrange("p a (r w) -> p a r w", w=W),
                    wide_ps[:, :, 0:T].rearrange("p a (r w) -> p a r w", w=W),
                    ALU.mult).then_inc(normed, 1)

            def statistics(it, k):
                if k % 2 == 0:
                    return
                count = it * (PER // 2) + k // 2
                dve.wait_ge(rt_done, count + 1)
                nc.vector.bn_stats(stats[:, bass.ds(count, 1), :].rearrange("p u s -> p (u s)"),
                                   rt[k // 2 % GROUPS][:, :]).then_inc(stats_done, 1)

            def step(it, k):
                a = before(it, k, PER, 2)
                if stands(*a, PER, STEPS):
                    normalise(*a)
                a = before(it, k, PER, 1)
                if stands(*a, PER, STEPS):
                    reciprocals(*a)
                a = before(it, k, PER, 3)
                if stands(*a, PER, STEPS):
                    statistics(*a)

            rounds(dve, STEPS, PER, 3, step)

            dve.wait_ge(stats_done, P8 * GROUPS)
            nc.vector.bn_aggr(mv[:, :], stats[:, :, :].rearrange("p n s -> p (n s)")).then_inc(bn_own, 1)
            dve.wait_ge(bn_own, 1)
            nc.vector.tensor_tensor(m2[:, :], mv[:, 0:1], mv[:, 0:1], ALU.mult).then_inc(bn_own, 1)
            dve.wait_ge(bn_own, 2)
            nc.vector.tensor_tensor(mv[:, 1:2], mv[:, 1:2], m2[:, :], ALU.add).then_inc(bn_own, 1)
            dve.wait_ge(bn_pe, 1)
            nc.vector.tensor_copy(chan[:, 0:2], var_ps[0:CR, 64:66]).then_inc(bn_own, 1)
            dve.wait_ge(bn_own, 4)
            nc.vector.tensor_tensor(chan[:, 4:5], chan[:, 0:1], chan[:, 0:1], ALU.mult).then_inc(bn_own, 1)
            dve.wait_ge(bn_own, 5)
            nc.vector.tensor_tensor(chan[:, 2:3], chan[:, 1:2], chan[:, 4:5], ALU.subtract).then_inc(bn_own, 1)
            nc.vector.memset(ab[:, 0:1], 0.0).then_inc(bn_own, 1)
            nc.vector.memset(ab[:, 1:2], 1.0).then_inc(bn_own, 1)
            dve.wait_ge(bn_sqrt, 1)
            nc.vector.reciprocal(chan[:, 4:5], chan[:, 3:4]).then_inc(bn_sqrt, 1)
            dve.wait_ge(bn_sqrt, 2)
            dve.wait_ge(bn_own, 8)
            dve.wait_ge(weights_in, WEIGHTS * 16)
            nc.vector.tensor_tensor(ab[0:CR, 0:1], gb[:, 0:1], chan[:, 4:5], ALU.mult).then_inc(bn_own, 1)
            dve.wait_ge(bn_own, 9)
            nc.vector.tensor_tensor(chan[:, 5:6], chan[:, 0:1], ab[0:CR, 0:1], ALU.mult).then_inc(bn_sqrt, 1)
            dve.wait_ge(bn_sqrt, 3)
            nc.vector.tensor_tensor(ab[0:CR, 1:2], gb[:, 1:2], chan[:, 5:6], ALU.subtract).then_inc(bn_own, 1)
            dve.wait_ge(bn_pe, 2)
            nc.vector.tensor_copy(affine[:, :], var_ps[0:MF, 128:130]).then_inc(bn_own, 1)
            dve.wait_ge(bn_own, 11)


def conv_stage(nc, xs, rs, vf, co, affine):
    STEPS = G * 2 * PARITY
    PER = 2 * PARITY
    XN = D * P8 * WP
    TN = JA * HH * F
    NZ = CH * 2

    with ExitStack() as ctx:
        def sb(name, shape, dt=F32):
            return ctx.enter_context(nc.sbuf_tensor(name, shape, dt))

        def sem(name):
            return ctx.enter_context(nc.semaphore(name))

        r_all = sb("r_all", [MF, 2, MB, PARITY, P8 * W])
        pick = sb("pick", [MF, 3 * MROWS + KR])
        xq = [sb(f"xq{i}", [P, XN]) for i in range(2)]
        xq_hi = [sb(f"xq_hi{i}", [P, XN], F32R) for i in range(2)]
        xq_lo = [sb(f"xq_lo{i}", [P, XN], F32R) for i in range(2)]
        band = [sb(f"band{i}", [P, TN]) for i in range(2)]
        band_hi = [sb(f"band_hi{i}", [P, TN], F32R) for i in range(2)]
        band_lo = [sb(f"band_lo{i}", [P, TN], F32R) for i in range(2)]
        prod = [sb(f"prod{i}", [MF, NZ, 2, CN]) for i in range(2)]
        ob = [sb(f"ob{i}", [P, CN]) for i in range(2)]
        z_ps = [ctx.enter_context(nc.psum_tensor(f"z_ps{i}", [P, 2, 512], F32)) for i in range(2)]
        o_ps = [ctx.enter_context(nc.psum_tensor(f"o_ps{i}", [P, 512], F32)) for i in range(2)]

        r_in = sem("r_in")
        r_ready = sem("r_ready")
        pick_own = sem("pick_own")
        x_in = [sem(f"xq_in{i}") for i in range(2)]
        band_in = [sem(f"band_in{i}") for i in range(2)]
        x_hi = sem("x_hi")
        x_lo = sem("x_lo")
        b_hi = sem("b_hi")
        b_lo = sem("b_lo")
        z_done = sem("z_done")
        weighted = sem("weighted")
        summed = sem("summed")
        ob_done = sem("ob_done")
        ob_out = [sem(f"ob_out{i}") for i in range(2)]

        block = ctx.enter_context(nc.Block())

        def quad(it, k):
            return it * PER + k, k // PARITY, k % PARITY

        @block.sync
        def _(sp):
            for half in range(2):
                for m in range(MB):
                    for row in range(MROWS):
                        h = HH * half + HH - 1 - (MROWS * m + row)
                        sp.dma_start(r_all[F * row:F * (row + 1), half, m, :, :],
                                     rs[h].rearrange("f i p w -> f i (p w)")).then_inc(r_in, 16)

            def load(it, k):
                n, half, par = quad(it, k)
                wait_count(sp, x_lo, n - 1)
                if par == 0:
                    wait_count(sp, b_lo, it * 2 + half - 1)
                    for s in range(KS):
                        at = s * V_J + TOFF[half] * F
                        for a in range(JA):
                            src = banded(vf, it, at + a * KS * V_J)
                            sp.dma_start(band[half][KR * s:KR * (s + 1), a * HH * F:(a + 1) * HH * F],
                                         src).then_inc(band_in[half], 16)
                for s in range(KS):
                    src = xs[s:s + XS_SIZE].rearrange("(i h g x) -> i h g x", i=PARITY, h=H, g=G)
                    sp.dma_start(xq[par][KR * s:KR * (s + 1), :],
                                 src[par, ROW0[half]:ROW0[half] + KR, bass.ds(it, 1), :]
                                 .rearrange("h u x -> h (u x)")).then_inc(x_in[par], 16)

            def banded(vf, it, at):
                rows = vf[0:V_SIZE].rearrange("(g v) -> g v", g=G)[bass.ds(it, 1), :]
                return bass.AP(rows.tensor, rows.offset + at, [[F, KR], [1, HH * F]])

            def store(it, k):
                n, half, par = quad(it, k)
                sp.wait_ge(ob_done, n + 1)
                for q in range(CH):
                    for j in range(2):
                        b = PARITY * (2 * q + j) + par
                        dst = co[b].rearrange("(g d) h w -> g h d w", g=G)
                        dst = dst[bass.ds(it, 1), HH * half:HH * (half + 1), :, :]
                        src = ob[k % 2][32 * q:32 * q + HH, :].rearrange("p (d j w) -> p d j w", d=D, j=2)
                        sp.dma_start(dst.rearrange("u h d w -> h (u d) w"),
                                     src[:, :, j, :]).then_inc(ob_out[k % 2], 16)

            def step(it, k):
                if stands(it, k, PER, STEPS):
                    load(it, k)
                a = before(it, k, PER, 2)
                if stands(*a, PER, STEPS):
                    store(*a)

            rounds(sp, STEPS, PER, 2, step)
            for i in range(2):
                sp.wait_ge(ob_out[i], STEPS // 2 * CH * 2 * 16)

        @block.gpsimd
        def _(pool):
            pool.memset(pick[:, :], 0.0).then_inc(pick_own, 1)
            pool.wait_ge(pick_own, 1)
            for f in range(F):
                cols = pick[:, 3 * MROWS:4 * MROWS]
                pool.wait_ge(pick_own, f + 1)
                pool.affine_select(out=cols, in_=cols, compare_op=ALU.not_equal, fill=1.0,
                                   base=-(F * (MROWS - 1) + f), pattern=[[F, MROWS]],
                                   channel_multiplier=1).then_inc(pick_own, 1)

            def split(it, k):
                n, half, par = quad(it, k)
                if par == 0:
                    pool.wait_ge(b_hi, it * 2 + half + 1)
                    wait_count(pool, z_done, (n - 2) * NZ)
                    pool.tensor_tensor(band_lo[half][:, :], band[half][:, :],
                                       band_hi[half][:, :].bitcast(F32), ALU.subtract).then_inc(b_lo, 1)
                pool.wait_ge(x_hi, n + 1)
                wait_count(pool, z_done, (n - 1) * NZ)
                pool.tensor_tensor(xq_lo[par][:, :], xq[par][:, :],
                                   xq_hi[par][:, :].bitcast(F32), ALU.subtract).then_inc(x_lo, 1)

            rounds(pool, STEPS, PER, 0, split)

        @block.scalar
        def _(act):
            def split(it, k):
                n, half, par = quad(it, k)
                if par == 0:
                    act.wait_ge(band_in[half], (it * KS * JA + KS * JA) * 16)
                    wait_count(act, z_done, (n - 2) * NZ)
                    nc.scalar.activation(band_hi[half][:, :], band[half][:, :], ACT.Copy).then_inc(b_hi, 1)
                act.wait_ge(x_in[par], (it * 2 + half + 1) * KS * 16)
                wait_count(act, z_done, (n - 1) * NZ)
                nc.scalar.activation(xq_hi[par][:, :], xq[par][:, :], ACT.Copy).then_inc(x_hi, 1)

            def evacuate(it, k):
                n, half, par = quad(it, k)
                act.wait_ge(summed, n + 1)
                wait_count(act, ob_out[k % 2], (it * 2 + half) * CH * 2 * 16)
                nc.scalar.activation(ob[k % 2][:, :], o_ps[k % 2][:, 0:CN], ACT.Copy).then_inc(ob_done, 1)

            def step(it, k):
                if stands(it, k, PER, STEPS):
                    split(it, k)
                    if isinstance(it, int) and it == 0 and k == 0:
                        act.wait_ge(r_in, 2 * MB * MROWS * 16)
                        nc.scalar.activation(r_all[:, :, :, :, :], r_all[:, :, :, :, :], ACT.Relu,
                                             scale=affine[:, 0:1], bias=affine[:, 1:2]).then_inc(r_ready, 1)
                a = before(it, k, PER, 1)
                if stands(*a, PER, STEPS):
                    evacuate(*a)

            rounds(act, STEPS, PER, 1, step)

        @block.tensor
        def _(pe):
            pe.wait_ge(pick_own, F + 1)

            def filters(it, k, units):
                n, half, par = quad(it, k)
                for u in units:
                    q, mp = u // 2, u % 2
                    wait_count(pe, weighted, n * NZ + u - 1)
                    for m in range(2):
                        zt = z_ps[u % 2][0:MF, m, 0:CN]
                        for a in range(JA):
                            cols = slice((a * MB + 2 * mp + m) * MF, (a * MB + 2 * mp + m + 1) * MF)

                            def maps(part):
                                return part[par][:, :].rearrange("p (d i w) -> p d i w", d=D, i=P8)[
                                    :, :, 2 * q:2 * q + 2, KS * a:KS * a + W]

                            nc.tensor.matmul(zt, band_hi[half][:, cols], maps(xq_hi),
                                             start=(a == 0), stop=False)
                            nc.tensor.matmul(zt, band_hi[half][:, cols], maps(xq_lo),
                                             start=False, stop=False)
                            mm = nc.tensor.matmul(zt, band_lo[half][:, cols], maps(xq_hi),
                                                  start=False, stop=(a == JA - 1))
                    mm.then_inc(z_done, 1)

            def sums(it, k):
                n = it * PER + k
                pe.wait_ge(weighted, n * NZ + NZ)
                wait_count(pe, ob_done, n - 1)
                for m in range(MB):
                    for q in range(CH):
                        mm = nc.tensor.matmul(o_ps[k % 2][32 * q:32 * (q + 1), 0:CN],
                                              pick[:, MROWS * m:MROWS * m + KR],
                                              prod[k % 2][:, 2 * q + m // 2, m % 2, :],
                                              start=(m == 0), stop=(m == MB - 1))
                mm.then_inc(summed, 1)

            def step(it, k):
                own = stands(it, k, PER, STEPS)
                if own:
                    n, half, par = quad(it, k)
                    pe.wait_ge(b_lo, it * 2 + half + 1)
                    pe.wait_ge(x_lo, n + 1)
                    filters(it, k, range(0, 2))
                a = before(it, k, PER, 1)
                if stands(*a, PER, STEPS):
                    sums(*a)
                if own:
                    filters(it, k, range(2, NZ))

            rounds(pe, STEPS, PER, 1, step)

        @block.vector
        def _(dve):
            dve.wait_ge(r_ready, 1)

            def weigh(it, k):
                n, half, par = quad(it, k)
                for u in range(NZ):
                    q, mp = u // 2, u % 2
                    dve.wait_ge(z_done, n * NZ + u + 1)
                    if u == 0:
                        wait_count(dve, summed, n - 1)
                    by = r_all[:, half, 2 * mp:2 * mp + 2, par, 2 * q * W:2 * (q + 1) * W]
                    nc.vector.tensor_tensor(
                        prod[k % 2][:, u, :, :].rearrange("p m (d x) -> p m d x", d=D),
                        z_ps[u % 2][0:MF, :, 0:CN].rearrange("p m (d x) -> p m d x", d=D),
                        by.unsqueeze(2).broadcast_to([MF, 2, D, 2 * W]),
                        ALU.mult).then_inc(weighted, 1)

            rounds(dve, STEPS, PER, 0, weigh)


def moe_stage(nc, x, co, wg, bg, w1, b1, w2, b2, out, ident):
    STEPS = B * UNITS
    PER = UNITS
    PAIRS = E // 2
    SLOTS = HB
    GATE_OPS = 18

    with ExitStack() as ctx:
        def sb(name, shape, dt=F32):
            return ctx.enter_context(nc.sbuf_tensor("moe_" + name, shape, dt))

        def sem(name):
            return ctx.enter_context(nc.semaphore(name))

        center = sb("center2", [P, P])
        twin = sb("twin", [P, C])
        mean_col = sb("mean_col2", [P, 1])
        neg_half = sb("neg_half", [SUB, NSUB])
        rank = sb("rank", [SUB, NSUB, E])
        w1_raw = sb("w1_raw", [P, HB * P])
        w1_hi = sb("w1_hi", [P, HB * P], F32R)
        w1_lo = sb("w1_lo", [P, HB * P], F32R)
        w2_s = sb("w2_s", [P, HB, C])
        b1_s = sb("b1_s", [P, HB])
        b2_s = sb("b2_s", [P, PAIRS])
        wg_raw = sb("wg_raw", [P, E])
        wg_half = sb("wg_half", [P, E])
        bg_s = sb("bg_s", [SUB, E])
        xc = [sb(f"xc{i}", [P, 2, T]) for i in range(4)]
        cen = sb("cen2", [P, UNIT])
        sq = sb("sq2", [P, UNIT])
        xn = sb("xn", [P, 2, T])
        tok = [sb(f"tok{i}", [P, 2, T], F32R) for i in range(2)]
        var_eps = sb("var_eps", [SUB, NSUB])
        rstd = sb("rstd2", [SUB, NSUB])
        logit = sb("logit", [SUB, NSUB, E])
        rest = sb("rest", [SUB, NSUB, E])
        match = sb("match", [SUB, NSUB, E])
        first = sb("first", [SUB, NSUB, E])
        second = sb("second", [SUB, NSUB, E])
        either = sb("either", [SUB, NSUB, E])
        weight2 = sb("weight2", [SUB, NSUB, E])
        top1 = sb("top1", [SUB, NSUB])
        top2 = sb("top2", [SUB, NSUB])
        best = sb("best", [SUB, NSUB])
        gap = sb("gap", [SUB, NSUB])
        tanh = sb("tanh", [SUB, NSUB])
        wide = [sb(f"wide{p}", [SUB, NSUB, 2, C]) for p in range(PAIRS)]
        wt = [sb(f"wt{p}", [P, 2, T]) for p in range(PAIRS)]
        hid = [sb(f"hid{i}", [P, 2, T]) for i in range(8)]
        term = [sb(f"term{p}", [P, 2, T]) for p in range(PAIRS)]
        acc = sb("acc", [P, 2, T])
        res = [sb(f"res{i}", [P, T]) for i in range(2)]
        h_ps = [ctx.enter_context(nc.psum_tensor(f"h_ps{i}", [P, 2, 512], F32)) for i in range(2)]
        y_ps = ctx.enter_context(nc.psum_tensor("y_ps", [P, 2, 512], F32))
        m_ps = [ctx.enter_context(nc.psum_tensor(f"m_ps{i}", [P, 512], F32)) for i in range(2)]

        fills = sem("fills")
        weights_in = sem("ffn_weights_in")
        w_hi = sem("w_hi")
        w_lo = sem("w_lo")
        wg_ready = sem("wg_ready")
        xc_in = [sem(f"xc_in{i}") for i in range(4)]
        misc_in = sem("misc_in")
        misc_out = sem("misc_out")
        squared = sem("squared2")
        var_done = sem("var_eps_done")
        rstd_done = sem("rstd_done2")
        tok_hi = sem("tok_hi")
        tok_lo = sem("tok_lo")
        gate = sem("gate")
        tanh_done = sem("tanh_done")
        wide_done = sem("wide_done2")
        h_done = sem("h_done")
        gelu_done = sem("gelu_done")
        y_done = sem("y_done")
        y_out = sem("y_out")
        added = sem("added")
        res_out = [sem(f"res_out{i}") for i in range(2)]

        FRONT = [("center0", 0), ("center1", 0), ("gates", 5), ("rstd0", 10), ("rstd1", 10)]
        MID = [(f"weight{p}{t}", s) for p, s in enumerate((1, 3, 6, 8)) for t in range(2)]
        END = [("result", 7)]

        def misc_uses(front, mid, end):
            uses = FRONT * front + MID * mid + END * end
            return sorted(uses, key=lambda u: u[1])

        def misc(it, k, name):
            if isinstance(it, int):
                n = it * PER + k
                flags = [(0 <= i < STEPS, 0 <= i - 1 < STEPS, 0 <= i - 2 < STEPS) for i in range(n + 1)]
                base = sum(len(misc_uses(*f)) for f in flags[:n])
                at = base + [u[0] for u in misc_uses(*flags[n])].index(name)
                return at, at % 2
            full = misc_uses(True, True, True)
            lack = 2 * len(END) + len(MID)
            at = [u[0] for u in full].index(name) - lack
            return (it * PER + k) * len(full) + at, at % 2

        block = ctx.enter_context(nc.Block())

        @block.sync
        def _(sp):
            def load(it, k):
                for src, half in ((x, 0), (co, 1)):
                    img = src.rearrange("b c h w -> b c (h w)") if half == 0 else \
                        src[:, :, :, :].rearrange("b c h w -> b c (h w)")
                    sp.dma_start(xc[k][C * half:C * (half + 1), :, :].rearrange("p a t -> p (a t)"),
                                 img[bass.ds(it, 1), :, UNIT * k:UNIT * (k + 1)]
                                 .rearrange("u c t -> (u c) t")).then_inc(xc_in[k], 16)

            def store(step, it, k):
                at, _ = misc(*step, "result")
                sp.wait_ge(misc_out, at + 1)
                img = out.rearrange("b c h w -> b c (h w)")
                for t in range(2):
                    sp.dma_start(img[bass.ds(it, 1), :, UNIT * k + T * t:UNIT * k + T * (t + 1)]
                                 .rearrange("u c t -> (u c) t"),
                                 res[k % 2][C * t:C * (t + 1), :]).then_inc(res_out[k % 2], 16)

            def step(it, k):
                if stands(it, k, PER, STEPS):
                    load(it, k)
                if isinstance(it, int) and it == 0 and k == 0:
                    for half in range(2):
                        rows = slice(C * half, C * (half + 1))
                        sp.dma_start(w1_raw[rows, :].rearrange("c (e n) -> c e n", e=E),
                                     w1.rearrange("e c n -> c e n")).then_inc(weights_in, 16)
                        sp.dma_start(wg_raw[rows, :], wg).then_inc(weights_in, 16)
                    sp.dma_start(w2_s[:, :, :], w2.rearrange("e (b p) d -> p (e b) d", p=P)).then_inc(weights_in, 16)
                    sp.dma_start(b1_s[:, :], b1.rearrange("e (b p) -> p (e b)", p=P),
                                 allow_slow_non_contiguous=True).then_inc(weights_in, 16)
                    sp.dma_start(b2_s[:, :], b2.rearrange("(q e) d -> (e d) q", e=2),
                                 allow_slow_non_contiguous=True).then_inc(weights_in, 16)
                    sp.dma_start(bg_s[:, :], bg.partition_broadcast(SUB)).then_inc(weights_in, 16)
                z = before(it, k, PER, 2)
                if stands(*z, PER, STEPS):
                    store((it, k), *z)

            rounds(sp, STEPS, PER, 2, step)
            for i in range(2):
                sp.wait_ge(res_out[i], STEPS * 16)

        WEIGHTS = 8 * 16

        @block.gpsimd
        def _(pool):
            consts = [(center[:, :], -1.0 / C), (twin[:, :], 0.0), (mean_col[:, :], 0.5 / C),
                      (neg_half[:, :], -0.5)] + [(rank[:, :, e:e + 1], float(E - e)) for e in range(E)]
            for n, (part, value) in enumerate(consts):
                pool.memset(part, value).then_inc(fills, 1)
                pool.wait_ge(fills, n + 1)
            done = len(consts)
            for mat, cols, fill in ((center, P, 1.0 - 1.0 / C), (twin, C, 1.0)):
                for shift in (0, C, -C):
                    pool.affine_select(out=mat[:, :], in_=mat[:, :], compare_op=ALU.not_equal,
                                       fill=fill, base=-shift, pattern=[[-1, cols]],
                                       channel_multiplier=1).then_inc(fills, 1)
                    done += 1
                    pool.wait_ge(fills, done)
            pool.wait_ge(w_hi, 1)
            pool.tensor_tensor(w1_lo[:, :], w1_raw[:, :], w1_hi[:, :].bitcast(F32),
                               ALU.subtract).then_inc(w_lo, 1)

            def add(n, nth, it, k):
                pool.wait_ge(y_out, n * 8 + 2 * nth + 2)
                wait_count(pool, added, n * 3 + nth - 1)
                pool.tensor_tensor(acc[:, :, :], term[0][:, :, :] if nth == 1 else acc[:, :, :],
                                   term[nth][:, :, :], ALU.add).then_inc(added, 1)

            def step(it, k):
                f, a, z = (it, k), before(it, k, PER, 1), before(it, k, PER, 2)
                own, mid, end = (stands(*i, PER, STEPS) for i in (f, a, z))
                n = it * PER + k
                if own:
                    at, _ = misc(it, k, "center1")
                    pool.wait_ge(misc_out, at + 1)
                    pool.tensor_tensor(sq[:, :], cen[:, :], cen[:, :], ALU.mult).then_inc(squared, 1)
                if end:
                    add(z[0] * PER + z[1], 3, *z)
                if own:
                    pool.wait_ge(var_done, n + 1)
                    pool.tensor_tensor(rstd[:, :], var_eps[:, :], neg_half[:, :], ALU.pow).then_inc(rstd_done, 1)
                if mid:
                    if not isinstance(it, int) or end:
                        at, _ = misc(it, k, "result")
                        pool.wait_ge(misc_in, at + 1)
                    add(a[0] * PER + a[1], 1, *a)
                if own:
                    pool.wait_ge(tok_hi, n + 1)
                    if mid:
                        pool.wait_ge(added, (n - 1) * 3 + 1)
                    pool.tensor_tensor(tok[k % 2][C:P, :, :], xn[C:P, :, :],
                                       tok[k % 2][C:P, :, :].bitcast(F32), ALU.subtract).then_inc(tok_lo, 1)
                if mid:
                    if own:
                        pool.wait_ge(tok_lo, n + 1)
                    add(a[0] * PER + a[1], 2, *a)

            rounds(pool, STEPS, PER, 2, step)

        @block.scalar
        def _(act):
            act.wait_ge(weights_in, WEIGHTS)
            nc.scalar.activation(w1_hi[:, :], w1_raw[:, :], ACT.Copy).then_inc(w_hi, 1)

            def gelu(it, k, slot):
                n = (it * PER + k) * SLOTS + slot
                act.wait_ge(h_done, n + 1)
                nc.scalar.activation(hid[slot % 8][:, :, :], h_ps[slot % 2][:, :, 0:T], ACT.Gelu,
                                     bias=b1_s[:, slot:slot + 1]).then_inc(gelu_done, 1)

            def widen(it, k, p):
                act.wait_ge(gate, (it * PER + k) * GATE_OPS + GATE_OPS)
                nc.scalar.activation(
                    wide[p][:, :, :, :],
                    weight2[:, :, 2 * p:2 * p + 2].unsqueeze(3).broadcast_to([SUB, NSUB, 2, C]),
                    ACT.Copy, scale=0.5).then_inc(wide_done, 1)

            def step(it, k):
                f, a = (it, k), before(it, k, PER, 1)
                own, mid = (stands(*i, PER, STEPS) for i in (f, a))
                n = it * PER + k
                for slot in range(SLOTS):
                    if mid:
                        gelu(*a, slot)
                        if slot in (1, 3, 5):
                            widen(*a, (slot + 1) // 2)
                    if own and slot == 11:
                        at, _ = misc(it, k, "rstd1")
                        act.wait_ge(misc_out, at + 1)
                        nc.scalar.activation(tok[k % 2][:, :, :], xn[:, :, :], ACT.Copy).then_inc(tok_hi, 1)
                    if own and slot == 13:
                        act.wait_ge(gate, n * GATE_OPS + 10)
                        nc.scalar.activation(tanh[:, :], gap[:, :], ACT.Tanh, scale=0.5).then_inc(tanh_done, 1)
                if own:
                    widen(it, k, 0)

            rounds(act, STEPS, PER, 1, step)

        @block.tensor
        def _(pe):
            pe.wait_ge(fills, 4 + E + 6)
            pe.wait_ge(w_lo, 1)
            pe.wait_ge(wg_ready, 1)

            def hidden(it, k, slot):
                n = (it * PER + k) * SLOTS + slot
                if slot == 0:
                    pe.wait_ge(tok_lo, it * PER + k + 1)
                wait_count(pe, gelu_done, n - 1)
                cols = slice(P * slot, P * (slot + 1))
                for part, last in ((w1_hi, False), (w1_lo, True)):
                    for t in range(2):
                        mm = nc.tensor.matmul(h_ps[slot % 2][:, t, 0:T], part[:, cols],
                                              tok[k % 2][:, t, :], start=not last, stop=last)
                mm.then_inc(h_done, 1)

            def outputs(it, k, p, u):
                n = it * PER + k
                t, blk = u // 2, u % 2
                if u == 0:
                    pe.wait_ge(gelu_done, n * SLOTS + 4 * p + 4)
                if blk == 0:
                    wait_count(pe, y_out, n * 8 + 2 * p + t - 1)
                for e in range(2):
                    hb = 4 * p + 2 * e + blk
                    mm = nc.tensor.matmul(y_ps[C * e:C * (e + 1), t, 0:T], w2_s[:, hb, :],
                                          hid[hb % 8][:, t, :], start=(blk == 0), stop=(blk == 1))
                if blk == 1:
                    mm.then_inc(y_done, 1)

            def use(it, k, name):
                at, bank = misc(it, k, name)
                wait_count(pe, misc_out, at - 1)
                return m_ps[bank]

            def front(it, k, slot):
                n = it * PER + k
                if slot == 0:
                    pe.wait_ge(xc_in[k], it * 32 + 32)
                    for t in range(2):
                        nc.tensor.matmul(use(it, k, f"center{t}")[:, 0:T], center[:, :],
                                         xc[k][:, t, :], start=True, stop=True).then_inc(misc_in, 1)
                if slot == 5:
                    bank = use(it, k, "gates")
                    pe.wait_ge(squared, n + 1)
                    for s in range(NSUB):
                        cols = slice(SUB * s, SUB * (s + 1))
                        nc.tensor.matmul(bank[0:SUB, s:s + 1], sq[:, cols], mean_col[:, :],
                                         start=True, stop=True)
                        mm = nc.tensor.matmul(bank[0:SUB, 64 + E * s:64 + E * (s + 1)], cen[:, cols],
                                              wg_half[:, :], start=True, stop=True)
                    mm.then_inc(misc_in, 1)
                if slot == 10:
                    pe.wait_ge(rstd_done, n + 1)
                    for t in range(2):
                        bank = use(it, k, f"rstd{t}")
                        for s in range(NSUB // 2):
                            i = t * NSUB // 2 + s
                            mm = nc.tensor.transpose(bank[:, SUB * s:SUB * (s + 1)],
                                                     rstd[:, i:i + 1].broadcast_to([SUB, P]),
                                                     ident[0:SUB, 0:SUB])
                        mm.then_inc(misc_in, 1)

            def weights(step, it, k, p):
                pe.wait_ge(wide_done, (it * PER + k) * PAIRS + p + 1)
                for t in range(2):
                    bank = use(*step, f"weight{p}{t}")
                    for s in range(NSUB // 2):
                        i = t * NSUB // 2 + s
                        mm = nc.tensor.transpose(bank[:, SUB * s:SUB * (s + 1)],
                                                 wide[p][:, i, :, :].rearrange("p e c -> p (e c)"),
                                                 ident[0:SUB, 0:SUB])
                    mm.then_inc(misc_in, 1)

            def result(step, it, k):
                bank = use(*step, "result")
                pe.wait_ge(added, (it * PER + k) * 3 + 3)
                for part, last in ((acc, False), (xc[k], True)):
                    for t in range(2):
                        mm = nc.tensor.matmul(bank[C * t:C * (t + 1), 0:T], twin[:, :],
                                              part[:, t, :], start=not last, stop=last)
                mm.then_inc(misc_in, 1)

            def step(it, k):
                f, a, z = (it, k), before(it, k, PER, 1), before(it, k, PER, 2)
                own, mid, end = (stands(*i, PER, STEPS) for i in (f, a, z))
                for slot in range(SLOTS):
                    p, u = slot // 4, slot % 4
                    if mid:
                        hidden(*a, slot)
                    if p > 0 and mid:
                        outputs(*a, p - 1, u)
                    if p == 0 and end:
                        outputs(*z, PAIRS - 1, u)
                    if own:
                        front(*f, slot)
                    if mid and slot in (1, 3, 6, 8):
                        weights(f, *a, (1, 3, 6, 8).index(slot))
                    if end and slot == 7:
                        result(f, *z)

            rounds(pe, STEPS, PER, 2, step)

        @block.vector
        def _(dve):
            dve.wait_ge(weights_in, WEIGHTS)
            nc.vector.tensor_scalar(wg_half[:, :], wg_raw[:, :], 0.5, None, ALU.mult).then_inc(wg_ready, 1)
            dve.wait_ge(fills, 4 + E + 6)

            def filled(it, k, name):
                at, bank = misc(it, k, name)
                dve.wait_ge(misc_in, at + 1)
                return m_ps[bank]

            def centered(it, k):
                for t in range(2):
                    nc.vector.tensor_copy(cen[:, T * t:T * (t + 1)],
                                          filled(it, k, f"center{t}")[:, 0:T]).then_inc(misc_out, 1)

            def gates(it, k):
                n = it * PER + k
                bank = filled(it, k, "gates")
                nc.vector.tensor_scalar(var_eps[:, :], bank[0:SUB, 0:NSUB], EPS_T, None,
                                        ALU.add).then_inc(var_done, 1)
                nc.vector.tensor_copy(logit[:, :, :], bank[0:SUB, 64:64 + NSUB * E]
                                      .rearrange("p (s e) -> p s e", e=E)).then_inc(misc_out, 1)

            def normalise(it, k):
                n = it * PER + k
                wait_count(dve, tok_lo, n)
                for t in range(2):
                    nc.vector.tensor_tensor(xn[:, t, :], cen[:, T * t:T * (t + 1)],
                                            filled(it, k, f"rstd{t}")[:, 0:T], ALU.mult).then_inc(misc_out, 1)

            def each(stat):
                return stat[:, :].unsqueeze(2).broadcast_to([SUB, NSUB, E])

            def pick_experts(it, k):
                n = it * PER + k
                base = n * GATE_OPS
                dve.wait_ge(rstd_done, n + 1)
                at, _ = misc(it, k, "gates")
                dve.wait_ge(misc_out, at + 1)
                nc.vector.tensor_tensor(logit[:, :, :], logit[:, :, :], each(rstd), ALU.mult).then_inc(gate, 1)
                dve.wait_ge(gate, base + 1)
                nc.vector.tensor_tensor(logit[:, :, :], logit[:, :, :],
                                        bg_s[:, :].unsqueeze(1).broadcast_to([SUB, NSUB, E]),
                                        ALU.add).then_inc(gate, 1)
                dve.wait_ge(gate, base + 2)
                nc.vector.tensor_reduce(top1[:, :], logit[:, :, :], AX_X, ALU.max).then_inc(gate, 1)
                dve.wait_ge(gate, base + 3)
                nc.vector.tensor_tensor(match[:, :, :], logit[:, :, :], each(top1), ALU.is_equal).then_inc(gate, 1)
                dve.wait_ge(gate, base + 4)
                nc.vector.tensor_tensor(match[:, :, :], match[:, :, :], rank[:, :, :], ALU.mult).then_inc(gate, 1)
                dve.wait_ge(gate, base + 5)
                nc.vector.tensor_reduce(best[:, :], match[:, :, :], AX_X, ALU.max).then_inc(gate, 1)
                dve.wait_ge(gate, base + 6)
                nc.vector.tensor_tensor(first[:, :, :], match[:, :, :], each(best), ALU.is_equal).then_inc(gate, 1)
                dve.wait_ge(gate, base + 7)
                nc.vector.scalar_tensor_tensor(rest[:, :, :], first[:, :, :], -3.0e38, logit[:, :, :],
                                               ALU.mult, ALU.add).then_inc(gate, 1)
                dve.wait_ge(gate, base + 8)
                nc.vector.tensor_reduce(top2[:, :], rest[:, :, :], AX_X, ALU.max).then_inc(gate, 1)
                dve.wait_ge(gate, base + 9)
                nc.vector.tensor_tensor(gap[:, :], top2[:, :], top1[:, :], ALU.subtract).then_inc(gate, 1)
                nc.vector.tensor_tensor(match[:, :, :], rest[:, :, :], each(top2), ALU.is_equal).then_inc(gate, 1)
                dve.wait_ge(gate, base + 11)
                nc.vector.tensor_tensor(match[:, :, :], match[:, :, :], rank[:, :, :], ALU.mult).then_inc(gate, 1)
                dve.wait_ge(gate, base + 12)
                nc.vector.tensor_reduce(best[:, :], match[:, :, :], AX_X, ALU.max).then_inc(gate, 1)
                dve.wait_ge(gate, base + 13)
                nc.vector.tensor_tensor(second[:, :, :], match[:, :, :], each(best), ALU.is_equal).then_inc(gate, 1)
                dve.wait_ge(gate, base + 14)
                nc.vector.tensor_tensor(either[:, :, :], first[:, :, :], second[:, :, :], ALU.add).then_inc(gate, 1)
                nc.vector.tensor_tensor(second[:, :, :], second[:, :, :], first[:, :, :],
                                        ALU.subtract).then_inc(gate, 1)

            def weigh_experts(it, k):
                n = it * PER + k
                base = n * GATE_OPS
                dve.wait_ge(tanh_done, n + 1)
                dve.wait_ge(gate, base + 16)
                nc.vector.tensor_tensor(second[:, :, :], second[:, :, :], each(tanh), ALU.mult).then_inc(gate, 1)
                wait_count(dve, wide_done, n * PAIRS)
                dve.wait_ge(gate, base + 17)
                nc.vector.tensor_tensor(weight2[:, :, :], either[:, :, :], second[:, :, :],
                                        ALU.add).then_inc(gate, 1)

            def weights(step, p):
                for t in range(2):
                    nc.vector.tensor_copy(wt[p][:, t, :],
                                          filled(*step, f"weight{p}{t}")[:, 0:T]).then_inc(misc_out, 1)

            def weighted(step, it, k, p, t):
                n = it * PER + k
                dve.wait_ge(y_done, n * 8 + 2 * p + t + 1)
                ahead = step if p < PAIRS - 1 else before(*step, PER, 1)
                dve.wait_ge(misc_out, misc(*ahead, f"weight{p}{t}")[0] + 1)
                wait_count(dve, added, (n - 1) * 3 + max(p, 1))
                nc.vector.scalar_tensor_tensor(term[p][:, t, :], y_ps[:, t, 0:T], b2_s[:, p:p + 1],
                                               wt[p][:, t, :], ALU.add, ALU.mult).then_inc(y_out, 1)

            def result(step, it, k):
                bank = filled(*step, "result")
                wait_count(dve, res_out[k % 2], (it * 2 + k // 2) * 2 * 16)
                nc.vector.tensor_copy(res[k % 2][:, :], bank[:, 0:T]).then_inc(misc_out, 1)

            def step(it, k):
                f, a, z = (it, k), before(it, k, PER, 1), before(it, k, PER, 2)
                own, mid, end = (stands(*i, PER, STEPS) for i in (f, a, z))
                for slot in range(SLOTS):
                    if own and slot == 0:
                        centered(*f)
                    if mid and slot in (1, 3, 6, 8):
                        weights(f, (1, 3, 6, 8).index(slot))
                    if end and slot in (1, 3):
                        weighted(f, *z, PAIRS - 1, slot // 2)
                    if mid and slot in (5, 7, 9, 11, 13, 15):
                        weighted(f, *a, slot // 4 - 1, slot % 4 // 2)
                    if own and slot == 5:
                        gates(*f)
                    if end and slot == 7:
                        result(f, *z)
                    if own and slot == 10:
                        normalise(*f)
                    if own and slot == 11:
                        pick_experts(*f)
                    if own and slot == 14:
                        weigh_experts(*f)

            rounds(dve, STEPS, PER, 2, step)


_INS = ["x", "L0_conv_w1", "L0_conv_b1", "L0_conv_gamma", "L0_conv_beta", "L0_conv_w2", "L0_conv_b2",
        "L0_ffn_Wg", "L0_ffn_bg", "L0_ffn_W1", "L0_ffn_b1", "L0_ffn_W2", "L0_ffn_b2"]
_OUTS = [((B, C, H, W), "float32")]


def kernel(**inputs):
    import numpy as _np
    import concourse.bacc as _bacc
    from concourse import mybir as _mybir
    from concourse.bass_utils import run_bass_kernel_spmd as _run

    nc = _bacc.Bacc("TRN2", target_bir_lowering=False, num_devices=1)
    arrays, args = {}, []
    for name in _INS:
        a = _np.ascontiguousarray(inputs[name])
        arrays[f"in_{name}_dram"] = a
        args.append(nc.dram_tensor(f"in_{name}_dram", a.shape, _mybir.dt.from_np(a.dtype), kind="ExternalInput").ap())
    for i, (shape, dtype) in enumerate(_OUTS):
        dt = _mybir.dt.from_np(_np.dtype(dtype))
        args.append(nc.dram_tensor(f"out_{i}_dram", shape, dt, kind="ExternalOutput").ap())
    metaformer_block(nc, *args)
    r = _run(nc, [arrays], core_ids=[0])
    return r.results[0]["out_0_dram"]
```

```python
from contextlib import ExitStack

import concourse.bass as bass
from concourse import mybir

F32 = mybir.dt.float32
F32R = mybir.dt.float32r
ALU = mybir.AluOpType
ACT = mybir.ActivationFunctionType
AX_X = mybir.AxisListType.X

P = 128

B, C, H, W = 16, 64, 56, 56
HW = H * W
K = 7
PAD = K // 2
G = 16
D = C // G
CR = 16
F = CR + 1
E = 8
HID = 256
HB = E * HID // P
EPS_C, EPS_BN, EPS_T = 1e-6, 1e-5, 1e-5

PARITY = 2
P8 = B // PARITY
T = 392
TR = T // W
UNIT = 2 * T
UNITS = HW // UNIT
SUB = 98
NSUB = UNIT // SUB
WP = 64
MROWS = 7
MF = MROWS * F
BLOCKS = H // MROWS
STRIP_BLOCKS = ((0, 1), (2,), (3,), (4,), (5,), (6, 7))
IN0 = (0, 11, 18, 25, 32, 39)
KR = (17, 16, 16, 16, 16, 17)
STRIPS = len(IN0)
KP = max(KR) * K
BAND0 = 1
TAP0 = BAND0 + 2 * MROWS - 1
TL = 40
BN = (max(IN0[b] - MROWS * m for b, blocks in enumerate(STRIP_BLOCKS) for m in blocks)
      + TAP0 - BAND0 + PAD + 1) * F
HALF_BLOCKS = BLOCKS // 2
HALF_ROWS = H // 2
PICK0 = HALF_ROWS - 1
CH = 4
CN = D * 2 * W
UNITS_OF = [(r, [(m, q) for m in blocks] if len(blocks) == 2 else [(blocks[0], q), (blocks[0], q + 1)])
            for r, blocks in enumerate(STRIP_BLOCKS) for q in range(0, CH, 3 - len(blocks))]
NU = len(UNITS_OF)
LAST_UNIT = [max(u for u, (s, _) in enumerate(UNITS_OF) if s == r) for r in range(STRIPS)]
BANK_OF = [u % 3 for u in range(NU - 1)] + [1]

XS_H = C * P8 * WP
XS_SIZE = PARITY * H * XS_H
V_J = TL * F
V_G = K * V_J
V_SIZE = G * V_G


def before(it, k, per, lag):
    return (it, k - lag) if k >= lag else (it - 1, k - lag + per)


def stands(it, k, per, total):
    return not isinstance(it, int) or 0 <= it * per + k < total


def rounds(eng, total, per, tail, step):
    for k in range(per):
        step(0, k)
    with eng.Fori(1, total // per) as it:
        for k in range(per):
            step(it, k)
    for k in range(tail):
        step(total // per, k)


def wait_count(eng, sem, count):
    if not isinstance(count, int) or count > 0:
        eng.wait_ge(sem, count)


def metaformer_block(nc, x, conv_w1, conv_b1, gamma, beta, conv_w2, conv_b2,
                     wg, bg, w1, b1, w2, b2, out):
    xs = nc.dram_tensor("xs", (XS_SIZE + WP,), F32)
    rs = nc.dram_tensor("rs", (H, PARITY, CR, P8, W), F32)
    ones = nc.dram_tensor("ones_rows", (MROWS, BLOCKS * PARITY * P8 * W), F32)
    vf = nc.dram_tensor("vf", (V_SIZE,), F32)
    co = nc.dram_tensor("co", (PARITY, C, H, P8, W), F32)
    with ExitStack() as kept:
        ident = kept.enter_context(nc.sbuf_tensor("ident", [P, P], F32))
        affine = kept.enter_context(nc.sbuf_tensor("affine", [MF, 2], F32))
        ident_r = kept.enter_context(nc.sbuf_tensor("ident_r", [P, P], F32R))
        sel = kept.enter_context(nc.sbuf_tensor("sel", [P, E, C], F32R))
        norm_stage(nc, x, conv_w1, conv_b1, gamma, beta, conv_w2, conv_b2, xs, rs, ones, vf,
                   ident, affine, ident_r, sel)
        conv_stage(nc, xs, rs, ones, vf, co, affine)
        moe_stage(nc, x, co, wg, bg, w1, b1, w2, b2, out, ident_r, sel)


def norm_stage(nc, x, conv_w1, conv_b1, gamma, beta, conv_w2, conv_b2, xs, rs, ones_rows, vf,
               ident, affine, ident_r, sel):
    STEPS = P8 * UNITS
    PER = 2 * UNITS
    PAIR_ROWS = H // UNITS
    GROUPS = 4

    with ExitStack() as ctx:
        def sb(name, shape, dt=F32):
            return ctx.enter_context(nc.sbuf_tensor(name, shape, dt))

        def ps(name, shape):
            return ctx.enter_context(nc.psum_tensor(name, shape, F32))

        def sem(name):
            return ctx.enter_context(nc.semaphore(name))

        center = sb("center", [P, P])
        mean_col = sb("mean_col", [P, 2])
        w1t = sb("w1t", [P, 2 * CR])
        b1c = sb("b1c", [P, 1])
        eps_c = sb("eps_c", [P, 1])
        eps_bn = sb("eps_bn", [P, 1])
        avg = sb("avg", [P, CR])
        spread = sb("spread", [F, MF])
        zeros = sb("zeros", [P, V_SIZE // P])
        sel_raw = sb("sel_raw", [P, E, C])
        ones = sb("ones", [MROWS * BLOCKS * PARITY, P8 * W])
        xin = sb("xin", [P, P8, HW])
        xpad = [sb(f"xpad{i}", [P, PAIR_ROWS, 2, WP]) for i in range(UNITS)]
        cen = [sb(f"cen{i}", [P, 2, T]) for i in range(4)]
        sq = [sb(f"sq{i}", [P, 2, T]) for i in range(2)]
        std = sb("std", [SUB, NSUB, 2])
        rstd = sb("rstd", [SUB, NSUB, 2])
        rstd_wide = sb("rstd_wide", [SUB, NSUB, 2, C])
        rt = [sb(f"rt{i}", [P, T]) for i in range(2)]
        stats = sb("stats", [P, STEPS // 2, 6])
        mv = sb("mv", [P, 2])
        m2 = sb("m2", [P, 1])
        chan = sb("chan", [CR, 6])
        gb = sb("gb", [CR, 2])
        ab = sb("ab", [F, 2])
        cen_ps = [ps(f"cen_ps{i}", [P, 2, 512]) for i in range(2)]
        wide_ps = ps("wide_ps", [P, 2, 512])
        var_ps = ps("var_ps", [P, 512])
        r_ps = ps("r_ps", [P, 512])

        weights_in = sem("weights_in")
        cleared = sem("cleared")
        pads_clear = sem("pads_clear")
        shaped = sem("shaped")
        blanks_done = sem("blanks_done")
        filters_out = sem("filters_out")
        x_in = [sem(f"x_in{i}") for i in range(2)]
        centered = sem("centered")
        cen_out = sem("cen_out")
        squared = sem("squared")
        var_done = sem("var_done")
        std_done = sem("std_done")
        rstd_own = sem("rstd_own")
        rstd_done = sem("rstd_done")
        wide_done = sem("wide_done")
        normed = sem("normed")
        r_done = sem("r_done")
        rt_done = sem("rt_done")
        stats_done = sem("stats_done")
        rs_out = [sem(f"rs_out{i}") for i in range(2)]
        xs_out = [sem(f"xs_out{i}") for i in range(UNITS)]
        bn_own = sem("bn_own")
        bn_pe = sem("bn_pe")
        bn_sqrt = sem("bn_sqrt")
        rounded = sem("rounded")

        xs_map = xs[0:XS_SIZE].rearrange("(i h c x) -> i c h x", i=PARITY, h=H, c=C)
        vf_map = vf[:].rearrange("(g j t f) -> g j t f", g=G, j=K, t=TL)
        w2_map = conv_w2.rearrange("(i j g) c -> i g j c", i=K, j=K)
        b2_map = conv_b2.rearrange("(i j g u) -> i g j u", i=K, j=K, u=1)
        WEIGHTS = 2 + 8 + 2
        CLEARED = 15

        block = ctx.enter_context(nc.Block())

        @block.sync
        def _(sp):
            x_pairs = x.rearrange("(p i) c h w -> p (i c) (h w)", i=PARITY)
            def load(pair):
                if pair >= 2:
                    sp.wait_ge(x_in[pair % 2], pair // 2 * 16)
                sp.dma_start(xin[:, pair, :], x_pairs[pair]).then_inc(x_in[pair % 2], 16)

            load(0)
            load(1)
            sp.wait_ge(cleared, 3)
            sp.dma_start(vf[:].rearrange("(p x) -> p x", p=P), zeros[:, :]).then_inc(blanks_done, 16)
            sp.dma_start(xs[XS_SIZE:XS_SIZE + WP].rearrange("(a x) -> a x", a=1),
                         zeros[0:1, 0:WP]).then_inc(blanks_done, 16)
            sp.dma_start(ones_rows.rearrange("j (x w) -> (j x) w", w=P8 * W),
                         ones[:, :]).then_inc(blanks_done, 16)
            for pair in range(2, P8):
                load(pair)

            def step(it, k):
                j, v = before(it, k, PER, 3)
                if v % 2 == 0 or not stands(j, v, PER, STEPS):
                    return
                u = v // 2
                grp = u % 2
                sp.wait_ge(rt_done, j * UNITS + u + 1)
                for q in range(4):
                    row = PAIR_ROWS * u + TR * (q % 2)
                    dst = rs[row:row + TR, :, :, bass.ds(j * 2 + q // 2, 1), :]
                    sp.dma_start(dst.rearrange("h i c u w -> (i c) h (u w)"),
                                 rt[grp][32 * q:32 * (q + 1), :]
                                 .rearrange("c (h w) -> c h w", h=TR)).then_inc(rs_out[grp], 16)
                for i in range(PARITY):
                    sp.dma_start(xs_map[i][:, PAIR_ROWS * u:PAIR_ROWS * (u + 1), bass.ds(j * 2 * WP, 2 * WP)],
                                 xpad[u][C * i:C * (i + 1), :, :, :].rearrange("c h p w -> c h (p w)")
                                 ).then_inc(xs_out[u], 16)

            rounds(sp, STEPS, PER, 3, step)
            sp.wait_ge(blanks_done, 3 * 16)
            sp.wait_ge(filters_out, 2 * K * 16)
            for i in range(2):
                sp.wait_ge(rs_out[i], STEPS // 4 * 4 * 16)
            for u in range(UNITS):
                sp.wait_ge(xs_out[u], P8 // 2 * PARITY * 16)

        @block.gpsimd
        def _(pool):
            blank = [(zeros[:, :], 0.0), (ones[:, :], 1.0), (w1t[:, :], 0.0), (ident[:, :], 0.0),
                     (avg[:, :], 0.0), (spread[:, :], 0.0), (center[:, :], 0.0), (mean_col[:, :], 0.0),
                     (eps_c[:, :], EPS_C), (eps_bn[:, :], EPS_BN),
                     (sel_raw[:, :, :], 0.0)]
            for i in range(PARITY):
                half = slice(C * i, C * (i + 1))
                blank += [(center[half, half], -1.0 / C), (mean_col[half, i:i + 1], 1.0 / C)]
            assert len(blank) == CLEARED
            for n, (part, value) in enumerate(blank):
                pool.memset(part, value).then_inc(cleared, 1)
                pool.wait_ge(cleared, n + 1)
            pool.affine_select(out=ident[:, :], in_=ident[:, :], compare_op=ALU.not_equal, fill=1.0,
                               base=0, pattern=[[-1, P]], channel_multiplier=1).then_inc(shaped, 1)
            pool.wait_ge(shaped, 1)
            pool.affine_select(out=center[:, :], in_=center[:, :], compare_op=ALU.not_equal,
                               fill=1.0 - 1.0 / C, base=0, pattern=[[-1, P]],
                               channel_multiplier=1).then_inc(shaped, 1)
            pool.wait_ge(shaped, 2)
            wide = spread[:, :].rearrange("p (r f) -> p r f", r=MROWS)
            pool.affine_select(out=wide, in_=wide, compare_op=ALU.not_equal, fill=1.0, base=0,
                               pattern=[[0, MROWS], [-1, F]], channel_multiplier=1).then_inc(shaped, 1)
            for n in range(P // CR):
                pool.wait_ge(shaped, 3 + n)
                pool.affine_select(out=avg[:, :], in_=avg[:, :], compare_op=ALU.not_equal,
                                   fill=CR / P, base=-CR * n, pattern=[[-1, CR]],
                                   channel_multiplier=1).then_inc(shaped, 1)
            for h in range(2):
                pool.wait_ge(shaped, 3 + P // CR + h)
                pool.affine_select(out=sel_raw[:, :, :], in_=sel_raw[:, :, :], compare_op=ALU.not_equal,
                                   fill=1.0, base=-E * h, pattern=[[-1, E], [0, C]],
                                   channel_multiplier=1).then_inc(shaped, 1)
            pool.wait_ge(blanks_done, 3 * 16)
            for i in range(K):
                pool.dma_start(vf_map[:, 0:K, TAP0 + i, 0:CR], w2_map[i]).then_inc(filters_out, 16)
                pool.dma_start(vf_map[:, 0:K, TAP0 + i, CR:F], b2_map[i],
                               allow_slow_non_contiguous=True).then_inc(filters_out, 16)

        @block.scalar
        def _(act):
            act.wait_ge(cleared, 3)
            for i in range(PARITY):
                act.dma_start(w1t[C * i:C * (i + 1), CR * i:CR * (i + 1)],
                              conv_w1.rearrange("o c -> c o"), allow_slow_non_contiguous=True).then_inc(weights_in, 16)
            for n in range(P // CR):
                act.dma_start(b1c[CR * n:CR * (n + 1), :],
                              conv_b1.rearrange("(c u) -> c u", u=1)).then_inc(weights_in, 16)
            act.dma_start(gb[:, 0:1], gamma.rearrange("(c u) -> c u", u=1)).then_inc(weights_in, 16)
            act.dma_start(gb[:, 1:2], beta.rearrange("(c u) -> c u", u=1)).then_inc(weights_in, 16)
            act.wait_ge(weights_in, WEIGHTS * 16)
            act.wait_ge(cleared, CLEARED)

            def center_and_square(it, k):
                n = it * PER + k
                act.wait_ge(centered, n + 1)
                wait_count(act, normed, n - 3)
                nc.scalar.activation(cen[k % 4][:, :, :], cen_ps[k % 2][:, :, 0:T],
                                     ACT.Copy).then_inc(cen_out, 1)
                wait_count(act, var_done, n - 1)
                act.wait_ge(cen_out, n + 1)
                nc.scalar.activation(sq[k % 2][:, :, :], cen[k % 4][:, :, :],
                                     ACT.Square).then_inc(squared, 1)

            def deviation(it, k):
                n = it * PER + k
                act.wait_ge(var_done, n + 1)
                wait_count(act, rstd_own, n)
                nc.scalar.activation(std[:, :, :], var_ps[0:SUB, 0:2 * NSUB]
                                     .rearrange("p (s i) -> p s i", i=2), ACT.Sqrt,
                                     bias=eps_c[0:SUB, :]).then_inc(std_done, 1)

            def r_tiles(it, k):
                if k % 2 == 0:
                    return
                grp = k // 2 % 2
                count = it * GROUPS + k // 2
                act.wait_ge(r_done, it * PER + k + 1)
                wait_count(act, rs_out[grp], (it * 2 + k // 4) * 4 * 16)
                wait_count(act, stats_done, count - 1)
                nc.scalar.activation(rt[grp][:, :], r_ps[:, 0:T], ACT.Identity,
                                     bias=b1c[:, :]).then_inc(rt_done, 1)

            def step(it, k):
                if stands(it, k, PER, STEPS):
                    center_and_square(it, k)
                a = before(it, k, PER, 1)
                if stands(*a, PER, STEPS):
                    deviation(*a)
                a = before(it, k, PER, 3)
                if stands(*a, PER, STEPS):
                    r_tiles(*a)

            rounds(act, STEPS, PER, 3, step)
            nc.scalar.activation(ident_r[:, :], ident[:, :], ACT.Copy).then_inc(rounded, 1)
            act.wait_ge(shaped, 5 + P // CR)
            nc.scalar.activation(sel[:, :, :], sel_raw[:, :, :], ACT.Copy).then_inc(rounded, 1)
            act.wait_ge(rounded, 2)
            act.wait_ge(bn_own, 6)
            nc.scalar.activation(chan[:, 3:4], chan[:, 2:3], ACT.Sqrt,
                                 bias=eps_bn[0:CR, :]).then_inc(bn_sqrt, 1)

        @block.tensor
        def _(pe):
            pe.wait_ge(shaped, 3 + P // CR)
            pe.wait_ge(weights_in, WEIGHTS * 16)

            def center_unit(it, k):
                n = it * PER + k
                if k < 2:
                    pe.wait_ge(x_in[k], it * 16 + 16)
                wait_count(pe, cen_out, n - 1)
                pair = xin[:, bass.ds(it * 2 + k % 2, 1), :].rearrange("p u n -> p (u n)")
                for t in range(2):
                    at = (2 * (k // 2) + t) * T
                    mm = nc.tensor.matmul(cen_ps[k % 2][:, t, 0:T], center[:, :],
                                          pair[:, at:at + T], start=True, stop=True)
                mm.then_inc(centered, 1)

            def variances(it, k):
                n = it * PER + k
                pe.wait_ge(squared, n + 1)
                wait_count(pe, std_done, n)
                flat = sq[k % 2][:, :, :].rearrange("p a t -> p (a t)")
                for s in range(NSUB):
                    mm = nc.tensor.matmul(var_ps[0:SUB, 2 * s:2 * s + 2],
                                          flat[:, SUB * s:SUB * (s + 1)], mean_col[:, :],
                                          start=True, stop=True)
                mm.then_inc(var_done, 1)

            def widen(it, k):
                n = it * PER + k
                pe.wait_ge(rstd_done, n + 1)
                wait_count(pe, normed, n)
                for s in range(NSUB):
                    t, at = s // (NSUB // 2), s % (NSUB // 2) * SUB
                    mm = nc.tensor.transpose(wide_ps[:, t, at:at + SUB],
                                             rstd_wide[:, s, :, :].rearrange("p i c -> p (i c)"),
                                             ident[0:SUB, 0:SUB])
                mm.then_inc(wide_done, 1)

            def reduce_channels(it, k):
                n = it * PER + k
                pe.wait_ge(normed, n + 1)
                if k % 2 == 0:
                    wait_count(pe, rt_done, it * GROUPS + k // 2)
                for t in range(2):
                    q = 2 * (k % 2) + t
                    mm = nc.tensor.matmul(r_ps[32 * q:32 * (q + 1), 0:T], w1t[:, :],
                                          xpad[k // 2][:, TR * t:TR * (t + 1), k % 2, PAD:PAD + W],
                                          start=True, stop=True)
                mm.then_inc(r_done, 1)

            def step(it, k):
                if stands(it, k, PER, STEPS):
                    center_unit(it, k)
                a = before(it, k, PER, 1)
                if stands(*a, PER, STEPS):
                    variances(*a)
                a = before(it, k, PER, 3)
                if stands(*a, PER, STEPS):
                    reduce_channels(*a)
                a = before(it, k, PER, 2)
                if stands(*a, PER, STEPS):
                    widen(*a)

            rounds(pe, STEPS, PER, 3, step)
            pe.wait_ge(bn_own, 3)
            nc.tensor.matmul(var_ps[0:CR, 64:66], avg[:, :], mv[:, :], start=True,
                             stop=True).then_inc(bn_pe, 1)
            pe.wait_ge(bn_own, 10)
            nc.tensor.matmul(var_ps[0:MF, 128:130], spread[:, :], ab[:, :], start=True,
                             stop=True).then_inc(bn_pe, 1)

        @block.vector
        def _(dve):
            for u in range(UNITS):
                nc.vector.memset(xpad[u][:, :, :, :], 0.0).then_inc(pads_clear, 1)
            dve.wait_ge(pads_clear, UNITS)

            def reciprocals(it, k):
                n = it * PER + k
                dve.wait_ge(std_done, n + 1)
                nc.vector.reciprocal(rstd[:, :, :], std[:, :, :]).then_inc(rstd_own, 1)
                wait_count(dve, wide_done, n)
                dve.wait_ge(rstd_own, n + 1)
                nc.vector.tensor_copy(rstd_wide[:, :, :, :],
                                      rstd[:, :, :].unsqueeze(3).broadcast_to([SUB, NSUB, 2, C])
                                      ).then_inc(rstd_done, 1)

            def normalise(it, k):
                n = it * PER + k
                dve.wait_ge(wide_done, n + 1)
                if k % 2 == 0:
                    wait_count(dve, xs_out[k // 2], it * PARITY * 16)
                nc.vector.tensor_tensor(
                    xpad[k // 2][:, :, k % 2, PAD:PAD + W].rearrange("p (a r) w -> p a r w", a=2),
                    cen[k % 4][:, :, :].rearrange("p a (r w) -> p a r w", w=W),
                    wide_ps[:, :, 0:T].rearrange("p a (r w) -> p a r w", w=W),
                    ALU.mult).then_inc(normed, 1)

            def statistics(it, k):
                if k % 2 == 0:
                    return
                count = it * GROUPS + k // 2
                dve.wait_ge(rt_done, count + 1)
                nc.vector.bn_stats(stats[:, bass.ds(count, 1), :].rearrange("p u s -> p (u s)"),
                                   rt[k // 2 % 2][:, :]).then_inc(stats_done, 1)

            def step(it, k):
                a = before(it, k, PER, 2)
                if stands(*a, PER, STEPS):
                    normalise(*a)
                a = before(it, k, PER, 1)
                if stands(*a, PER, STEPS):
                    reciprocals(*a)
                a = before(it, k, PER, 3)
                if stands(*a, PER, STEPS):
                    statistics(*a)

            rounds(dve, STEPS, PER, 3, step)

            dve.wait_ge(stats_done, STEPS // 2)
            nc.vector.bn_aggr(mv[:, :], stats[:, :, :].rearrange("p n s -> p (n s)")).then_inc(bn_own, 1)
            dve.wait_ge(bn_own, 1)
            nc.vector.tensor_tensor(m2[:, :], mv[:, 0:1], mv[:, 0:1], ALU.mult).then_inc(bn_own, 1)
            dve.wait_ge(bn_own, 2)
            nc.vector.tensor_tensor(mv[:, 1:2], mv[:, 1:2], m2[:, :], ALU.add).then_inc(bn_own, 1)
            dve.wait_ge(bn_pe, 1)
            nc.vector.tensor_copy(chan[:, 0:2], var_ps[0:CR, 64:66]).then_inc(bn_own, 1)
            dve.wait_ge(bn_own, 4)
            nc.vector.tensor_tensor(chan[:, 4:5], chan[:, 0:1], chan[:, 0:1], ALU.mult).then_inc(bn_own, 1)
            dve.wait_ge(bn_own, 5)
            nc.vector.tensor_tensor(chan[:, 2:3], chan[:, 1:2], chan[:, 4:5], ALU.subtract).then_inc(bn_own, 1)
            nc.vector.memset(ab[:, 0:1], 0.0).then_inc(bn_own, 1)
            nc.vector.memset(ab[:, 1:2], 1.0).then_inc(bn_own, 1)
            dve.wait_ge(bn_sqrt, 1)
            nc.vector.reciprocal(chan[:, 4:5], chan[:, 3:4]).then_inc(bn_sqrt, 1)
            dve.wait_ge(bn_sqrt, 2)
            dve.wait_ge(bn_own, 8)
            dve.wait_ge(weights_in, WEIGHTS * 16)
            nc.vector.tensor_tensor(ab[0:CR, 0:1], gb[:, 0:1], chan[:, 4:5], ALU.mult).then_inc(bn_own, 1)
            dve.wait_ge(bn_own, 9)
            nc.vector.tensor_tensor(chan[:, 5:6], chan[:, 0:1], ab[0:CR, 0:1], ALU.mult).then_inc(bn_sqrt, 1)
            dve.wait_ge(bn_sqrt, 3)
            nc.vector.tensor_tensor(ab[0:CR, 1:2], gb[:, 1:2], chan[:, 5:6], ALU.subtract).then_inc(bn_own, 1)
            dve.wait_ge(bn_pe, 2)
            nc.vector.tensor_copy(affine[:, :], var_ps[0:MF, 128:130]).then_inc(bn_own, 1)
            dve.wait_ge(bn_own, 11)


def conv_stage(nc, xs, rs, ones_rows, vf, co, affine):
    STEPS = G * PARITY
    PER = 2 * PARITY
    XN = D * P8 * WP
    XP = XN * 3 // 4
    XR, PR = 4, 2
    HALVES = 2

    with ExitStack() as ctx:
        def sb(name, shape, dt=F32):
            return ctx.enter_context(nc.sbuf_tensor(name, shape, dt))

        def sem(name):
            return ctx.enter_context(nc.semaphore(name))

        r_all = sb("r_all", [MF, BLOCKS, PARITY, P8 * W])
        pick = sb("pick", [MF, PICK0 + 32])
        xq = [sb(f"xq{i}", [KP, XN]) for i in range(XR)]
        xq_hi = [sb(f"xq_hi{i}", [KP, XN], F32R) for i in range(XR)]
        xq_lo = [sb(f"xq_lo{i}", [KP, XN], F32R) for i in range(XR)]
        band = [sb(f"band{i}", [KP, BN]) for i in range(2)]
        band_hi = [sb(f"band_hi{i}", [KP, BN], F32R) for i in range(2)]
        band_lo = [sb(f"band_lo{i}", [KP, BN], F32R) for i in range(2)]
        prod = [sb(f"prod{i}", [MF, 2 * CH, CN]) for i in range(PR)]
        ob = [sb(f"ob{i}", [P, CN]) for i in range(HALVES)]
        z_ps = [ctx.enter_context(nc.psum_tensor(f"z_ps{i}", [P, 2, 512], F32)) for i in range(3)]
        o_ps = [ctx.enter_context(nc.psum_tensor(f"o_ps{i}", [P, 512], F32)) for i in range(HALVES)]

        r_in = [sem(f"r_in{i}") for i in range(3)]
        r_ready = sem("r_ready")
        pick_own = sem("pick_own")
        x_in = [sem(f"xq_in{i}") for i in range(XR)]
        x_edge = [sem(f"xq_edge{i}") for i in range(2)]
        band_in = [sem(f"band_in{i}") for i in range(2)]
        x_hi = sem("x_hi")
        x_lo_pool = sem("x_lo_pool")
        x_lo_dve = sem("x_lo_dve")
        b_hi = sem("b_hi")
        b_lo = sem("b_lo")
        z_done = sem("z_done")
        weighted = sem("weighted")
        summed = sem("summed")
        ob_done = sem("ob_done")
        ob_out = [sem(f"ob_out{i}") for i in range(HALVES)]

        block = ctx.enter_context(nc.Block())

        def strip(it, k, r):
            return (it * PER + k) * STRIPS + r

        def slot_of(k, r):
            return (k * STRIPS + r) % XR

        def slot_free(it, k, r):
            j, v = (it, k) if r >= XR else before(it, k, PER, 1)
            return (j * PER + v) * NU + LAST_UNIT[(r - XR) % STRIPS] + 1

        def half_of(r):
            return STRIP_BLOCKS[r][0] // HALF_BLOCKS

        R_PARTS = ((0, 2, 0), (2, BLOCKS, 0), (0, BLOCKS, 1))
        R_SLOTS = (0, 1, 4)

        @block.sync
        def _(sp):
            def load_maps(it, k, r):
                slot = slot_of(k, r)
                wait_count(sp, x_lo_pool, strip(it, k, r) - XR + 1)
                wait_count(sp, x_lo_dve, strip(it, k, r) - XR + 1)
                top, par = IN0[r], k % PARITY
                rows = xs[0:XS_SIZE].rearrange("(i h g x) -> i h g x", i=PARITY, h=H, g=G)[
                    par, top:top + KR[r], bass.ds(it * 2 + k // PARITY, 1), :]
                src = bass.AP(rows.tensor, rows.offset, [[XS_H, 16], [1, K], [1, XN]])
                sp.dma_start(xq[slot][0:16 * K, :], src).then_inc(x_in[slot], 16)
                if KR[r] > 16:
                    src = bass.AP(rows.tensor, rows.offset + 16 * XS_H, [[1, K], [1, XN]])
                    sp.dma_start(xq[slot][16 * K:17 * K, :], src).then_inc(x_edge[half_of(r)], 16)

            def load_band(it, k):
                slot = k // PARITY
                wait_count(sp, b_lo, it * 2 + slot - 1)
                rows = vf[0:V_SIZE].rearrange("(g v) -> g v", g=G)[bass.ds(it * 2 + slot, 1), :]
                src = bass.AP(rows.tensor, rows.offset + BAND0 * F, [[F, max(KR)], [V_J, K], [1, BN]])
                sp.dma_start(band[slot][:, :], src).then_inc(band_in[slot], 16)

            def store(it, k, s):
                sp.wait_ge(ob_done, (it * PER + k) * HALVES + s + 1)
                for q in range(CH):
                    dst = co[k % PARITY].rearrange("(g d) h p w -> g h d (p w)", g=G)
                    dst = dst[bass.ds(it * 2 + k // PARITY, 1), HALF_ROWS * s:HALF_ROWS * (s + 1), :,
                              2 * q * W:2 * (q + 1) * W]
                    sp.dma_start(dst.rearrange("u h d w -> h (u d) w"),
                                 ob[s][32 * q:32 * q + HALF_ROWS, :]
                                 .rearrange("p (d w) -> p d w", d=D)).then_inc(ob_out[s], 16)

            def load_r(part):
                first, end, i = R_PARTS[part]
                for j in range(MROWS):
                    top = MROWS * first + MROWS - 1 - j
                    sp.dma_start(r_all[F * j:F * j + CR, first:end, i, :],
                                 rs[top:MROWS * end:MROWS, i].rearrange("b f p w -> f b (p w)")
                                 ).then_inc(r_in[part], 16)
                sp.dma_start(r_all[CR:MF:F, first:end, i, :],
                             ones_rows.rearrange("j (b i x) -> j b i x", b=BLOCKS, i=PARITY)[:, first:end, i]
                             ).then_inc(r_in[part], 16)

            def step(it, k):
                own = stands(it, k, PER, STEPS)
                a = before(it, k, PER, 1)
                start = isinstance(it, int) and it == 0 and k == 0
                if own and k % PARITY == 0:
                    load_band(it, k)
                for r in range(STRIPS):
                    if own:
                        load_maps(it, k, r)
                    if start and r in R_SLOTS:
                        load_r(R_SLOTS.index(r))
                if stands(*a, PER, STEPS):
                    store(*a, 0)
                    store(*a, 1)

            rounds(sp, STEPS, PER, 1, step)
            for i in range(HALVES):
                sp.wait_ge(ob_out[i], STEPS * CH * 16)

        @block.gpsimd
        def _(pool):
            pool.memset(pick[:, :], 0.0).then_inc(pick_own, 1)
            for f in range(F):
                cols = pick[:, PICK0 + 1 - MROWS:PICK0 + 1]
                pool.wait_ge(pick_own, f + 1)
                pool.affine_select(out=cols, in_=cols, compare_op=ALU.not_equal, fill=1.0,
                                   base=-(F * (MROWS - 1) + f), pattern=[[F, MROWS]],
                                   channel_multiplier=1).then_inc(pick_own, 1)

            def step(it, k):
                if k % PARITY == 0:
                    slot = k // PARITY
                    pool.wait_ge(b_hi, it * 2 + slot + 1)
                    wait_count(pool, z_done, (it * PER + k - 2) * NU)
                    pool.tensor_tensor(band_lo[slot][:, :], band[slot][:, :],
                                       band_hi[slot][:, :].bitcast(F32), ALU.subtract).then_inc(b_lo, 1)
                for r in range(STRIPS):
                    n, slot, rows = strip(it, k, r), slot_of(k, r), slice(0, KR[r] * K)
                    pool.wait_ge(x_hi, n + 1)
                    wait_count(pool, z_done, slot_free(it, k, r))
                    pool.tensor_tensor(xq_lo[slot][rows, 0:XP], xq[slot][rows, 0:XP],
                                       xq_hi[slot][rows, 0:XP].bitcast(F32), ALU.subtract).then_inc(x_lo_pool, 1)

            rounds(pool, STEPS, PER, 0, step)

        @block.scalar
        def _(act):
            def split_band(it, k):
                slot = k // PARITY
                act.wait_ge(band_in[slot], it * 16 + 16)
                wait_count(act, z_done, (it * PER + k - 2) * NU)
                nc.scalar.activation(band_hi[slot][:, :], band[slot][:, :], ACT.Copy).then_inc(b_hi, 1)

            def split_maps(it, k, r):
                slot, rows = slot_of(k, r), slice(0, KR[r] * K)
                uses = (k * STRIPS + r) // XR
                act.wait_ge(x_in[slot], (it * (PER * STRIPS // XR) + uses + 1) * 16)
                if KR[r] > 16:
                    act.wait_ge(x_edge[half_of(r)], (it * PER + k + 1) * 16)
                wait_count(act, z_done, slot_free(it, k, r))
                nc.scalar.activation(xq_hi[slot][rows, :], xq[slot][rows, :], ACT.Copy).then_inc(x_hi, 1)

            def evacuate(it, k, s):
                n = it * PER + k
                act.wait_ge(summed, n * HALVES + s + 1)
                wait_count(act, ob_out[s], n * CH * 16)
                nc.scalar.activation(ob[s][:, :], o_ps[s][:, 0:CN], ACT.Copy).then_inc(ob_done, 1)

            def step(it, k):
                own = stands(it, k, PER, STEPS)
                a = before(it, k, PER, 1)
                start = isinstance(it, int) and it == 0 and k == 0
                if own and k % PARITY == 0:
                    split_band(it, k)
                for r in range(STRIPS):
                    if own:
                        split_maps(it, k, r)
                    if start and r in R_SLOTS:
                        first, end, i = R_PARTS[R_SLOTS.index(r)]
                        act.wait_ge(r_in[R_SLOTS.index(r)], (MROWS + 1) * 16)
                        part = r_all[:, first:end, i, :]
                        nc.scalar.activation(part, part, ACT.Relu, scale=affine[:, 0:1],
                                             bias=affine[:, 1:2]).then_inc(r_ready, 1)
                    if r in (1, 3) and stands(*a, PER, STEPS):
                        evacuate(*a, r // 2)

            rounds(act, STEPS, PER, 1, step)

        @block.tensor
        def _(pe):
            pe.wait_ge(pick_own, F + 1)

            def filters(it, k, u):
                n = it * PER + k
                r, parts = UNITS_OF[u]
                slot, bank = slot_of(k, r), BANK_OF[u]
                if u == 0 or UNITS_OF[u - 1][0] != r:
                    pe.wait_ge(x_lo_pool, strip(it, k, r) + 1)
                    pe.wait_ge(x_lo_dve, strip(it, k, r) + 1)
                last = [v - NU for v in range(NU) if BANK_OF[v] == bank] + [
                    v for v in range(u) if BANK_OF[v] == bank]
                wait_count(pe, weighted, n * NU + last[-1] + 1)
                rows = slice(0, KR[r] * K)
                for i, (m, q) in enumerate(parts):
                    maps = [part[slot][rows, :].rearrange("p (d i w) -> p d i w", d=D, i=P8)[
                        :, :, 2 * q:2 * q + 2, 0:W] for part in (xq_hi, xq_lo)]
                    zt = z_ps[bank][0:MF, i, 0:CN]
                    at = (TAP0 - BAND0 + PAD + IN0[r] - MROWS * m - (MROWS - 1)) * F
                    hi, lo = (part[k // PARITY][rows, at:at + MF] for part in (band_hi, band_lo))
                    nc.tensor.matmul(zt, hi, maps[0], start=True, stop=False)
                    nc.tensor.matmul(zt, hi, maps[1], start=False, stop=False)
                    mm = nc.tensor.matmul(zt, lo, maps[0], start=False, stop=True)
                mm.then_inc(z_done, 1)

            def sums(it, k, r):
                n, s = it * PER + k, half_of(r)
                pe.wait_ge(weighted, n * NU + LAST_UNIT[r] + 1)
                if STRIP_BLOCKS[r][0] % HALF_BLOCKS == 0:
                    wait_count(pe, ob_done, (n - 1) * HALVES + s + 1)
                for i, m in enumerate(STRIP_BLOCKS[r]):
                    bottom = MROWS * (m % HALF_BLOCKS) + MROWS - 1
                    cols = slice(PICK0 - bottom, PICK0 - bottom + 32)
                    for q in range(CH):
                        mm = nc.tensor.matmul(o_ps[s][32 * q:32 * (q + 1), 0:CN], pick[:, cols],
                                              prod[r % PR][:, q * len(STRIP_BLOCKS[r]) + i, :],
                                              start=m % HALF_BLOCKS == 0,
                                              stop=m % HALF_BLOCKS == HALF_BLOCKS - 1)
                if m % HALF_BLOCKS == HALF_BLOCKS - 1:
                    mm.then_inc(summed, 1)

            def step(it, k):
                own = stands(it, k, PER, STEPS)
                a = before(it, k, PER, 1)
                if own and k % PARITY == 0:
                    pe.wait_ge(b_lo, it * 2 + k // PARITY + 1)
                for u in range(NU):
                    if own:
                        filters(it, k, u)
                    if u == 1 and stands(*a, PER, STEPS):
                        sums(*a, STRIPS - 1)
                    if u - 2 in LAST_UNIT and own:
                        sums(it, k, LAST_UNIT.index(u - 2))

            rounds(pe, STEPS, PER, 1, step)

        @block.vector
        def _(dve):
            def low_part(it, k, r):
                n, slot, rows = strip(it, k, r), slot_of(k, r), slice(0, KR[r] * K)
                dve.wait_ge(x_hi, n + 1)
                wait_count(dve, z_done, slot_free(it, k, r))
                nc.vector.tensor_tensor(xq_lo[slot][rows, XP:XN], xq[slot][rows, XP:XN],
                                        xq_hi[slot][rows, XP:XN].bitcast(F32), ALU.subtract).then_inc(x_lo_dve, 1)

            def weigh(it, k, u):
                r, ((m, q), (m1, _)) = UNITS_OF[u]
                dve.wait_ge(z_done, (it * PER + k) * NU + u + 1)
                if m1 != m:
                    into = prod[r % PR][:, 2 * q:2 * q + 2, :]
                    by = r_all[:, m:m + 2, k % PARITY, 2 * q * W:2 * (q + 1) * W]
                else:
                    into = prod[r % PR][:, q:q + 2, :]
                    by = r_all[:, m, k % PARITY, 2 * q * W:2 * (q + 2) * W].rearrange("p (m x) -> p m x", m=2)
                nc.vector.tensor_tensor(into.rearrange("p m (d x) -> p m d x", d=D),
                                        z_ps[BANK_OF[u]][0:MF, :, 0:CN].rearrange("p m (d x) -> p m d x", d=D),
                                        by.unsqueeze(2).broadcast_to([MF, 2, D, 2 * W]),
                                        ALU.mult).then_inc(weighted, 1)

            def step(it, k):
                for r in range(STRIPS):
                    if stands(it, k, PER, STEPS):
                        low_part(it, k, r)
                    b = (it, k) if r >= 2 else before(it, k, PER, 1)
                    if not stands(*b, PER, STEPS):
                        continue
                    back = (r - 2) % STRIPS
                    if isinstance(it, int) and it == 0:
                        dve.wait_ge(r_ready, 3 if b[1] > 0 else min(back, 1) + 1)
                    for u in range(NU):
                        if UNITS_OF[u][0] == back:
                            weigh(*b, u)

            rounds(dve, STEPS, PER, 1, step)


def moe_stage(nc, x, co, wg, bg, w1, b1, w2, b2, out, ident_r, sel):
    STEPS = B * UNITS
    PER = PARITY * UNITS
    PAIRS = E // 2
    SLOTS = HB
    WEIGHT_SLOTS = (3, 7, 11, 13)
    GATE_OPS = 20
    STACK = P // (2 * E)

    with ExitStack() as ctx:
        def sb(name, shape, dt=F32):
            return ctx.enter_context(nc.sbuf_tensor("moe_" + name, shape, dt))

        def sem(name):
            return ctx.enter_context(nc.semaphore(name))

        center = sb("center2", [P, P])
        twin = sb("twin", [P, C])
        mean_cols = sb("mean_cols", [P, 32])
        gate_raw = sb("gate_raw", [P, T])
        turn_gate = sb("turn_gate", [P, 2, E + 1])
        neg_half = sb("neg_half", [SUB, NSUB])
        rank = sb("rank", [SUB, NSUB, E])
        w1_raw = sb("w1_raw", [P, HB * P])
        w1_hi = sb("w1_hi", [P, HB * P], F32R)
        w1_lo = sb("w1_lo", [P, HB * P], F32R)
        w2_s = sb("w2_s", [P, HB, C])
        b1_s = sb("b1_s", [P, HB])
        b2_s = sb("b2_s", [P, PAIRS])
        wg_raw = sb("wg_raw", [P, E])
        wg_half = sb("wg_half", [P, 32])
        bg_s = sb("bg_s", [SUB, E])
        xc = [sb(f"xc{i}", [P, 2, T]) for i in range(4)]
        cen = sb("cen2", [P, UNIT])
        sq = sb("sq2", [P, UNIT])
        xn = sb("xn", [P, 2, T])
        tok = [sb(f"tok{i}", [P, 2, T], F32R) for i in range(2)]
        var_eps = sb("var_eps", [SUB, NSUB])
        rstd = sb("rstd2", [SUB, NSUB])
        logit = sb("logit", [SUB, NSUB, E])
        rest = sb("rest", [SUB, NSUB, E])
        match = sb("match", [SUB, NSUB, E])
        first = sb("first", [SUB, NSUB, E])
        second = sb("second", [SUB, NSUB, E])
        either = sb("either", [SUB, NSUB, E])
        weight2 = sb("weight2", [SUB, NSUB, E])
        top1 = sb("top1", [SUB, NSUB])
        top2 = sb("top2", [SUB, NSUB])
        best = sb("best", [SUB, NSUB])
        gap = sb("gap", [SUB, NSUB])
        tanh = sb("tanh", [SUB, NSUB])
        rstd_st = sb("rstd_st", [SUB, NSUB - 1 + STACK, 2, E], F32R)
        weight_st = sb("weight_st", [SUB, NSUB - 1 + STACK, 2, E], F32R)
        rstd_t = sb("rstd_t", [P, 2, T], F32R)
        weight_t = sb("weight_t", [P, 2, T], F32R)
        wt = [sb(f"wt{p}", [P, 2, T]) for p in range(PAIRS)]
        hid = [sb(f"hid{i}", [P, 2, T]) for i in range(8)]
        term = [sb(f"term{p}", [P, 2, T]) for p in range(PAIRS)]
        acc = sb("acc", [P, 2, T])
        res = [sb(f"res{i}", [P, T]) for i in range(2)]
        h_ps = [ctx.enter_context(nc.psum_tensor(f"h_ps{i}", [P, 2, 512], F32)) for i in range(2)]
        y_ps = ctx.enter_context(nc.psum_tensor("y_ps", [P, 2, 512], F32))
        m_ps = [ctx.enter_context(nc.psum_tensor(f"m_ps{i}", [P, 512], F32)) for i in range(2)]

        fills = sem("fills")
        weights_in = sem("ffn_weights_in")
        w_hi = sem("w_hi")
        w_lo = sem("w_lo")
        wg_ready = sem("wg_ready")
        xc_in = [sem(f"xc_in{i}") for i in range(4)]
        misc_in = sem("misc_in")
        misc_out = sem("misc_out")
        squared = sem("squared2")
        var_done = sem("var_eps_done")
        rstd_done = sem("rstd_done2")
        tok_hi = sem("tok_hi")
        tok_lo = sem("tok_lo")
        gate = sem("gate")
        tanh_done = sem("tanh_done")
        stacks_blank = sem("stacks_blank")
        rstd_split = sem("rstd_split")
        h_done = sem("h_done")
        gelu_done = sem("gelu_done")
        y_done = sem("y_done")
        y_out = sem("y_out")
        added = sem("added")
        res_out = [sem(f"res_out{i}") for i in range(2)]

        FRONT = [("center0", 0), ("center1", 0), ("gates", 4), ("gates_t", 5), ("rstd_t0", 8), ("rstd_t1", 8),
                 ("rstd0", 10), ("rstd1", 10)]
        MID = [("weight_t0", 1), ("weight_t1", 1)] + [(f"weight{p}{t}", s) for p, s in enumerate(WEIGHT_SLOTS) for t in range(2)]
        END = [("result", 9)]

        def misc_uses(front, mid, end):
            uses = FRONT * front + MID * mid + END * end
            return sorted(uses, key=lambda u: u[1])

        def misc(it, k, name):
            if isinstance(it, int):
                n = it * PER + k
                flags = [(0 <= i < STEPS, 0 <= i - 1 < STEPS, 0 <= i - 2 < STEPS) for i in range(n + 1)]
                base = sum(len(misc_uses(*f)) for f in flags[:n])
                at = base + [u[0] for u in misc_uses(*flags[n])].index(name)
                return at, at % 2
            full = misc_uses(True, True, True)
            lack = 2 * len(END) + len(MID)
            at = [u[0] for u in full].index(name) - lack
            return (it * PER + k) * len(full) + at, (k * len(full) + at) % 2

        block = ctx.enter_context(nc.Block())

        @block.sync
        def _(sp):
            def load(it, k):
                par, u = k // UNITS, k % UNITS
                img = x.rearrange("(p i) c h w -> p i c (h w)", i=PARITY)
                sp.dma_start(xc[k % 4][0:C, :, :].rearrange("p a t -> p (a t)"),
                             img[bass.ds(it, 1), par, :, UNIT * u:UNIT * (u + 1)]
                             .rearrange("u c t -> (u c) t")).then_inc(xc_in[k % 4], 16)
                rows = H // UNITS
                sp.dma_start(xc[k % 4][C:P, :, :].rearrange("p a t -> p (a t)").rearrange("p (h w) -> p h w", w=W),
                             co[par][:, rows * u:rows * (u + 1), bass.ds(it, 1), :]
                             .rearrange("c h u w -> c h (u w)")).then_inc(xc_in[k % 4], 16)

            def store(step, it, k):
                at, _ = misc(*step, "result")
                sp.wait_ge(misc_out, at + 1)
                img = out.rearrange("(p i) c h w -> p i c (h w)", i=PARITY)
                for t in range(2):
                    at0 = UNIT * (k % UNITS) + T * t
                    sp.dma_start(img[bass.ds(it, 1), k // UNITS, :, at0:at0 + T]
                                 .rearrange("u c t -> (u c) t"),
                                 res[k % 2][C * t:C * (t + 1), :]).then_inc(res_out[k % 2], 16)

            def step(it, k):
                if stands(it, k, PER, STEPS):
                    load(it, k)
                if isinstance(it, int) and it == 0 and k == 0:
                    for half in range(2):
                        rows = slice(C * half, C * (half + 1))
                        sp.dma_start(w1_raw[rows, :].rearrange("c (e n) -> c e n", e=E),
                                     w1.rearrange("e c n -> c e n")).then_inc(weights_in, 16)
                        sp.dma_start(wg_raw[rows, :], wg).then_inc(weights_in, 16)
                    sp.dma_start(w2_s[:, :, :], w2.rearrange("e (b p) d -> p (e b) d", p=P)).then_inc(weights_in, 16)
                    sp.dma_start(b1_s[:, :], b1.rearrange("e (b p) -> p (e b)", p=P),
                                 allow_slow_non_contiguous=True).then_inc(weights_in, 16)
                    sp.dma_start(b2_s[:, :], b2.rearrange("(q e) d -> (e d) q", e=2),
                                 allow_slow_non_contiguous=True).then_inc(weights_in, 16)
                    sp.dma_start(bg_s[:, :], bg.partition_broadcast(SUB)).then_inc(weights_in, 16)
                z = before(it, k, PER, 2)
                if stands(*z, PER, STEPS):
                    store((it, k), *z)

            rounds(sp, STEPS, PER, 2, step)
            for i in range(2):
                sp.wait_ge(res_out[i], STEPS * 16)

        WEIGHTS = 8 * 16
        FILLS = 6 + E + 8

        @block.gpsimd
        def _(pool):
            consts = [(center[:, :], -1.0 / C), (twin[:, :], 0.0), (mean_cols[:, :], 0.5 / C),
                      (neg_half[:, :], -0.5), (wg_half[:, :], 0.0), (turn_gate[:, :, :], 0.0)] + [(rank[:, :, e:e + 1], float(E - e)) for e in range(E)]
            for n, (part, value) in enumerate(consts):
                pool.memset(part, value).then_inc(fills, 1)
                pool.wait_ge(fills, n + 1)
            done = len(consts)
            for mat, cols, fill in ((center, P, 1.0 - 1.0 / C), (twin, C, 1.0)):
                for shift in (0, C, -C):
                    pool.affine_select(out=mat[:, :], in_=mat[:, :], compare_op=ALU.not_equal,
                                       fill=fill, base=-shift, pattern=[[-1, cols]],
                                       channel_multiplier=1).then_inc(fills, 1)
                    done += 1
                    pool.wait_ge(fills, done)
            for cols, rows, base in ((slice(0, E), [[-1, E]], 0), (E, [], -2 * 32)):
                pool.affine_select(out=turn_gate[:, :, cols], in_=turn_gate[:, :, cols],
                                   compare_op=ALU.not_equal, fill=1.0, base=base,
                                   pattern=[[-32, 2]] + rows, channel_multiplier=1).then_inc(fills, 1)
                done += 1
                pool.wait_ge(fills, done)
            assert done == FILLS
            pool.wait_ge(w_hi, 1)
            pool.tensor_tensor(w1_lo[:, :], w1_raw[:, :], w1_hi[:, :].bitcast(F32),
                               ALU.subtract).then_inc(w_lo, 1)

            def add(nth, it, k):
                n = it * PER + k
                pool.wait_ge(y_out, n * 8 + 2 * nth + 2)
                wait_count(pool, added, n * PAIRS + nth)
                pool.tensor_tensor(acc[:, :, :], xc[k % 4][:, :, :] if nth == 0 else acc[:, :, :],
                                   term[nth][:, :, :], ALU.add).then_inc(added, 1)

            def step(it, k):
                f, a, z = (it, k), before(it, k, PER, 1), before(it, k, PER, 2)
                own, mid, end = (stands(*i, PER, STEPS) for i in (f, a, z))
                n = it * PER + k
                if own:
                    at, _ = misc(it, k, "center1")
                    pool.wait_ge(misc_out, at + 1)
                    pool.tensor_tensor(sq[:, :], cen[:, :], cen[:, :], ALU.mult).then_inc(squared, 1)
                if end:
                    add(3, *z)
                if own:
                    pool.wait_ge(var_done, n + 1)
                    pool.tensor_tensor(rstd[:, :], var_eps[:, :], neg_half[:, :], ALU.pow).then_inc(rstd_done, 1)
                if mid:
                    if not isinstance(it, int) or end:
                        at, _ = misc(it, k, "result")
                        pool.wait_ge(misc_in, at + 1)
                    add(0, *a)
                if own:
                    pool.wait_ge(tok_hi, n + 1)
                    if mid:
                        pool.wait_ge(added, (n - 1) * PAIRS + 1)
                    pool.tensor_tensor(tok[k % 2][C:P, :, :], xn[C:P, :, :],
                                       tok[k % 2][C:P, :, :].bitcast(F32), ALU.subtract).then_inc(tok_lo, 1)
                if mid:
                    if own:
                        pool.wait_ge(tok_lo, n + 1)
                    add(1, *a)
                    add(2, *a)

            rounds(pool, STEPS, PER, 2, step)

        @block.scalar
        def _(act):
            for stack in (rstd_st, weight_st):
                nc.scalar.activation(stack[:, NSUB:, :, :].rearrange("p s h e -> p (s h e)"),
                                     ident_r[0:SUB, 0:(STACK - 1) * 2 * E].bitcast(F32), ACT.Copy,
                                     scale=0.0).then_inc(stacks_blank, 1)
            act.wait_ge(weights_in, WEIGHTS)
            nc.scalar.activation(w1_hi[:, :], w1_raw[:, :], ACT.Copy).then_inc(w_hi, 1)

            def gelu(it, k, slot):
                n = (it * PER + k) * SLOTS + slot
                act.wait_ge(h_done, n + 1)
                nc.scalar.activation(hid[slot % 8][:, :, :], h_ps[slot % 2][:, :, 0:T], ACT.Gelu,
                                     bias=b1_s[:, slot:slot + 1]).then_inc(gelu_done, 1)

            def step(it, k):
                f, a = (it, k), before(it, k, PER, 1)
                own, mid = (stands(*i, PER, STEPS) for i in (f, a))
                n = it * PER + k
                for slot in range(SLOTS):
                    if mid:
                        gelu(*a, slot)
                    if own and slot == 11:
                        at, _ = misc(it, k, "rstd1")
                        act.wait_ge(misc_out, at + 1)
                        nc.scalar.activation(tok[k % 2][:, :, :], xn[:, :, :], ACT.Copy).then_inc(tok_hi, 1)
                    if own and slot == 13:
                        act.wait_ge(gate, n * GATE_OPS + 10)
                        nc.scalar.activation(tanh[:, :], gap[:, :], ACT.Tanh, scale=0.5).then_inc(tanh_done, 1)

            rounds(act, STEPS, PER, 1, step)

        @block.tensor
        def _(pe):
            pe.wait_ge(fills, FILLS)
            pe.wait_ge(stacks_blank, 2)
            pe.wait_ge(w_lo, 1)
            pe.wait_ge(wg_ready, 1)

            def hidden(it, k, slot):
                n = (it * PER + k) * SLOTS + slot
                if slot == 0:
                    pe.wait_ge(tok_lo, it * PER + k + 1)
                wait_count(pe, gelu_done, n - 1)
                cols = slice(P * slot, P * (slot + 1))
                for part, last in ((w1_hi, False), (w1_lo, True)):
                    for t in range(2):
                        mm = nc.tensor.matmul(h_ps[slot % 2][:, t, 0:T], part[:, cols],
                                              tok[k % 2][:, t, :], start=not last, stop=last)
                mm.then_inc(h_done, 1)

            def outputs(it, k, p, u):
                n = it * PER + k
                t, blk = u // 2, u % 2
                if u == 0:
                    pe.wait_ge(gelu_done, n * SLOTS + 4 * p + 4)
                if blk == 0:
                    wait_count(pe, y_out, n * 8 + 2 * p + t - 1)
                for e in range(2):
                    hb = 4 * p + 2 * e + blk
                    mm = nc.tensor.matmul(y_ps[C * e:C * (e + 1), t, 0:T], w2_s[:, hb, :],
                                          hid[hb % 8][:, t, :], start=(blk == 0), stop=(blk == 1))
                if blk == 1:
                    mm.then_inc(y_done, 1)

            def use(it, k, name):
                at, bank = misc(it, k, name)
                wait_count(pe, misc_out, at - 1)
                return m_ps[bank]

            def turn(bank, stack, t):
                for i in range(NSUB // 2):
                    s = t * NSUB // 2 + i
                    mm = nc.tensor.matmul(bank[:, SUB * i:SUB * (i + 1)],
                                          stack[:, s:s + STACK, :, :].rearrange("p s h e -> p (s h e)"),
                                          ident_r[0:SUB, 0:SUB], start=True, stop=True)
                mm.then_inc(misc_in, 1)

            def spread(step, name, turned, p, t):
                pe.wait_ge(misc_out, misc(*step, f"{name}_t{t}")[0] + 1)
                bank = use(*step, f"{name}{t}" if name == "rstd" else f"{name}{p}{t}")
                nc.tensor.matmul(bank[:, 0:T], sel[:, 2 * p:2 * p + 2, :].rearrange("p e c -> p (e c)"),
                                 turned[:, t, :], start=True, stop=True).then_inc(misc_in, 1)

            def weights(step, it, k, slot):
                if slot == 1:
                    pe.wait_ge(gate, (it * PER + k) * GATE_OPS + GATE_OPS)
                    for t in range(2):
                        turn(use(*step, f"weight_t{t}"), weight_st, t)
                if slot in WEIGHT_SLOTS:
                    for t in range(2):
                        spread(step, "weight", weight_t, WEIGHT_SLOTS.index(slot), t)

            def front(it, k, slot):
                n = it * PER + k
                if slot == 0:
                    pe.wait_ge(xc_in[k % 4], (it * 2 + k // 4) * 32 + 32)
                    for t in range(2):
                        nc.tensor.matmul(use(it, k, f"center{t}")[:, 0:T], center[:, :],
                                         xc[k % 4][:, t, :], start=True, stop=True).then_inc(misc_in, 1)
                if slot == 4:
                    bank = use(it, k, "gates")
                    pe.wait_ge(squared, n + 1)
                    for q, (cols, data) in enumerate(((wg_half, cen), (wg_half, cen), (mean_cols, sq), (mean_cols, sq))):
                        t = q % 2
                        mm = nc.tensor.matmul(bank[32 * q:32 * (q + 1), 0:T], cols[:, :],
                                              data[:, T * t:T * (t + 1)], start=True, stop=True)
                    mm.then_inc(misc_in, 1)
                if slot == 5:
                    pe.wait_ge(misc_out, misc(it, k, "gates")[0] + 1)
                    bank = use(it, k, "gates_t")
                    for i in range(NSUB // 2):
                        mm = nc.tensor.matmul(bank[0:SUB, 32 * i:32 * i + 2 * (E + 1)],
                                              gate_raw[:, SUB * i:SUB * (i + 1)],
                                              turn_gate[:, :, :].rearrange("p t e -> p (t e)"),
                                              start=True, stop=True)
                    mm.then_inc(misc_in, 1)
                if slot == 8:
                    pe.wait_ge(rstd_split, 2 * n + 2)
                    for t in range(2):
                        turn(use(it, k, f"rstd_t{t}"), rstd_st, t)
                if slot == 10:
                    for t in range(2):
                        spread((it, k), "rstd", rstd_t, 0, t)

            def result(step, it, k):
                bank = use(*step, "result")
                pe.wait_ge(added, (it * PER + k) * PAIRS + PAIRS)
                for t in range(2):
                    mm = nc.tensor.matmul(bank[C * t:C * (t + 1), 0:T], twin[:, :], acc[:, t, :],
                                          start=True, stop=True)
                mm.then_inc(misc_in, 1)

            def step(it, k):
                f, a, z = (it, k), before(it, k, PER, 1), before(it, k, PER, 2)
                own, mid, end = (stands(*i, PER, STEPS) for i in (f, a, z))
                for slot in range(SLOTS):
                    p, u = slot // 4, slot % 4
                    if mid:
                        hidden(*a, slot)
                    if p > 0 and mid:
                        outputs(*a, p - 1, u)
                    if p == 0 and end:
                        outputs(*z, PAIRS - 1, u)
                    if own:
                        front(*f, slot)
                    if mid:
                        weights(f, *a, slot)
                    if end and slot == 9:
                        result(f, *z)

            rounds(pe, STEPS, PER, 2, step)

        @block.vector
        def _(dve):
            dve.wait_ge(weights_in, WEIGHTS)
            dve.wait_ge(fills, FILLS)
            nc.vector.tensor_scalar(wg_half[:, 0:E], wg_raw[:, :], 0.5, None, ALU.mult).then_inc(wg_ready, 1)

            def filled(it, k, name):
                at, bank = misc(it, k, name)
                dve.wait_ge(misc_in, at + 1)
                return m_ps[bank]

            def centered(it, k):
                for t in range(2):
                    nc.vector.tensor_copy(cen[:, T * t:T * (t + 1)],
                                          filled(it, k, f"center{t}")[:, 0:T]).then_inc(misc_out, 1)

            def gates(it, k):
                nc.vector.tensor_copy(gate_raw[:, :], filled(it, k, "gates")[:, 0:T]).then_inc(misc_out, 1)

            def gates_turned(it, k):
                turned = filled(it, k, "gates_t")[0:SUB, 0:32 * NSUB // 2].rearrange(
                    "p (i x) -> p i x", x=32)[:, :, 0:2 * (E + 1)].rearrange("p i (t e) -> p t i e", t=2)
                nc.vector.tensor_scalar(var_eps[:, :].rearrange("p (t i u) -> p t i u", t=2, u=1),
                                        turned[:, :, :, E:E + 1], EPS_T, None,
                                        ALU.add).then_inc(var_done, 1)
                nc.vector.tensor_copy(logit[:, :, :].rearrange("p (t i) e -> p t i e", t=2),
                                      turned[:, :, :, 0:E]).then_inc(misc_out, 1)

            def each(stat):
                return stat[:, :].unsqueeze(2).broadcast_to([SUB, NSUB, E])

            def split_rstd(it, k):
                n = it * PER + k
                dve.wait_ge(rstd_done, n + 1)
                nc.vector.tensor_copy(rstd_st[:, 0:NSUB, 0, :], each(rstd)).then_inc(rstd_split, 1)
                dve.wait_ge(rstd_split, 2 * n + 1)
                nc.vector.tensor_tensor(rstd_st[:, 0:NSUB, 1, :], each(rstd), rstd_st[:, 0:NSUB, 0, :].bitcast(F32),
                                        ALU.subtract).then_inc(rstd_split, 1)

            def normalise(it, k):
                n = it * PER + k
                wait_count(dve, tok_lo, n)
                for t in range(2):
                    nc.vector.tensor_tensor(xn[:, t, :], cen[:, T * t:T * (t + 1)],
                                            filled(it, k, f"rstd{t}")[:, 0:T], ALU.mult).then_inc(misc_out, 1)

            def pick_experts(it, k):
                n = it * PER + k
                base = n * GATE_OPS
                dve.wait_ge(rstd_done, n + 1)
                at, _ = misc(it, k, "gates_t")
                dve.wait_ge(misc_out, at + 1)
                nc.vector.tensor_tensor(logit[:, :, :], logit[:, :, :], each(rstd), ALU.mult).then_inc(gate, 1)
                dve.wait_ge(gate, base + 1)
                nc.vector.tensor_tensor(logit[:, :, :], logit[:, :, :],
                                        bg_s[:, :].unsqueeze(1).broadcast_to([SUB, NSUB, E]),
                                        ALU.add).then_inc(gate, 1)
                dve.wait_ge(gate, base + 2)
                nc.vector.tensor_reduce(top1[:, :], logit[:, :, :], AX_X, ALU.max).then_inc(gate, 1)
                dve.wait_ge(gate, base + 3)
                nc.vector.tensor_tensor(match[:, :, :], logit[:, :, :], each(top1), ALU.is_equal).then_inc(gate, 1)
                dve.wait_ge(gate, base + 4)
                nc.vector.tensor_tensor(match[:, :, :], match[:, :, :], rank[:, :, :], ALU.mult).then_inc(gate, 1)
                dve.wait_ge(gate, base + 5)
                nc.vector.tensor_reduce(best[:, :], match[:, :, :], AX_X, ALU.max).then_inc(gate, 1)
                dve.wait_ge(gate, base + 6)
                nc.vector.tensor_tensor(first[:, :, :], match[:, :, :], each(best), ALU.is_equal).then_inc(gate, 1)
                dve.wait_ge(gate, base + 7)
                nc.vector.scalar_tensor_tensor(rest[:, :, :], first[:, :, :], -3.0e38, logit[:, :, :],
                                               ALU.mult, ALU.add).then_inc(gate, 1)
                dve.wait_ge(gate, base + 8)
                nc.vector.tensor_reduce(top2[:, :], rest[:, :, :], AX_X, ALU.max).then_inc(gate, 1)
                dve.wait_ge(gate, base + 9)
                nc.vector.tensor_tensor(gap[:, :], top2[:, :], top1[:, :], ALU.subtract).then_inc(gate, 1)
                nc.vector.tensor_tensor(match[:, :, :], rest[:, :, :], each(top2), ALU.is_equal).then_inc(gate, 1)
                dve.wait_ge(gate, base + 11)
                nc.vector.tensor_tensor(match[:, :, :], match[:, :, :], rank[:, :, :], ALU.mult).then_inc(gate, 1)
                dve.wait_ge(gate, base + 12)
                nc.vector.tensor_reduce(best[:, :], match[:, :, :], AX_X, ALU.max).then_inc(gate, 1)
                dve.wait_ge(gate, base + 13)
                nc.vector.tensor_tensor(second[:, :, :], match[:, :, :], each(best), ALU.is_equal).then_inc(gate, 1)
                dve.wait_ge(gate, base + 14)
                nc.vector.tensor_tensor(either[:, :, :], first[:, :, :], second[:, :, :], ALU.add).then_inc(gate, 1)
                nc.vector.tensor_tensor(second[:, :, :], second[:, :, :], first[:, :, :],
                                        ALU.subtract).then_inc(gate, 1)

            def weigh_experts(it, k):
                n = it * PER + k
                base = n * GATE_OPS
                dve.wait_ge(tanh_done, n + 1)
                dve.wait_ge(gate, base + 16)
                nc.vector.tensor_tensor(second[:, :, :], second[:, :, :], each(tanh), ALU.mult).then_inc(gate, 1)
                dve.wait_ge(gate, base + 17)
                nc.vector.tensor_tensor(weight2[:, :, :], either[:, :, :], second[:, :, :],
                                        ALU.add).then_inc(gate, 1)
                dve.wait_ge(gate, base + 18)
                nc.vector.tensor_scalar(weight_st[:, 0:NSUB, 0, :], weight2[:, :, :], 0.5, None,
                                        ALU.mult).then_inc(gate, 1)
                dve.wait_ge(gate, base + 19)
                nc.vector.scalar_tensor_tensor(weight_st[:, 0:NSUB, 1, :], weight2[:, :, :], 0.5,
                                               weight_st[:, 0:NSUB, 0, :].bitcast(F32),
                                               ALU.mult, ALU.subtract).then_inc(gate, 1)

            def turn(step, name, turned):
                for t in range(2):
                    nc.vector.tensor_copy(turned[:, t, :],
                                          filled(*step, f"{name}{t}")[:, 0:T]).then_inc(misc_out, 1)

            def weights(step, p):
                for t in range(2):
                    nc.vector.tensor_copy(wt[p][:, t, :],
                                          filled(*step, f"weight{p}{t}")[:, 0:T]).then_inc(misc_out, 1)

            def weighted(step, it, k, p, t):
                n = it * PER + k
                dve.wait_ge(y_done, n * 8 + 2 * p + t + 1)
                ahead = step if p < PAIRS - 1 else before(*step, PER, 1)
                dve.wait_ge(misc_out, misc(*ahead, f"weight{p}{t}")[0] + 1)
                wait_count(dve, added, (n - 1) * PAIRS + p + 1)
                nc.vector.scalar_tensor_tensor(term[p][:, t, :], y_ps[:, t, 0:T], b2_s[:, p:p + 1],
                                               wt[p][:, t, :], ALU.add, ALU.mult).then_inc(y_out, 1)

            def result(step, it, k):
                bank = filled(*step, "result")
                wait_count(dve, res_out[k % 2], (it * (PER // 2) + k // 2) * 2 * 16)
                nc.vector.tensor_copy(res[k % 2][:, :], bank[:, 0:T]).then_inc(misc_out, 1)

            def step(it, k):
                f, a, z = (it, k), before(it, k, PER, 1), before(it, k, PER, 2)
                own, mid, end = (stands(*i, PER, STEPS) for i in (f, a, z))
                for slot in range(SLOTS):
                    if own and slot == 0:
                        centered(*f)
                    if mid and slot == 1:
                        turn(f, "weight_t", weight_t)
                    if end and slot in (1, 3):
                        weighted(f, *z, PAIRS - 1, slot // 2)
                    if mid and slot in (5, 7, 9, 11, 13, 15):
                        weighted(f, *a, slot // 4 - 1, slot % 4 // 2)
                    if own and slot == 4:
                        gates(*f)
                    if own and slot == 5:
                        gates_turned(*f)
                    if own and slot == 7:
                        split_rstd(*f)
                    if own and slot == 8:
                        turn(f, "rstd_t", rstd_t)
                    if own and slot == 10:
                        normalise(*f)
                    if mid and slot in WEIGHT_SLOTS:
                        weights(f, WEIGHT_SLOTS.index(slot))
                    if end and slot == 9:
                        result(f, *z)
                    if own and slot == 11:
                        pick_experts(*f)
                    if own and slot == 14:
                        weigh_experts(*f)

            rounds(dve, STEPS, PER, 2, step)


_INS = ["x", "L0_conv_w1", "L0_conv_b1", "L0_conv_gamma", "L0_conv_beta", "L0_conv_w2", "L0_conv_b2",
        "L0_ffn_Wg", "L0_ffn_bg", "L0_ffn_W1", "L0_ffn_b1", "L0_ffn_W2", "L0_ffn_b2"]
_OUTS = [((B, C, H, W), "float32")]


def kernel(**inputs):
    import numpy as _np
    import concourse.bacc as _bacc
    from concourse import mybir as _mybir
    from concourse.bass_utils import run_bass_kernel_spmd as _run

    nc = _bacc.Bacc("TRN2", target_bir_lowering=False, num_devices=1)
    arrays, args = {}, []
    for name in _INS:
        a = _np.ascontiguousarray(inputs[name])
        arrays[f"in_{name}_dram"] = a
        args.append(nc.dram_tensor(f"in_{name}_dram", a.shape, _mybir.dt.from_np(a.dtype), kind="ExternalInput").ap())
    for i, (shape, dtype) in enumerate(_OUTS):
        dt = _mybir.dt.from_np(_np.dtype(dtype))
        args.append(nc.dram_tensor(f"out_{i}_dram", shape, dt, kind="ExternalOutput").ap())
    metaformer_block(nc, *args)
    r = _run(nc, [arrays], core_ids=[0])
    return r.results[0]["out_0_dram"]
```

```python
from contextlib import ExitStack

import concourse.bass as bass
from concourse import mybir

F32 = mybir.dt.float32
F32R = mybir.dt.float32r
ALU = mybir.AluOpType
ACT = mybir.ActivationFunctionType
AX_X = mybir.AxisListType.X

P = 128

B, C, H, W = 16, 64, 56, 56
HW = H * W
K = 7
PAD = K // 2
G = 16
D = C // G
CR = 16
F = CR + 1
E = 8
HID = 256
HB = E * HID // P
PAIRS = E // 2
EPS_C, EPS_BN, EPS_T = 1e-6, 1e-5, 1e-5

PARITY = 2
P8 = B // PARITY
T = 392
TR = T // W
UNIT = 2 * T
UNITS = HW // UNIT
SUB = 98
NSUB = UNIT // SUB
STACK = P // (2 * E)
WP = 64
MROWS = 7
MF = MROWS * F
BLOCKS = H // MROWS
STRIP_BLOCKS = ((0, 1), (2,), (3,), (4,), (5,), (6, 7))
IN0 = (0, 11, 18, 25, 32, 39)
KR = (17, 16, 16, 16, 16, 17)
STRIPS = len(IN0)
KP = max(KR) * K
BAND0 = 1
TAP0 = BAND0 + 2 * MROWS - 1
TL = 40
BN = (max(IN0[b] - MROWS * m for b, blocks in enumerate(STRIP_BLOCKS) for m in blocks)
      + TAP0 - BAND0 + PAD + 1) * F
HALF_BLOCKS = BLOCKS // 2
HALF_ROWS = H // 2
PICK0 = HALF_ROWS - 1
CH = 4
CN = D * 2 * W
UNITS_OF = [(r, [(m, q) for m in blocks] if len(blocks) == 2 else [(blocks[0], q), (blocks[0], q + 1)])
            for r, blocks in enumerate(STRIP_BLOCKS) for q in range(0, CH, 3 - len(blocks))]
NU = len(UNITS_OF)
LAST_UNIT = [max(u for u, (s, _) in enumerate(UNITS_OF) if s == r) for r in range(STRIPS)]
BANK_OF = [u % 3 for u in range(NU - 1)] + [1]

XS_H = C * P8 * WP
XS_SIZE = PARITY * H * XS_H
V_J = TL * F
V_G = K * V_J
V_SIZE = G * V_G


def before(it, k, per, lag):
    return (it, k - lag) if k >= lag else (it - 1, k - lag + per)


def stands(it, k, per, total):
    return not isinstance(it, int) or 0 <= it * per + k < total


def rounds(eng, total, per, tail, step):
    for k in range(per):
        step(0, k)
    with eng.Fori(1, total // per) as it:
        for k in range(per):
            step(it, k)
    for k in range(tail):
        step(total // per, k)


def wait_count(eng, sem, count):
    if not isinstance(count, int) or count > 0:
        eng.wait_ge(sem, count)


class ExpertTables:

    def __init__(self, nc, kept):
        def sb(name, shape, dt=F32):
            return kept.enter_context(nc.sbuf_tensor("moe_" + name, shape, dt))

        self.sel = sb("sel", [P, 2, E, C], F32R)
        self.ident_r = sb("ident_r", [P, P], F32R)
        self.center = sb("center", [P, C])
        self.twin = sb("twin", [P, C])
        self.mean_cols = sb("mean_cols", [P, 32])
        self.turn_gate = sb("turn_gate", [2 * 32, 2, E + 1])
        self.neg_half = sb("neg_half", [SUB, NSUB])
        self.rank = sb("rank", [SUB, NSUB, E])
        self.w1_hi = sb("w1_hi", [P, HB * P], F32R)
        self.w1_lo = sb("w1_lo", [P, HB * P], F32R)
        self.w2_s = sb("w2_s", [P, HB, C])
        self.b1_s = sb("b1_s", [P, HB])
        self.b2_s = sb("b2_s", [P, PAIRS])
        self.wg_raw = sb("wg_raw", [P, E])
        self.wg_cols = sb("wg_cols", [P, 32])
        self.bg_s = sb("bg_s", [SUB, E])
        self.rstd_st = sb("rstd_st", [SUB, NSUB // 2 - 1 + STACK, 2, E], F32R)
        self.weight_st = sb("weight_st", [SUB, NSUB // 2 - 1 + STACK // 2, 2, 2, E], F32R)


def metaformer_block(nc, x, conv_w1, conv_b1, gamma, beta, conv_w2, conv_b2,
                     wg, bg, w1, b1, w2, b2, out):
    xs = nc.dram_tensor("xs", (XS_SIZE + WP,), F32)
    rs = nc.dram_tensor("rs", (H, PARITY, CR, P8, W), F32)
    ones = nc.dram_tensor("ones_rows", (MROWS, BLOCKS * PARITY * P8 * W), F32)
    vf = nc.dram_tensor("vf", (V_SIZE,), F32)
    co = nc.dram_tensor("co", (PARITY, C, H, P8, W), F32)
    with ExitStack() as kept:
        ident = kept.enter_context(nc.sbuf_tensor("ident", [P, P], F32))
        affine = kept.enter_context(nc.sbuf_tensor("affine", [MF, 2], F32))
        pick = kept.enter_context(nc.sbuf_tensor("pick", [MF, PICK0 + 32], F32))
        tables = ExpertTables(nc, kept)
        norm_stage(nc, x, conv_w1, conv_b1, gamma, beta, conv_w2, conv_b2, xs, rs, ones, vf,
                   ident, affine, pick, wg, bg, w1, b1, w2, b2, tables)
        conv_stage(nc, xs, rs, ones, vf, co, affine, pick)
        moe_stage(nc, x, co, tables, out)


def norm_stage(nc, x, conv_w1, conv_b1, gamma, beta, conv_w2, conv_b2, xs, rs, ones_rows, vf,
               ident, affine, pick, wg, bg, w1, b1, w2, b2, tables):
    STEPS = P8 * UNITS
    PER = 2 * UNITS
    PAIR_ROWS = H // UNITS
    GROUPS = 4

    with ExitStack() as ctx:
        def sb(name, shape, dt=F32):
            return ctx.enter_context(nc.sbuf_tensor(name, shape, dt))

        def ps(name, shape):
            return ctx.enter_context(nc.psum_tensor(name, shape, F32))

        def sem(name):
            return ctx.enter_context(nc.semaphore(name))

        center = sb("center", [P, P])
        mean_col = sb("mean_col", [P, 2])
        w1t = sb("w1t", [P, 2 * CR])
        b1c = sb("b1c", [P, 1])
        eps_c = sb("eps_c", [P, 1])
        eps_bn = sb("eps_bn", [P, 1])
        avg = sb("avg", [P, CR])
        spread = sb("spread", [F, MF])
        zeros = sb("zeros", [P, V_SIZE // P])
        sel_raw = sb("sel_raw", [P, 2, E, C])
        w1_raw = sb("w1_raw", [P, HB * P // 2])
        ones = sb("ones", [MROWS * BLOCKS * PARITY, P8 * W])
        xin = sb("xin", [P, P8, HW])
        xpad = [sb(f"xpad{i}", [P, PAIR_ROWS, 2, WP]) for i in range(UNITS)]
        cen = [sb(f"cen{i}", [P, 2, T]) for i in range(4)]
        sq = [sb(f"sq{i}", [P, 2, T]) for i in range(2)]
        std = sb("std", [SUB, NSUB, 2])
        rstd = sb("rstd", [SUB, NSUB, 2])
        rstd_wide = sb("rstd_wide", [SUB, NSUB, 2, C])
        rt = [sb(f"rt{i}", [P, T]) for i in range(2)]
        stats = sb("stats", [P, STEPS // 2, 6])
        mv = sb("mv", [P, 2])
        m2 = sb("m2", [P, 1])
        chan = sb("chan", [CR, 6])
        gb = sb("gb", [CR, 2])
        ab = sb("ab", [F, 2])
        cen_ps = [ps(f"cen_ps{i}", [P, 2, 512]) for i in range(2)]
        wide_ps = ps("wide_ps", [P, 2, 512])
        var_ps = ps("var_ps", [P, 512])
        r_ps = ps("r_ps", [P, 512])

        weights_in = sem("weights_in")
        cleared = sem("cleared")
        pads_clear = sem("pads_clear")
        shaped = sem("shaped")
        blanks_done = sem("blanks_done")
        filters_out = sem("filters_out")
        x_in = [sem(f"x_in{i}") for i in range(2)]
        centered = sem("centered")
        cen_out = sem("cen_out")
        squared = sem("squared")
        var_done = sem("var_done")
        std_done = sem("std_done")
        rstd_own = sem("rstd_own")
        rstd_done = sem("rstd_done")
        wide_done = sem("wide_done")
        normed = sem("normed")
        r_done = sem("r_done")
        rt_done = sem("rt_done")
        stats_done = sem("stats_done")
        rs_out = [sem(f"rs_out{i}") for i in range(2)]
        xs_out = [sem(f"xs_out{i}") for i in range(UNITS)]
        bn_own = sem("bn_own")
        bn_pe = sem("bn_pe")
        bn_sqrt = sem("bn_sqrt")
        rounded = sem("rounded")
        pick_own = sem("pick_own")
        fills = sem("fills")
        experts_in = sem("experts_in")
        w1_in = sem("w1_in")
        w_hi = sem("w_hi")
        w_lo = sem("w_lo")
        wg_ready = sem("wg_ready")

        xs_map = xs[0:XS_SIZE].rearrange("(i h c x) -> i c h x", i=PARITY, h=H, c=C)
        vf_map = vf[:].rearrange("(g j t f) -> g j t f", g=G, j=K, t=TL)
        w2_map = conv_w2.rearrange("(i j g) c -> i g j c", i=K, j=K)
        b2_map = conv_b2.rearrange("(i j g u) -> i g j u", i=K, j=K, u=1)
        WEIGHTS = 2 + 8 + 2
        CLEARED = 15
        EXPERTS = 6 * 16
        FILLS = 8 + E + 8
        tab = tables

        block = ctx.enter_context(nc.Block())

        @block.sync
        def _(sp):
            x_pairs = x.rearrange("(p i) c h w -> p (i c) (h w)", i=PARITY)
            def load(pair):
                if pair >= 2:
                    sp.wait_ge(x_in[pair % 2], pair // 2 * 16)
                sp.dma_start(xin[:, pair, :], x_pairs[pair]).then_inc(x_in[pair % 2], 16)

            load(0)
            load(1)
            sp.wait_ge(cleared, 3)
            sp.dma_start(vf[:].rearrange("(p x) -> p x", p=P), zeros[:, :]).then_inc(blanks_done, 16)
            sp.dma_start(xs[XS_SIZE:XS_SIZE + WP].rearrange("(a x) -> a x", a=1),
                         zeros[0:1, 0:WP]).then_inc(blanks_done, 16)
            sp.dma_start(ones_rows.rearrange("j (x w) -> (j x) w", w=P8 * W),
                         ones[:, :]).then_inc(blanks_done, 16)
            load(2)
            load(3)

            def step(it, k):
                if isinstance(it, int) and it == 0 and k % 2 == 0:
                    load(4 + k // 2)
                j, v = before(it, k, PER, 3)
                if v % 2 == 0 or not stands(j, v, PER, STEPS):
                    return
                u = v // 2
                grp = u % 2
                sp.wait_ge(rt_done, j * UNITS + u + 1)
                for q in range(4):
                    row = PAIR_ROWS * u + TR * (q % 2)
                    dst = rs[row:row + TR, :, :, bass.ds(j * 2 + q // 2, 1), :]
                    sp.dma_start(dst.rearrange("h i c u w -> (i c) h (u w)"),
                                 rt[grp][32 * q:32 * (q + 1), :]
                                 .rearrange("c (h w) -> c h w", h=TR)).then_inc(rs_out[grp], 16)
                for i in range(PARITY):
                    sp.dma_start(xs_map[i][:, PAIR_ROWS * u:PAIR_ROWS * (u + 1), bass.ds(j * 2 * WP, 2 * WP)],
                                 xpad[u][C * i:C * (i + 1), :, :, :].rearrange("c h p w -> c h (p w)")
                                 ).then_inc(xs_out[u], 16)

            rounds(sp, STEPS, PER, 3, step)
            sp.wait_ge(blanks_done, 3 * 16)
            sp.wait_ge(filters_out, 2 * K * 16)
            for i in range(2):
                sp.wait_ge(rs_out[i], STEPS // 4 * 4 * 16)
            for u in range(UNITS):
                sp.wait_ge(xs_out[u], P8 // 2 * PARITY * 16)

        @block.gpsimd
        def _(pool):
            blank = [(zeros[:, :], 0.0), (ones[:, :], 1.0), (w1t[:, :], 0.0), (ident[:, :], 0.0),
                     (avg[:, :], 0.0), (spread[:, :], 0.0), (center[:, :], 0.0), (mean_col[:, :], 0.0),
                     (eps_c[:, :], EPS_C), (eps_bn[:, :], EPS_BN),
                     (sel_raw[:, :, :, :], 0.0)]
            for i in range(PARITY):
                half = slice(C * i, C * (i + 1))
                blank += [(center[half, half], -1.0 / C), (mean_col[half, i:i + 1], 1.0 / C)]
            assert len(blank) == CLEARED
            for n, (part, value) in enumerate(blank):
                pool.memset(part, value).then_inc(cleared, 1)
                pool.wait_ge(cleared, n + 1)
            pool.affine_select(out=ident[:, :], in_=ident[:, :], compare_op=ALU.not_equal, fill=1.0,
                               base=0, pattern=[[-1, P]], channel_multiplier=1).then_inc(shaped, 1)
            pool.wait_ge(shaped, 1)
            pool.affine_select(out=center[:, :], in_=center[:, :], compare_op=ALU.not_equal,
                               fill=1.0 - 1.0 / C, base=0, pattern=[[-1, P]],
                               channel_multiplier=1).then_inc(shaped, 1)
            pool.wait_ge(shaped, 2)
            wide = spread[:, :].rearrange("p (r f) -> p r f", r=MROWS)
            pool.affine_select(out=wide, in_=wide, compare_op=ALU.not_equal, fill=1.0, base=0,
                               pattern=[[0, MROWS], [-1, F]], channel_multiplier=1).then_inc(shaped, 1)
            for n in range(P // CR):
                pool.wait_ge(shaped, 3 + n)
                pool.affine_select(out=avg[:, :], in_=avg[:, :], compare_op=ALU.not_equal,
                                   fill=CR / P, base=-CR * n, pattern=[[-1, CR]],
                                   channel_multiplier=1).then_inc(shaped, 1)
            for h in range(2):
                pool.wait_ge(shaped, 3 + P // CR + h)
                pool.affine_select(out=sel_raw[:, :, :, :], in_=sel_raw[:, :, :, :], compare_op=ALU.not_equal,
                                   fill=1.0, base=-E * h, pattern=[[-2 * E, 2], [-1, E], [0, C]],
                                   channel_multiplier=1).then_inc(shaped, 1)
            pool.wait_ge(blanks_done, 3 * 16)
            for i in range(K):
                pool.dma_start(vf_map[:, 0:K, TAP0 + i, 0:CR], w2_map[i]).then_inc(filters_out, 16)
                pool.dma_start(vf_map[:, 0:K, TAP0 + i, CR:F], b2_map[i],
                               allow_slow_non_contiguous=True).then_inc(filters_out, 16)
            for half in range(2):
                rows = slice(C * half, C * (half + 1))
                pool.dma_start(tab.wg_raw[rows, :], wg).then_inc(experts_in, 16)
            pool.dma_start(tab.w2_s[:, :, :], w2.rearrange("e (b p) d -> p (e b) d", p=P)).then_inc(experts_in, 16)
            pool.dma_start(tab.b1_s[:, :], b1.rearrange("e (b p) -> p (e b)", p=P),
                          allow_slow_non_contiguous=True).then_inc(experts_in, 16)
            pool.dma_start(tab.b2_s[:, :], b2.rearrange("(q e) d -> (e d) q", e=2),
                          allow_slow_non_contiguous=True).then_inc(experts_in, 16)
            pool.dma_start(tab.bg_s[:, :], bg.partition_broadcast(SUB)).then_inc(experts_in, 16)
            pool.memset(pick[:, :], 0.0).then_inc(pick_own, 1)
            for f in range(F):
                cols = pick[:, PICK0 + 1 - MROWS:PICK0 + 1]
                pool.wait_ge(pick_own, f + 1)
                pool.affine_select(out=cols, in_=cols, compare_op=ALU.not_equal, fill=1.0,
                                   base=-(F * (MROWS - 1) + f), pattern=[[F, MROWS]],
                                   channel_multiplier=1).then_inc(pick_own, 1)
            pool.wait_ge(pick_own, F + 1)
            consts = [(tab.center[:, :], -1.0 / C), (tab.twin[:, :], 0.0), (tab.mean_cols[:, :], 0.0),
                      (tab.neg_half[:, :], -0.5), (tab.wg_cols[:, :], 0.0), (tab.turn_gate[:, :, :], 0.0)]
            consts += [(tab.mean_cols[C * t:C * (t + 1), t:t + 1], 1.0 / C) for t in range(2)]
            consts += [(tab.rank[:, :, e:e + 1], float(E - e)) for e in range(E)]
            for n, (part, value) in enumerate(consts):
                pool.memset(part, value).then_inc(fills, 1)
                pool.wait_ge(fills, n + 1)
            done = len(consts)
            for mat, fill in ((tab.center, 1.0 - 1.0 / C), (tab.twin, 1.0)):
                for shift in (0, C, -C):
                    pool.affine_select(out=mat[:, :], in_=mat[:, :], compare_op=ALU.not_equal,
                                       fill=fill, base=-shift, pattern=[[-1, C]],
                                       channel_multiplier=1).then_inc(fills, 1)
                    done += 1
                    pool.wait_ge(fills, done)
            for cols, pattern, base in ((slice(0, E), [[-E, 2], [-1, E]], 0), (E, [[-1, 2]], -32)):
                pool.affine_select(out=tab.turn_gate[:, :, cols], in_=tab.turn_gate[:, :, cols],
                                   compare_op=ALU.not_equal, fill=1.0, base=base,
                                   pattern=pattern, channel_multiplier=1).then_inc(fills, 1)
                done += 1
                pool.wait_ge(fills, done)
            assert done == FILLS
            for n in range(2):
                for half in range(2):
                    pool.dma_start(w1_raw[C * half:C * (half + 1), :].rearrange("c (e n) -> c e n", e=E // 2),
                                   w1[E // 2 * n:E // 2 * (n + 1)].rearrange("e c n -> c e n")).then_inc(w1_in, 16)
                cols = slice(HB * P // 2 * n, HB * P // 2 * (n + 1))
                pool.wait_ge(w1_in, 2 * 16 * (n + 1))
                pool.tensor_copy(tab.w1_hi[:, cols], w1_raw[:, :]).then_inc(w_hi, 1)
                pool.wait_ge(w_hi, n + 1)
                pool.tensor_tensor(tab.w1_lo[:, cols], w1_raw[:, :], tab.w1_hi[:, cols].bitcast(F32),
                                   ALU.subtract).then_inc(w_lo, 1)
                pool.wait_ge(w_lo, n + 1)

        @block.scalar
        def _(act):
            act.wait_ge(cleared, 3)
            for i in range(PARITY):
                act.dma_start(w1t[C * i:C * (i + 1), CR * i:CR * (i + 1)],
                              conv_w1.rearrange("o c -> c o"), allow_slow_non_contiguous=True).then_inc(weights_in, 16)
            for n in range(P // CR):
                act.dma_start(b1c[CR * n:CR * (n + 1), :],
                              conv_b1.rearrange("(c u) -> c u", u=1)).then_inc(weights_in, 16)
            act.dma_start(gb[:, 0:1], gamma.rearrange("(c u) -> c u", u=1)).then_inc(weights_in, 16)
            act.dma_start(gb[:, 1:2], beta.rearrange("(c u) -> c u", u=1)).then_inc(weights_in, 16)
            act.wait_ge(cleared, CLEARED)

            def center_and_square(it, k):
                n = it * PER + k
                act.wait_ge(centered, n + 1)
                wait_count(act, normed, n - 3)
                nc.scalar.activation(cen[k % 4][:, :, :], cen_ps[k % 2][:, :, 0:T],
                                     ACT.Copy).then_inc(cen_out, 1)
                wait_count(act, var_done, n - 1)
                act.wait_ge(cen_out, n + 1)
                nc.scalar.activation(sq[k % 2][:, :, :], cen[k % 4][:, :, :],
                                     ACT.Square).then_inc(squared, 1)

            def deviation(it, k):
                n = it * PER + k
                act.wait_ge(var_done, n + 1)
                wait_count(act, rstd_own, n)
                nc.scalar.activation(std[:, :, :], var_ps[0:SUB, 0:2 * NSUB]
                                     .rearrange("p (s i) -> p s i", i=2), ACT.Sqrt,
                                     bias=eps_c[0:SUB, :]).then_inc(std_done, 1)

            def r_tiles(it, k):
                if k % 2 == 0:
                    return
                grp = k // 2 % 2
                count = it * GROUPS + k // 2
                if isinstance(it, int) and it * PER + k == 1:
                    act.wait_ge(weights_in, WEIGHTS * 16)
                act.wait_ge(r_done, it * PER + k + 1)
                wait_count(act, rs_out[grp], (it * 2 + k // 4) * 4 * 16)
                wait_count(act, stats_done, count - 1)
                nc.scalar.activation(rt[grp][:, :], r_ps[:, 0:T], ACT.Identity,
                                     bias=b1c[:, :]).then_inc(rt_done, 1)

            def step(it, k):
                if stands(it, k, PER, STEPS):
                    center_and_square(it, k)
                a = before(it, k, PER, 1)
                if stands(*a, PER, STEPS):
                    deviation(*a)
                a = before(it, k, PER, 3)
                if stands(*a, PER, STEPS):
                    r_tiles(*a)

            rounds(act, STEPS, PER, 3, step)
            nc.scalar.activation(tab.ident_r[:, :], ident[:, :], ACT.Copy).then_inc(rounded, 1)
            act.wait_ge(shaped, 5 + P // CR)
            nc.scalar.activation(tab.sel[:, :, :, :], sel_raw[:, :, :, :], ACT.Copy).then_inc(rounded, 1)
            act.wait_ge(rounded, 1)
            flat = "p s h e -> p (s h e)"
            for part in (tab.rstd_st[:, 0:NSUB // 2, :, :].rearrange(flat),
                         tab.rstd_st[:, NSUB // 2:, :, :].rearrange(flat),
                         tab.weight_st[:, NSUB // 2:, :, :, :].rearrange("p s t h e -> p (s t h e)")):
                nc.scalar.activation(part, tab.ident_r[0:SUB, 0:part.shape[1]].bitcast(F32), ACT.Copy,
                                     scale=0.0).then_inc(rounded, 1)
            act.wait_ge(rounded, 5)
            act.wait_ge(bn_own, 6)
            nc.scalar.activation(chan[:, 3:4], chan[:, 2:3], ACT.Sqrt,
                                 bias=eps_bn[0:CR, :]).then_inc(bn_sqrt, 1)

        @block.tensor
        def _(pe):
            pe.wait_ge(shaped, 2)
            pe.wait_ge(cleared, CLEARED)

            def center_unit(it, k):
                n = it * PER + k
                if k < 2:
                    pe.wait_ge(x_in[k], it * 16 + 16)
                wait_count(pe, cen_out, n - 1)
                pair = xin[:, bass.ds(it * 2 + k % 2, 1), :].rearrange("p u n -> p (u n)")
                for t in range(2):
                    at = (2 * (k // 2) + t) * T
                    mm = nc.tensor.matmul(cen_ps[k % 2][:, t, 0:T], center[:, :],
                                          pair[:, at:at + T], start=True, stop=True)
                mm.then_inc(centered, 1)

            def variances(it, k):
                n = it * PER + k
                pe.wait_ge(squared, n + 1)
                wait_count(pe, std_done, n)
                flat = sq[k % 2][:, :, :].rearrange("p a t -> p (a t)")
                for s in range(NSUB):
                    mm = nc.tensor.matmul(var_ps[0:SUB, 2 * s:2 * s + 2],
                                          flat[:, SUB * s:SUB * (s + 1)], mean_col[:, :],
                                          start=True, stop=True)
                mm.then_inc(var_done, 1)

            def widen(it, k):
                n = it * PER + k
                pe.wait_ge(rstd_done, n + 1)
                wait_count(pe, normed, n)
                for s in range(NSUB):
                    t, at = s // (NSUB // 2), s % (NSUB // 2) * SUB
                    mm = nc.tensor.transpose(wide_ps[:, t, at:at + SUB],
                                             rstd_wide[:, s, :, :].rearrange("p i c -> p (i c)"),
                                             ident[0:SUB, 0:SUB])
                mm.then_inc(wide_done, 1)

            def reduce_channels(it, k):
                n = it * PER + k
                if isinstance(it, int) and n == 0:
                    pe.wait_ge(weights_in, WEIGHTS * 16)
                pe.wait_ge(normed, n + 1)
                if k % 2 == 0:
                    wait_count(pe, rt_done, it * GROUPS + k // 2)
                for t in range(2):
                    q = 2 * (k % 2) + t
                    mm = nc.tensor.matmul(r_ps[32 * q:32 * (q + 1), 0:T], w1t[:, :],
                                          xpad[k // 2][:, TR * t:TR * (t + 1), k % 2, PAD:PAD + W],
                                          start=True, stop=True)
                mm.then_inc(r_done, 1)

            def step(it, k):
                if stands(it, k, PER, STEPS):
                    center_unit(it, k)
                a = before(it, k, PER, 1)
                if stands(*a, PER, STEPS):
                    variances(*a)
                a = before(it, k, PER, 3)
                if stands(*a, PER, STEPS):
                    reduce_channels(*a)
                a = before(it, k, PER, 2)
                if stands(*a, PER, STEPS):
                    widen(*a)

            rounds(pe, STEPS, PER, 3, step)
            pe.wait_ge(shaped, 3 + P // CR)
            pe.wait_ge(bn_own, 3)
            nc.tensor.matmul(var_ps[0:CR, 64:66], avg[:, :], mv[:, :], start=True,
                             stop=True).then_inc(bn_pe, 1)
            pe.wait_ge(bn_own, 10)
            nc.tensor.matmul(var_ps[0:MF, 128:130], spread[:, :], ab[:, :], start=True,
                             stop=True).then_inc(bn_pe, 1)

        @block.vector
        def _(dve):
            for u in range(UNITS):
                nc.vector.memset(xpad[u][:, :, :, :], 0.0).then_inc(pads_clear, 1)
            dve.wait_ge(pads_clear, UNITS)

            def reciprocals(it, k):
                n = it * PER + k
                dve.wait_ge(std_done, n + 1)
                nc.vector.reciprocal(rstd[:, :, :], std[:, :, :]).then_inc(rstd_own, 1)
                wait_count(dve, wide_done, n)
                dve.wait_ge(rstd_own, n + 1)
                nc.vector.tensor_copy(rstd_wide[:, :, :, :],
                                      rstd[:, :, :].unsqueeze(3).broadcast_to([SUB, NSUB, 2, C])
                                      ).then_inc(rstd_done, 1)

            def normalise(it, k):
                n = it * PER + k
                dve.wait_ge(wide_done, n + 1)
                if k % 2 == 0:
                    wait_count(dve, xs_out[k // 2], it * PARITY * 16)
                nc.vector.tensor_tensor(
                    xpad[k // 2][:, :, k % 2, PAD:PAD + W].rearrange("p (a r) w -> p a r w", a=2),
                    cen[k % 4][:, :, :].rearrange("p a (r w) -> p a r w", w=W),
                    wide_ps[:, :, 0:T].rearrange("p a (r w) -> p a r w", w=W),
                    ALU.mult).then_inc(normed, 1)

            def statistics(it, k):
                if k % 2 == 0:
                    return
                count = it * GROUPS + k // 2
                dve.wait_ge(rt_done, count + 1)
                nc.vector.bn_stats(stats[:, bass.ds(count, 1), :].rearrange("p u s -> p (u s)"),
                                   rt[k // 2 % 2][:, :]).then_inc(stats_done, 1)

            def step(it, k):
                a = before(it, k, PER, 2)
                if stands(*a, PER, STEPS):
                    normalise(*a)
                a = before(it, k, PER, 1)
                if stands(*a, PER, STEPS):
                    reciprocals(*a)
                a = before(it, k, PER, 3)
                if stands(*a, PER, STEPS):
                    statistics(*a)

            rounds(dve, STEPS, PER, 3, step)

            dve.wait_ge(experts_in, EXPERTS)
            dve.wait_ge(fills, FILLS)
            for t in range(2):
                half = slice(C * t, C * (t + 1))
                nc.vector.tensor_copy(tab.wg_cols[half, E * t:E * (t + 1)], tab.wg_raw[half, :]).then_inc(wg_ready, 1)
            dve.wait_ge(wg_ready, 2)

            dve.wait_ge(stats_done, STEPS // 2)
            nc.vector.bn_aggr(mv[:, :], stats[:, :, :].rearrange("p n s -> p (n s)")).then_inc(bn_own, 1)
            dve.wait_ge(bn_own, 1)
            nc.vector.tensor_tensor(m2[:, :], mv[:, 0:1], mv[:, 0:1], ALU.mult).then_inc(bn_own, 1)
            dve.wait_ge(bn_own, 2)
            nc.vector.tensor_tensor(mv[:, 1:2], mv[:, 1:2], m2[:, :], ALU.add).then_inc(bn_own, 1)
            dve.wait_ge(bn_pe, 1)
            nc.vector.tensor_copy(chan[:, 0:2], var_ps[0:CR, 64:66]).then_inc(bn_own, 1)
            dve.wait_ge(bn_own, 4)
            nc.vector.tensor_tensor(chan[:, 4:5], chan[:, 0:1], chan[:, 0:1], ALU.mult).then_inc(bn_own, 1)
            dve.wait_ge(bn_own, 5)
            nc.vector.tensor_tensor(chan[:, 2:3], chan[:, 1:2], chan[:, 4:5], ALU.subtract).then_inc(bn_own, 1)
            nc.vector.memset(ab[:, 0:1], 0.0).then_inc(bn_own, 1)
            nc.vector.memset(ab[:, 1:2], 1.0).then_inc(bn_own, 1)
            dve.wait_ge(bn_sqrt, 1)
            nc.vector.reciprocal(chan[:, 4:5], chan[:, 3:4]).then_inc(bn_sqrt, 1)
            dve.wait_ge(bn_sqrt, 2)
            dve.wait_ge(bn_own, 8)
            dve.wait_ge(weights_in, WEIGHTS * 16)
            nc.vector.tensor_tensor(ab[0:CR, 0:1], gb[:, 0:1], chan[:, 4:5], ALU.mult).then_inc(bn_own, 1)
            dve.wait_ge(bn_own, 9)
            nc.vector.tensor_tensor(chan[:, 5:6], chan[:, 0:1], ab[0:CR, 0:1], ALU.mult).then_inc(bn_sqrt, 1)
            dve.wait_ge(bn_sqrt, 3)
            nc.vector.tensor_tensor(ab[0:CR, 1:2], gb[:, 1:2], chan[:, 5:6], ALU.subtract).then_inc(bn_own, 1)
            dve.wait_ge(bn_pe, 2)
            nc.vector.tensor_copy(affine[:, :], var_ps[0:MF, 128:130]).then_inc(bn_own, 1)
            dve.wait_ge(bn_own, 11)


def conv_stage(nc, xs, rs, ones_rows, vf, co, affine, pick):
    STEPS = G * PARITY
    PER = 2 * PARITY
    XN = D * P8 * WP
    XP = XN * 3 // 4
    XR, PR = 4, 2
    HALVES = 2

    with ExitStack() as ctx:
        def sb(name, shape, dt=F32):
            return ctx.enter_context(nc.sbuf_tensor(name, shape, dt))

        def sem(name):
            return ctx.enter_context(nc.semaphore(name))

        r_all = sb("r_all", [MF, BLOCKS, PARITY, P8 * W])
        xq = [sb(f"xq{i}", [KP, XN]) for i in range(XR)]
        xq_hi = [sb(f"xq_hi{i}", [KP, XN], F32R) for i in range(XR)]
        xq_lo = [sb(f"xq_lo{i}", [KP, XN], F32R) for i in range(XR)]
        band = [sb(f"band{i}", [KP, BN]) for i in range(2)]
        band_hi = [sb(f"band_hi{i}", [KP, BN], F32R) for i in range(2)]
        band_lo = [sb(f"band_lo{i}", [KP, BN], F32R) for i in range(2)]
        prod = [sb(f"prod{i}", [MF, 2 * CH, CN]) for i in range(PR)]
        ob = [sb(f"ob{i}", [P, CN]) for i in range(HALVES)]
        z_ps = [ctx.enter_context(nc.psum_tensor(f"z_ps{i}", [P, 2, 512], F32)) for i in range(3)]
        o_ps = [ctx.enter_context(nc.psum_tensor(f"o_ps{i}", [P, 512], F32)) for i in range(HALVES)]

        r_in = [sem(f"r_in{i}") for i in range(3)]
        r_ready = sem("r_ready")
        x_in = [sem(f"xq_in{i}") for i in range(XR)]
        x_edge = [sem(f"xq_edge{i}") for i in range(2)]
        band_in = [sem(f"band_in{i}") for i in range(2)]
        x_hi = sem("x_hi")
        x_lo_pool = sem("x_lo_pool")
        x_lo_dve = sem("x_lo_dve")
        b_hi = sem("b_hi")
        b_lo = sem("b_lo")
        z_done = sem("z_done")
        weighted = sem("weighted")
        summed = sem("summed")
        ob_done = sem("ob_done")
        ob_out = [sem(f"ob_out{i}") for i in range(HALVES)]

        block = ctx.enter_context(nc.Block())

        def strip(it, k, r):
            return (it * PER + k) * STRIPS + r

        def slot_of(k, r):
            return (k * STRIPS + r) % XR

        def slot_free(it, k, r):
            j, v = (it, k) if r >= XR else before(it, k, PER, 1)
            return (j * PER + v) * NU + LAST_UNIT[(r - XR) % STRIPS] + 1

        def half_of(r):
            return STRIP_BLOCKS[r][0] // HALF_BLOCKS

        R_PARTS = ((0, 2, 0), (2, BLOCKS, 0), (0, BLOCKS, 1))
        R_SLOTS = (0, 1, 4)

        @block.sync
        def _(sp):
            def load_maps(it, k, r):
                slot = slot_of(k, r)
                wait_count(sp, x_lo_pool, strip(it, k, r) - XR + 1)
                wait_count(sp, x_lo_dve, strip(it, k, r) - XR + 1)
                top, par = IN0[r], k % PARITY
                rows = xs[0:XS_SIZE].rearrange("(i h g x) -> i h g x", i=PARITY, h=H, g=G)[
                    par, top:top + KR[r], bass.ds(it * 2 + k // PARITY, 1), :]
                src = bass.AP(rows.tensor, rows.offset, [[XS_H, 16], [1, K], [1, XN]])
                sp.dma_start(xq[slot][0:16 * K, :], src).then_inc(x_in[slot], 16)
                if KR[r] > 16:
                    src = bass.AP(rows.tensor, rows.offset + 16 * XS_H, [[1, K], [1, XN]])
                    sp.dma_start(xq[slot][16 * K:17 * K, :], src).then_inc(x_edge[half_of(r)], 16)

            def load_band(it, k):
                slot = k // PARITY
                wait_count(sp, b_lo, it * 2 + slot - 1)
                rows = vf[0:V_SIZE].rearrange("(g v) -> g v", g=G)[bass.ds(it * 2 + slot, 1), :]
                src = bass.AP(rows.tensor, rows.offset + BAND0 * F, [[F, max(KR)], [V_J, K], [1, BN]])
                sp.dma_start(band[slot][:, :], src).then_inc(band_in[slot], 16)

            def store(it, k, s):
                sp.wait_ge(ob_done, (it * PER + k) * HALVES + s + 1)
                for q in range(CH):
                    dst = co[k % PARITY].rearrange("(g d) h p w -> g h d (p w)", g=G)
                    dst = dst[bass.ds(it * 2 + k // PARITY, 1), HALF_ROWS * s:HALF_ROWS * (s + 1), :,
                              2 * q * W:2 * (q + 1) * W]
                    sp.dma_start(dst.rearrange("u h d w -> h (u d) w"),
                                 ob[s][32 * q:32 * q + HALF_ROWS, :]
                                 .rearrange("p (d w) -> p d w", d=D)).then_inc(ob_out[s], 16)

            def load_r(part):
                first, end, i = R_PARTS[part]
                for j in range(MROWS):
                    top = MROWS * first + MROWS - 1 - j
                    sp.dma_start(r_all[F * j:F * j + CR, first:end, i, :],
                                 rs[top:MROWS * end:MROWS, i].rearrange("b f p w -> f b (p w)")
                                 ).then_inc(r_in[part], 16)
                sp.dma_start(r_all[CR:MF:F, first:end, i, :],
                             ones_rows.rearrange("j (b i x) -> j b i x", b=BLOCKS, i=PARITY)[:, first:end, i]
                             ).then_inc(r_in[part], 16)

            def step(it, k):
                own = stands(it, k, PER, STEPS)
                a = before(it, k, PER, 1)
                start = isinstance(it, int) and it == 0 and k == 0
                if own and k % PARITY == 0:
                    load_band(it, k)
                for r in range(STRIPS):
                    if own:
                        load_maps(it, k, r)
                    if start and r in R_SLOTS:
                        load_r(R_SLOTS.index(r))
                if stands(*a, PER, STEPS):
                    store(*a, 0)
                    store(*a, 1)

            rounds(sp, STEPS, PER, 1, step)
            for i in range(HALVES):
                sp.wait_ge(ob_out[i], STEPS * CH * 16)

        @block.gpsimd
        def _(pool):
            def step(it, k):
                if k % PARITY == 0:
                    slot = k // PARITY
                    pool.wait_ge(b_hi, it * 2 + slot + 1)
                    wait_count(pool, z_done, (it * PER + k - 2) * NU)
                    pool.tensor_tensor(band_lo[slot][:, :], band[slot][:, :],
                                       band_hi[slot][:, :].bitcast(F32), ALU.subtract).then_inc(b_lo, 1)
                for r in range(STRIPS):
                    n, slot, rows = strip(it, k, r), slot_of(k, r), slice(0, KR[r] * K)
                    pool.wait_ge(x_hi, n + 1)
                    wait_count(pool, z_done, slot_free(it, k, r))
                    pool.tensor_tensor(xq_lo[slot][rows, 0:XP], xq[slot][rows, 0:XP],
                                       xq_hi[slot][rows, 0:XP].bitcast(F32), ALU.subtract).then_inc(x_lo_pool, 1)

            rounds(pool, STEPS, PER, 0, step)

        @block.scalar
        def _(act):
            def split_band(it, k):
                slot = k // PARITY
                act.wait_ge(band_in[slot], it * 16 + 16)
                wait_count(act, z_done, (it * PER + k - 2) * NU)
                nc.scalar.activation(band_hi[slot][:, :], band[slot][:, :], ACT.Copy).then_inc(b_hi, 1)

            def split_maps(it, k, r):
                slot, rows = slot_of(k, r), slice(0, KR[r] * K)
                uses = (k * STRIPS + r) // XR
                act.wait_ge(x_in[slot], (it * (PER * STRIPS // XR) + uses + 1) * 16)
                if KR[r] > 16:
                    act.wait_ge(x_edge[half_of(r)], (it * PER + k + 1) * 16)
                wait_count(act, z_done, slot_free(it, k, r))
                nc.scalar.activation(xq_hi[slot][rows, :], xq[slot][rows, :], ACT.Copy).then_inc(x_hi, 1)

            def evacuate(it, k, s):
                n = it * PER + k
                act.wait_ge(summed, n * HALVES + s + 1)
                wait_count(act, ob_out[s], n * CH * 16)
                nc.scalar.activation(ob[s][:, :], o_ps[s][:, 0:CN], ACT.Copy).then_inc(ob_done, 1)

            def step(it, k):
                own = stands(it, k, PER, STEPS)
                a = before(it, k, PER, 1)
                start = isinstance(it, int) and it == 0 and k == 0
                if own and k % PARITY == 0:
                    split_band(it, k)
                for r in range(STRIPS):
                    if own:
                        split_maps(it, k, r)
                    if start and r in R_SLOTS:
                        first, end, i = R_PARTS[R_SLOTS.index(r)]
                        act.wait_ge(r_in[R_SLOTS.index(r)], (MROWS + 1) * 16)
                        part = r_all[:, first:end, i, :]
                        nc.scalar.activation(part, part, ACT.Relu, scale=affine[:, 0:1],
                                             bias=affine[:, 1:2]).then_inc(r_ready, 1)
                    if r in (1, 3) and stands(*a, PER, STEPS):
                        evacuate(*a, r // 2)

            rounds(act, STEPS, PER, 1, step)

        @block.tensor
        def _(pe):
            def filters(it, k, u):
                n = it * PER + k
                r, parts = UNITS_OF[u]
                slot, bank = slot_of(k, r), BANK_OF[u]
                if u == 0 or UNITS_OF[u - 1][0] != r:
                    pe.wait_ge(x_lo_pool, strip(it, k, r) + 1)
                    pe.wait_ge(x_lo_dve, strip(it, k, r) + 1)
                last = [v - NU for v in range(NU) if BANK_OF[v] == bank] + [
                    v for v in range(u) if BANK_OF[v] == bank]
                wait_count(pe, weighted, n * NU + last[-1] + 1)
                rows = slice(0, KR[r] * K)
                for i, (m, q) in enumerate(parts):
                    maps = [part[slot][rows, :].rearrange("p (d i w) -> p d i w", d=D, i=P8)[
                        :, :, 2 * q:2 * q + 2, 0:W] for part in (xq_hi, xq_lo)]
                    zt = z_ps[bank][0:MF, i, 0:CN]
                    at = (TAP0 - BAND0 + PAD + IN0[r] - MROWS * m - (MROWS - 1)) * F
                    hi, lo = (part[k // PARITY][rows, at:at + MF] for part in (band_hi, band_lo))
                    nc.tensor.matmul(zt, hi, maps[0], start=True, stop=False)
                    nc.tensor.matmul(zt, hi, maps[1], start=False, stop=False)
                    mm = nc.tensor.matmul(zt, lo, maps[0], start=False, stop=True)
                mm.then_inc(z_done, 1)

            def sums(it, k, r):
                n, s = it * PER + k, half_of(r)
                pe.wait_ge(weighted, n * NU + LAST_UNIT[r] + 1)
                if STRIP_BLOCKS[r][0] % HALF_BLOCKS == 0:
                    wait_count(pe, ob_done, (n - 1) * HALVES + s + 1)
                for i, m in enumerate(STRIP_BLOCKS[r]):
                    bottom = MROWS * (m % HALF_BLOCKS) + MROWS - 1
                    cols = slice(PICK0 - bottom, PICK0 - bottom + 32)
                    for q in range(CH):
                        mm = nc.tensor.matmul(o_ps[s][32 * q:32 * (q + 1), 0:CN], pick[:, cols],
                                              prod[r % PR][:, q * len(STRIP_BLOCKS[r]) + i, :],
                                              start=m % HALF_BLOCKS == 0,
                                              stop=m % HALF_BLOCKS == HALF_BLOCKS - 1)
                if m % HALF_BLOCKS == HALF_BLOCKS - 1:
                    mm.then_inc(summed, 1)

            def step(it, k):
                own = stands(it, k, PER, STEPS)
                a = before(it, k, PER, 1)
                if own and k % PARITY == 0:
                    pe.wait_ge(b_lo, it * 2 + k // PARITY + 1)
                for u in range(NU):
                    if own:
                        filters(it, k, u)
                    if u == 1 and stands(*a, PER, STEPS):
                        sums(*a, STRIPS - 1)
                    if u - 2 in LAST_UNIT and own:
                        sums(it, k, LAST_UNIT.index(u - 2))

            rounds(pe, STEPS, PER, 1, step)

        @block.vector
        def _(dve):
            def low_part(it, k, r):
                n, slot, rows = strip(it, k, r), slot_of(k, r), slice(0, KR[r] * K)
                dve.wait_ge(x_hi, n + 1)
                wait_count(dve, z_done, slot_free(it, k, r))
                nc.vector.tensor_tensor(xq_lo[slot][rows, XP:XN], xq[slot][rows, XP:XN],
                                        xq_hi[slot][rows, XP:XN].bitcast(F32), ALU.subtract).then_inc(x_lo_dve, 1)

            def weigh(it, k, u):
                r, ((m, q), (m1, _)) = UNITS_OF[u]
                dve.wait_ge(z_done, (it * PER + k) * NU + u + 1)
                if m1 != m:
                    into = prod[r % PR][:, 2 * q:2 * q + 2, :]
                    by = r_all[:, m:m + 2, k % PARITY, 2 * q * W:2 * (q + 1) * W]
                else:
                    into = prod[r % PR][:, q:q + 2, :]
                    by = r_all[:, m, k % PARITY, 2 * q * W:2 * (q + 2) * W].rearrange("p (m x) -> p m x", m=2)
                nc.vector.tensor_tensor(into.rearrange("p m (d x) -> p m d x", d=D),
                                        z_ps[BANK_OF[u]][0:MF, :, 0:CN].rearrange("p m (d x) -> p m d x", d=D),
                                        by.unsqueeze(2).broadcast_to([MF, 2, D, 2 * W]),
                                        ALU.mult).then_inc(weighted, 1)

            def step(it, k):
                for r in range(STRIPS):
                    if stands(it, k, PER, STEPS):
                        low_part(it, k, r)
                    b = (it, k) if r >= 2 else before(it, k, PER, 1)
                    if not stands(*b, PER, STEPS):
                        continue
                    back = (r - 2) % STRIPS
                    if isinstance(it, int) and it == 0:
                        dve.wait_ge(r_ready, 3 if b[1] > 0 else min(back, 1) + 1)
                    for u in range(NU):
                        if UNITS_OF[u][0] == back:
                            weigh(*b, u)

            rounds(dve, STEPS, PER, 1, step)


def moe_stage(nc, x, co, tables, out):
    STEPS = B * UNITS
    PER = PARITY * UNITS
    SLOTS = HB
    AT = {"center": 0, "weight_t": 2, "gates": 5, "gates_t": 6, "result": 9, "rstd_t": 10, "rstd": 12}
    WEIGHT_SLOTS = (4, 8, 11, 14)
    GATE_OPS = 21

    with ExitStack() as ctx:
        def sb(name, shape, dt=F32):
            return ctx.enter_context(nc.sbuf_tensor("moe_" + name, shape, dt))

        center, twin, mean_cols, turn_gate = tables.center, tables.twin, tables.mean_cols, tables.turn_gate
        neg_half, rank, sel, ident_r = tables.neg_half, tables.rank, tables.sel, tables.ident_r
        w1_hi, w1_lo, w2_s, b1_s, b2_s = tables.w1_hi, tables.w1_lo, tables.w2_s, tables.b1_s, tables.b2_s
        wg_cols, bg_s, rstd_st, weight_st = tables.wg_cols, tables.bg_s, tables.rstd_st, tables.weight_st

        def sem(name):
            return ctx.enter_context(nc.semaphore(name))

        gate_raw = sb("gate_raw", [2 * 32, T])
        xc = [sb(f"xc{i}", [P, 2, T]) for i in range(4)]
        cen = sb("cen2", [P, T])
        sq = sb("sq2", [P, T])
        xn = sb("xn", [P, T])
        xn_hi = sb("xn_hi", [P, T], F32R)
        tok = [sb(f"tok{i}", [P, 2, T], F32R) for i in range(2)]
        var_eps = sb("var_eps", [SUB, NSUB])
        rstd = sb("rstd2", [SUB, NSUB])
        logit = sb("logit", [SUB, NSUB, E])
        rest = sb("rest", [SUB, NSUB, E])
        match = sb("match", [SUB, NSUB, E])
        first = sb("first", [SUB, NSUB, E])
        second = sb("second", [SUB, NSUB, E])
        either = sb("either", [SUB, NSUB, E])
        weight2 = sb("weight2", [SUB, NSUB, E])
        top1 = sb("top1", [SUB, NSUB])
        top2 = sb("top2", [SUB, NSUB])
        best = sb("best", [SUB, NSUB])
        gap = sb("gap", [SUB, NSUB])
        tanh = sb("tanh", [SUB, NSUB])
        rstd_t = sb("rstd_t", [P, T], F32R)
        weight_t = sb("weight_t", [P, T], F32R)
        wt = [sb(f"wt{p}", [P, 2, T]) for p in range(PAIRS)]
        hid = [sb(f"hid{i}", [P, 2, T]) for i in range(8)]
        term = [sb(f"term{p}", [P, 2, T]) for p in range(PAIRS)]
        acc = sb("acc", [P, 2, T])
        res = [sb(f"res{i}", [P, T]) for i in range(2)]
        h_ps = [ctx.enter_context(nc.psum_tensor(f"h_ps{i}", [P, 2, 512], F32)) for i in range(2)]
        y_ps = ctx.enter_context(nc.psum_tensor("y_ps", [P, 2, 512], F32))
        m_ps = [ctx.enter_context(nc.psum_tensor(f"m_ps{i}", [P, 512], F32)) for i in range(2)]

        xc_in = [sem(f"xc_in{i}") for i in range(4)]
        misc_in = sem("misc_in")
        misc_out = sem("misc_out")
        squared = sem("squared2")
        var_done = sem("var_eps_done")
        rstd_done = sem("rstd_done2")
        tok_hi = sem("tok_hi")
        tok_lo = sem("tok_lo")
        gate = sem("gate")
        tanh_done = sem("tanh_done")
        rstd_split = sem("rstd_split")
        h_done = sem("h_done")
        gelu_done = sem("gelu_done")
        y_done = sem("y_done")
        y_out = sem("y_out")
        added = sem("added")
        res_out = [sem(f"res_out{i}") for i in range(2)]

        FRONT = [(use, AT[use]) for use in ("center", "gates", "gates_t", "rstd_t", "rstd")]
        MID = [("weight_t", AT["weight_t"])] + [
            (f"weight{p}{t}", s) for p, s in enumerate(WEIGHT_SLOTS) for t in range(2)]
        END = [("result", AT["result"])]

        def misc_uses(front, mid, end):
            uses = FRONT * front + MID * mid + END * end
            return sorted(uses, key=lambda u: u[1])

        def misc(it, k, name):
            if isinstance(it, int):
                n = it * PER + k
                flags = [(0 <= i < STEPS, 0 <= i - 1 < STEPS, 0 <= i - 2 < STEPS) for i in range(n + 1)]
                base = sum(len(misc_uses(*f)) for f in flags[:n])
                at = base + [u[0] for u in misc_uses(*flags[n])].index(name)
                return at, at % 2
            full = misc_uses(True, True, True)
            lack = 2 * len(END) + len(MID)
            at = [u[0] for u in full].index(name) - lack
            return (it * PER + k) * len(full) + at, (k * len(full) + at) % 2

        block = ctx.enter_context(nc.Block())

        @block.sync
        def _(sp):
            def load(it, k):
                par, u = k // UNITS, k % UNITS
                img = x.rearrange("(p i) c h w -> p i c (h w)", i=PARITY)
                sp.dma_start(xc[k % 4][0:C, :, :].rearrange("p a t -> p (a t)"),
                             img[bass.ds(it, 1), par, :, UNIT * u:UNIT * (u + 1)]
                             .rearrange("u c t -> (u c) t")).then_inc(xc_in[k % 4], 16)
                rows = H // UNITS
                sp.dma_start(xc[k % 4][C:P, :, :].rearrange("p a t -> p (a t)").rearrange("p (h w) -> p h w", w=W),
                             co[par][:, rows * u:rows * (u + 1), bass.ds(it, 1), :]
                             .rearrange("c h u w -> c h (u w)")).then_inc(xc_in[k % 4], 16)

            def store(step, it, k):
                at, _ = misc(*step, "result")
                sp.wait_ge(misc_out, at + 1)
                img = out.rearrange("(p i) c h w -> p i c (h w)", i=PARITY)
                for t in range(2):
                    at0 = UNIT * (k % UNITS) + T * t
                    sp.dma_start(img[bass.ds(it, 1), k // UNITS, :, at0:at0 + T]
                                 .rearrange("u c t -> (u c) t"),
                                 res[k % 2][C * t:C * (t + 1), :]).then_inc(res_out[k % 2], 16)

            def step(it, k):
                if stands(it, k, PER, STEPS):
                    load(it, k)
                z = before(it, k, PER, 2)
                if stands(*z, PER, STEPS):
                    store((it, k), *z)

            rounds(sp, STEPS, PER, 2, step)
            for i in range(2):
                sp.wait_ge(res_out[i], STEPS * 16)

        @block.gpsimd
        def _(pool):
            def add(nth, it, k):
                n = it * PER + k
                pool.wait_ge(y_out, n * 8 + 2 * nth + 2)
                wait_count(pool, added, n * PAIRS + nth)
                pool.tensor_tensor(acc[:, :, :], xc[k % 4][:, :, :] if nth == 0 else acc[:, :, :],
                                   term[nth][:, :, :], ALU.add).then_inc(added, 1)

            def step(it, k):
                f, a, z = (it, k), before(it, k, PER, 1), before(it, k, PER, 2)
                own, mid, end = (stands(*i, PER, STEPS) for i in (f, a, z))
                n = it * PER + k
                if own:
                    at, _ = misc(it, k, "center")
                    pool.wait_ge(misc_out, at + 1)
                    pool.tensor_tensor(sq[:, :], cen[:, :], cen[:, :], ALU.mult).then_inc(squared, 1)
                if end:
                    add(3, *z)
                if own:
                    pool.wait_ge(var_done, n + 1)
                    pool.tensor_tensor(rstd[:, :], var_eps[:, :], neg_half[:, :], ALU.pow).then_inc(rstd_done, 1)
                if mid:
                    if not isinstance(it, int) or end:
                        at, _ = misc(it, k, "result")
                        pool.wait_ge(misc_in, at + 1)
                    add(0, *a)
                if own:
                    pool.wait_ge(tok_hi, 3 * n + 3)
                    if mid:
                        pool.wait_ge(added, (n - 1) * PAIRS + 1)
                    pool.tensor_tensor(tok[k % 2][C:P, 0, :], xn[0:C, :],
                                       tok[k % 2][0:C, 0, :].bitcast(F32), ALU.subtract).then_inc(tok_lo, 1)
                    pool.wait_ge(tok_lo, 2 * n + 1)
                    pool.tensor_tensor(tok[k % 2][C:P, 1, :], xn[C:P, :],
                                       xn_hi[C:P, :].bitcast(F32), ALU.subtract).then_inc(tok_lo, 1)
                if mid:
                    if own:
                        pool.wait_ge(tok_lo, 2 * n + 2)
                    add(1, *a)
                    add(2, *a)

            rounds(pool, STEPS, PER, 2, step)

        @block.scalar
        def _(act):
            def gelu(it, k, slot):
                n = (it * PER + k) * SLOTS + slot
                act.wait_ge(h_done, n + 1)
                nc.scalar.activation(hid[slot % 8][:, :, :], h_ps[slot % 2][:, :, 0:T], ACT.Gelu,
                                     bias=b1_s[:, slot:slot + 1]).then_inc(gelu_done, 1)

            def step(it, k):
                f, a = (it, k), before(it, k, PER, 1)
                own, mid = (stands(*i, PER, STEPS) for i in (f, a))
                n = it * PER + k
                for slot in range(SLOTS):
                    if mid:
                        gelu(*a, slot)
                    if own and slot == AT["rstd"] + 1:
                        at, _ = misc(it, k, "rstd")
                        act.wait_ge(misc_out, at + 1)
                        for part, half in ((tok[k % 2][0:C, 0, :], 0), (xn_hi[C:P, :], 1),
                                           (tok[k % 2][0:C, 1, :], 1)):
                            nc.scalar.activation(part, xn[C * half:C * (half + 1), :], ACT.Copy).then_inc(tok_hi, 1)
                    if own and slot == 14:
                        act.wait_ge(gate, n * GATE_OPS + 10)
                        nc.scalar.activation(tanh[:, :], gap[:, :], ACT.Tanh, scale=0.5).then_inc(tanh_done, 1)

            rounds(act, STEPS, PER, 1, step)

        @block.tensor
        def _(pe):
            def hidden(it, k, slot):
                n = (it * PER + k) * SLOTS + slot
                if slot == 0:
                    pe.wait_ge(tok_lo, 2 * (it * PER + k) + 2)
                wait_count(pe, gelu_done, n - 1)
                cols = slice(P * slot, P * (slot + 1))
                for part, last in ((w1_hi, False), (w1_lo, True)):
                    for t in range(2):
                        mm = nc.tensor.matmul(h_ps[slot % 2][:, t, 0:T], part[:, cols],
                                              tok[k % 2][:, t, :], start=not last, stop=last)
                mm.then_inc(h_done, 1)

            def outputs(it, k, p, u):
                n = it * PER + k
                t, blk = u // 2, u % 2
                if u == 0:
                    pe.wait_ge(gelu_done, n * SLOTS + 4 * p + 4)
                if blk == 0:
                    wait_count(pe, y_out, n * 8 + 2 * p + t - 1)
                for e in range(2):
                    hb = 4 * p + 2 * e + blk
                    mm = nc.tensor.matmul(y_ps[C * e:C * (e + 1), t, 0:T], w2_s[:, hb, :],
                                          hid[hb % 8][:, t, :], start=(blk == 0), stop=(blk == 1))
                if blk == 1:
                    mm.then_inc(y_done, 1)

            def use(it, k, name):
                at, bank = misc(it, k, name)
                wait_count(pe, misc_out, at - 1)
                return m_ps[bank]

            def turn(bank, stack, per):
                cols = stack.rearrange("p s h e -> p (s h e)") if per == 1 else stack.rearrange(
                    "p s t h e -> p (s t h e)")
                for i in range(NSUB // 2):
                    at = i * per * 2 * E
                    mm = nc.tensor.matmul(bank[:, SUB * i:SUB * (i + 1)], cols[:, at:at + P],
                                          ident_r[0:SUB, 0:SUB], start=True, stop=True)
                mm.then_inc(misc_in, 1)

            def spread(step, p, t):
                pe.wait_ge(misc_out, misc(*step, "weight_t")[0] + 1)
                nc.tensor.matmul(use(*step, f"weight{p}{t}")[:, 0:T],
                                 sel[:, t, 2 * p:2 * p + 2, :].rearrange("p e c -> p (e c)"),
                                 weight_t[:, :], start=True, stop=True).then_inc(misc_in, 1)

            def weights(step, it, k, slot):
                if slot == AT["weight_t"]:
                    pe.wait_ge(gate, (it * PER + k) * GATE_OPS + GATE_OPS)
                    turn(use(*step, "weight_t"), weight_st[:, :, :, :, :], 2)
                if slot in WEIGHT_SLOTS:
                    for t in range(2):
                        spread(step, WEIGHT_SLOTS.index(slot), t)

            def front(it, k, slot):
                n = it * PER + k
                if slot == AT["center"]:
                    pe.wait_ge(xc_in[k % 4], (it * 2 + k // 4) * 32 + 32)
                    bank = use(it, k, "center")
                    for t in range(2):
                        mm = nc.tensor.matmul(bank[C * t:C * (t + 1), 0:T], center[:, :],
                                              xc[k % 4][:, t, :], start=True, stop=True)
                    mm.then_inc(misc_in, 1)
                if slot == AT["gates"]:
                    bank = use(it, k, "gates")
                    pe.wait_ge(squared, n + 1)
                    for q, (cols, data) in enumerate(((wg_cols, cen), (mean_cols, sq))):
                        mm = nc.tensor.matmul(bank[32 * q:32 * (q + 1), 0:T], cols[:, :], data[:, :],
                                              start=True, stop=True)
                    mm.then_inc(misc_in, 1)
                if slot == AT["gates_t"]:
                    pe.wait_ge(misc_out, misc(it, k, "gates")[0] + 1)
                    bank = use(it, k, "gates_t")
                    for i in range(NSUB // 2):
                        mm = nc.tensor.matmul(bank[0:SUB, 32 * i:32 * i + 2 * (E + 1)],
                                              gate_raw[:, SUB * i:SUB * (i + 1)],
                                              turn_gate[:, :, :].rearrange("p t e -> p (t e)"),
                                              start=True, stop=True)
                    mm.then_inc(misc_in, 1)
                if slot == AT["rstd_t"]:
                    pe.wait_ge(rstd_split, 2 * n + 2)
                    turn(use(it, k, "rstd_t"), rstd_st[:, :, :, :], 1)
                if slot == AT["rstd"]:
                    pe.wait_ge(misc_out, misc(it, k, "rstd_t")[0] + 1)
                    bank = use(it, k, "rstd")
                    nc.tensor.matmul(bank[:, 0:T], sel[:, 0, 0:2, :].rearrange("p e c -> p (e c)"),
                                     rstd_t[:, :], start=True, stop=True).then_inc(misc_in, 1)

            def result(step, it, k):
                bank = use(*step, "result")
                pe.wait_ge(added, (it * PER + k) * PAIRS + PAIRS)
                for t in range(2):
                    mm = nc.tensor.matmul(bank[C * t:C * (t + 1), 0:T], twin[:, :], acc[:, t, :],
                                          start=True, stop=True)
                mm.then_inc(misc_in, 1)

            def step(it, k):
                f, a, z = (it, k), before(it, k, PER, 1), before(it, k, PER, 2)
                own, mid, end = (stands(*i, PER, STEPS) for i in (f, a, z))

                def others(slot):
                    if own:
                        front(*f, slot)
                    if mid:
                        weights(f, *a, slot)
                    if end and slot == AT["result"]:
                        result(f, *z)

                for two in range(0, SLOTS, 2):
                    for slot in (two, two + 1):
                        if mid:
                            hidden(*a, slot)
                    others(two)
                    for slot in (two, two + 1):
                        p, u = slot // 4, slot % 4
                        if p > 0 and mid:
                            outputs(*a, p - 1, u)
                        if p == 0 and end:
                            outputs(*z, PAIRS - 1, u)
                    others(two + 1)

            rounds(pe, STEPS, PER, 2, step)

        @block.vector
        def _(dve):
            def filled(it, k, name):
                at, bank = misc(it, k, name)
                dve.wait_ge(misc_in, at + 1)
                return m_ps[bank]

            def centered(it, k):
                nc.vector.tensor_copy(cen[:, :], filled(it, k, "center")[:, 0:T]).then_inc(misc_out, 1)

            def gates(it, k):
                nc.vector.tensor_copy(gate_raw[:, :], filled(it, k, "gates")[0:2 * 32, 0:T]).then_inc(misc_out, 1)

            def gates_turned(it, k):
                turned = filled(it, k, "gates_t")[0:SUB, 0:32 * NSUB // 2].rearrange(
                    "p (i x) -> p i x", x=32)[:, :, 0:2 * (E + 1)].rearrange("p i (t e) -> p t i e", t=2)
                nc.vector.tensor_scalar(var_eps[:, :].rearrange("p (t i u) -> p t i u", t=2, u=1),
                                        turned[:, :, :, E:E + 1], EPS_T, None,
                                        ALU.add).then_inc(var_done, 1)
                nc.vector.tensor_copy(logit[:, :, :].rearrange("p (t i) e -> p t i e", t=2),
                                      turned[:, :, :, 0:E]).then_inc(misc_out, 1)

            def each(stat):
                return stat[:, :].unsqueeze(2).broadcast_to([SUB, NSUB, E])

            def split_rstd(it, k):
                n = it * PER + k
                dve.wait_ge(rstd_done, n + 1)
                halves = rstd[:, :].rearrange("p (e s) -> p s e", e=2)
                high, low = (rstd_st[:, 0:NSUB // 2, part, 0:2] for part in range(2))
                nc.vector.tensor_copy(high, halves).then_inc(rstd_split, 1)
                dve.wait_ge(rstd_split, 2 * n + 1)
                nc.vector.tensor_tensor(low, halves, high.bitcast(F32), ALU.subtract).then_inc(rstd_split, 1)

            def normalise(it, k):
                n = it * PER + k
                wait_count(dve, tok_lo, 2 * n)
                nc.vector.tensor_tensor(xn[:, :], cen[:, :], filled(it, k, "rstd")[:, 0:T],
                                        ALU.mult).then_inc(misc_out, 1)

            def pick_experts(it, k):
                n = it * PER + k
                base = n * GATE_OPS
                dve.wait_ge(rstd_done, n + 1)
                at, _ = misc(it, k, "gates_t")
                dve.wait_ge(misc_out, at + 1)
                nc.vector.tensor_tensor(logit[:, :, :], logit[:, :, :], each(rstd), ALU.mult).then_inc(gate, 1)
                dve.wait_ge(gate, base + 1)
                nc.vector.tensor_tensor(logit[:, :, :], logit[:, :, :],
                                        bg_s[:, :].unsqueeze(1).broadcast_to([SUB, NSUB, E]),
                                        ALU.add).then_inc(gate, 1)
                dve.wait_ge(gate, base + 2)
                nc.vector.tensor_reduce(top1[:, :], logit[:, :, :], AX_X, ALU.max).then_inc(gate, 1)
                dve.wait_ge(gate, base + 3)
                nc.vector.tensor_tensor(match[:, :, :], logit[:, :, :], each(top1), ALU.is_equal).then_inc(gate, 1)
                dve.wait_ge(gate, base + 4)
                nc.vector.tensor_tensor(match[:, :, :], match[:, :, :], rank[:, :, :], ALU.mult).then_inc(gate, 1)
                dve.wait_ge(gate, base + 5)
                nc.vector.tensor_reduce(best[:, :], match[:, :, :], AX_X, ALU.max).then_inc(gate, 1)
                dve.wait_ge(gate, base + 6)
                nc.vector.tensor_tensor(first[:, :, :], match[:, :, :], each(best), ALU.is_equal).then_inc(gate, 1)
                dve.wait_ge(gate, base + 7)
                nc.vector.scalar_tensor_tensor(rest[:, :, :], first[:, :, :], -3.0e38, logit[:, :, :],
                                               ALU.mult, ALU.add).then_inc(gate, 1)
                dve.wait_ge(gate, base + 8)
                nc.vector.tensor_reduce(top2[:, :], rest[:, :, :], AX_X, ALU.max).then_inc(gate, 1)
                dve.wait_ge(gate, base + 9)
                nc.vector.tensor_tensor(gap[:, :], top2[:, :], top1[:, :], ALU.subtract).then_inc(gate, 1)
                nc.vector.tensor_tensor(match[:, :, :], rest[:, :, :], each(top2), ALU.is_equal).then_inc(gate, 1)
                dve.wait_ge(gate, base + 11)
                nc.vector.tensor_tensor(match[:, :, :], match[:, :, :], rank[:, :, :], ALU.mult).then_inc(gate, 1)
                dve.wait_ge(gate, base + 12)
                nc.vector.tensor_reduce(best[:, :], match[:, :, :], AX_X, ALU.max).then_inc(gate, 1)
                dve.wait_ge(gate, base + 13)
                nc.vector.tensor_tensor(second[:, :, :], match[:, :, :], each(best), ALU.is_equal).then_inc(gate, 1)
                dve.wait_ge(gate, base + 14)
                nc.vector.tensor_tensor(either[:, :, :], first[:, :, :], second[:, :, :], ALU.add).then_inc(gate, 1)
                nc.vector.tensor_tensor(second[:, :, :], second[:, :, :], first[:, :, :],
                                        ALU.subtract).then_inc(gate, 1)

            def weigh_experts(it, k):
                n = it * PER + k
                base = n * GATE_OPS
                dve.wait_ge(tanh_done, n + 1)
                dve.wait_ge(gate, base + 16)
                nc.vector.tensor_tensor(second[:, :, :], second[:, :, :], each(tanh), ALU.mult).then_inc(gate, 1)
                dve.wait_ge(gate, base + 17)
                nc.vector.tensor_tensor(weight2[:, :, :], either[:, :, :], second[:, :, :],
                                        ALU.add).then_inc(gate, 1)
                dve.wait_ge(gate, base + 18)
                both = weight2[:, :, :].rearrange("p (t s) e -> p s t e", t=2)
                high, low = (weight_st[:, 0:NSUB // 2, :, part, :] for part in range(2))
                nc.vector.tensor_scalar(high, both, 0.5, None, ALU.mult).then_inc(gate, 1)
                dve.wait_ge(gate, base + 19)
                for t in range(2):
                    nc.vector.scalar_tensor_tensor(low[:, :, t, :], both[:, :, t, :], 0.5,
                                                   high[:, :, t, :].bitcast(F32),
                                                   ALU.mult, ALU.subtract).then_inc(gate, 1)

            def turn(step, name, turned):
                nc.vector.tensor_copy(turned, filled(*step, name)[:, 0:T]).then_inc(misc_out, 1)

            def weights(step, p):
                for t in range(2):
                    nc.vector.tensor_copy(wt[p][:, t, :],
                                          filled(*step, f"weight{p}{t}")[:, 0:T]).then_inc(misc_out, 1)

            def weighted(step, it, k, p, t):
                n = it * PER + k
                dve.wait_ge(y_done, n * 8 + 2 * p + t + 1)
                ahead = step if p < PAIRS - 1 else before(*step, PER, 1)
                dve.wait_ge(misc_out, misc(*ahead, f"weight{p}{t}")[0] + 1)
                wait_count(dve, added, (n - 1) * PAIRS + p + 1)
                nc.vector.scalar_tensor_tensor(term[p][:, t, :], y_ps[:, t, 0:T], b2_s[:, p:p + 1],
                                               wt[p][:, t, :], ALU.add, ALU.mult).then_inc(y_out, 1)

            def result(step, it, k):
                bank = filled(*step, "result")
                wait_count(dve, res_out[k % 2], (it * (PER // 2) + k // 2) * 2 * 16)
                nc.vector.tensor_copy(res[k % 2][:, :], bank[:, 0:T]).then_inc(misc_out, 1)

            def step(it, k):
                f, a, z = (it, k), before(it, k, PER, 1), before(it, k, PER, 2)
                own, mid, end = (stands(*i, PER, STEPS) for i in (f, a, z))
                for slot in range(SLOTS):
                    if own and slot == AT["center"]:
                        centered(*f)
                    if mid and slot == AT["weight_t"]:
                        turn(f, "weight_t", weight_t[:, :])
                    if mid and slot in WEIGHT_SLOTS:
                        weights(f, WEIGHT_SLOTS.index(slot))
                    if own and slot == AT["gates"]:
                        gates(*f)
                    if own and slot == AT["gates_t"]:
                        gates_turned(*f)
                    if own and slot == AT["rstd_t"]:
                        turn(f, "rstd_t", rstd_t[:, :])
                    if own and slot == AT["rstd"]:
                        normalise(*f)
                    if own and slot == AT["rstd_t"] - 1:
                        split_rstd(*f)
                    if end and slot == AT["result"]:
                        result(f, *z)
                    if end and slot in (1, 3):
                        weighted(f, *z, PAIRS - 1, slot // 2)
                    if mid and slot in (5, 7, 9, 11, 13, 15):
                        weighted(f, *a, slot // 4 - 1, slot % 4 // 2)
                    if own and slot == AT["rstd"]:
                        pick_experts(*f)
                    if own and slot == 15:
                        weigh_experts(*f)

            rounds(dve, STEPS, PER, 2, step)


_INS = ["x", "L0_conv_w1", "L0_conv_b1", "L0_conv_gamma", "L0_conv_beta", "L0_conv_w2", "L0_conv_b2",
        "L0_ffn_Wg", "L0_ffn_bg", "L0_ffn_W1", "L0_ffn_b1", "L0_ffn_W2", "L0_ffn_b2"]
_OUTS = [((B, C, H, W), "float32")]


def kernel(**inputs):
    import numpy as _np
    import concourse.bacc as _bacc
    from concourse import mybir as _mybir
    from concourse.bass_utils import run_bass_kernel_spmd as _run

    nc = _bacc.Bacc("TRN2", target_bir_lowering=False, num_devices=1)
    arrays, args = {}, []
    for name in _INS:
        a = _np.ascontiguousarray(inputs[name])
        arrays[f"in_{name}_dram"] = a
        args.append(nc.dram_tensor(f"in_{name}_dram", a.shape, _mybir.dt.from_np(a.dtype), kind="ExternalInput").ap())
    for i, (shape, dtype) in enumerate(_OUTS):
        dt = _mybir.dt.from_np(_np.dtype(dtype))
        args.append(nc.dram_tensor(f"out_{i}_dram", shape, dt, kind="ExternalOutput").ap())
    metaformer_block(nc, *args)
    r = _run(nc, [arrays], core_ids=[0])
    return r.results[0]["out_0_dram"]
```
